# Optimizing a Trainium2 kernel written in Bass

```python
import numpy as np
import jax
import jax.numpy as jnp

def _softmax(x, axis=-1):
    return jax.nn.softmax(x, axis=axis)

def _gelu(x):
    return jax.nn.gelu(x, approximate=True)

def _silu(x):
    return jax.nn.silu(x)

def _sigmoid(x):
    return jax.nn.sigmoid(x)

def _layernorm(x, axis=-1, eps=1e-05):
    m = jnp.mean(x, axis=axis, keepdims=True)
    v = jnp.var(x, axis=axis, keepdims=True)
    return (x - m) / jnp.sqrt(v + eps)

def _scatter_add(tgt, idx, src, axis=0):
    return tgt.at[idx].add(src)

def _segment_sum(src, seg, n):
    return jax.ops.segment_sum(src, seg, n)
kernel_name = 'mk_xattn_ffn_d2_seqx_r4_33d37f'

def setup_inputs(seed: int=0):
    np.random.seed(seed)
    _w = jnp.asarray

    def _rec_inputs():
        import jax
        import jax.numpy as jnp
        _rk = jax.random.key(seed)
        x = 0.002226 + 0.9996 * jax.random.normal(jax.random.fold_in(_rk, 1), (8, 256, 256), jnp.float32)
        _lenS = 256 - jax.random.randint(jax.random.fold_in(_rk, 7), (8,), 0, max(1, 256 // 4) + 1, jnp.int32)
        _lenS2 = 256 - jax.random.randint(jax.random.fold_in(_rk, 8), (8,), 0, max(1, 256 // 4) + 1, jnp.int32)
        _ctx_1024P = jax.random.normal(jax.random.fold_in(_rk, 11), (8, 16, 256), jnp.float32)
        _ctx_1024c = jax.random.dirichlet(jax.random.fold_in(_rk, 511), 0.3 * jnp.ones((16,), jnp.float32), (8, 256))
        _ctx_1024t = jnp.einsum('bsk,bkd->bsd', _ctx_1024c, _ctx_1024P)
        _ctx_1024t = _ctx_1024t * jax.lax.rsqrt(jnp.mean(jnp.square(_ctx_1024t)) + 1e-12) * 0.953939
        ctx_1024 = -0.000125008 + 0.999885 * (_ctx_1024t + 0.3 * jax.random.normal(jax.random.fold_in(_rk, 611), (8, 256, 256), jnp.float32))
        return (x, ctx_1024)
    x, ctx_1024 = _rec_inputs()

    def _L0_xattn_setup():
        import jax, jax.numpy as jnp
        import numpy as np
        DIM = 256
        HEADS = 16
        DIM_HEAD = 64
        INNER = HEADS * DIM_HEAD
        EPS = 1e-05

        def _layernorm(t, w, b):
            mu = jnp.mean(t, axis=-1, keepdims=True)
            var = jnp.mean(jnp.square(t - mu), axis=-1, keepdims=True)
            return (t - mu) * jax.lax.rsqrt(var + EPS) * w + b
        key = jax.random.key(seed)
        ks = jax.random.split(key, 8)
        b, n, l = (8, 1024, 64)
        x = jax.random.normal(ks[0], (b, n, DIM), dtype=jnp.float32)
        latents = jax.random.normal(ks[1], (b, l, DIM), dtype=jnp.float32)
        ln1_w = jnp.ones((DIM,), jnp.float32)
        ln1_b = jnp.zeros((DIM,), jnp.float32)
        ln2_w = jnp.ones((DIM,), jnp.float32)
        ln2_b = jnp.zeros((DIM,), jnp.float32)
        Wq = jax.random.normal(ks[2], (DIM, INNER), dtype=jnp.float32) / np.sqrt(DIM)
        Wkv = jax.random.normal(ks[3], (DIM, 2 * INNER), dtype=jnp.float32) / np.sqrt(DIM)
        Wo = jax.random.normal(ks[4], (INNER, DIM), dtype=jnp.float32) / np.sqrt(INNER)
        return {'x': x, 'latents': latents, 'ln1_w': ln1_w, 'ln1_b': ln1_b, 'ln2_w': ln2_w, 'ln2_b': ln2_b, 'Wq': Wq, 'Wkv': Wkv, 'Wo': Wo}
    _L0_xattn_all = _L0_xattn_setup()
    _L0_xattn_in = {k: v for k, v in _L0_xattn_all.items() if k in ('ln1_w', 'ln1_b', 'ln2_w', 'ln2_b', 'Wq', 'Wkv', 'Wo')}
    del _L0_xattn_all

    def _L0_ffn_setup():
        import jax, jax.numpy as jnp
        import numpy as np
        E = 16
        H = 256
        F = 512
        TOP_K = 1
        B, S = (2, 256)
        key = jax.random.key(seed)
        ks = jax.random.split(key, 7)
        s = 0.02
        return {'hidden_states': jax.random.normal(ks[0], (B, S, H), jnp.float32), 'w_router': jax.random.normal(ks[1], (E, H), jnp.float32) * s, 'gate_up_proj': jax.random.normal(ks[2], (E, H, 2 * F), jnp.float32) * s, 'down_proj': jax.random.normal(ks[3], (E, F, H), jnp.float32) * s, 'w_gate': jax.random.normal(ks[4], (F, H), jnp.float32) * s, 'w_up': jax.random.normal(ks[5], (F, H), jnp.float32) * s, 'w_down': jax.random.normal(ks[6], (H, F), jnp.float32) * s}
    _L0_ffn_all = _L0_ffn_setup()
    _L0_ffn_in = {k: v for k, v in _L0_ffn_all.items() if k in ('w_router', 'gate_up_proj', 'down_proj', 'w_gate', 'w_up', 'w_down')}
    del _L0_ffn_all

    def _L1_xattn_setup():
        import jax, jax.numpy as jnp
        import numpy as np
        import math
        EMB = 256
        HEADS = 16
        HEAD_DIM = EMB // HEADS
        key = jax.random.key(seed)
        ks = jax.random.split(key, 11)
        B, S = (4, 512)
        s = 1.0 / math.sqrt(EMB)
        return {'query': jax.random.normal(ks[0], (B, S, EMB), jnp.float32), 'key': jax.random.normal(ks[1], (B, S, EMB), jnp.float32), 'value': jax.random.normal(ks[2], (B, S, EMB), jnp.float32), 'Wq': jax.random.normal(ks[3], (EMB, EMB), jnp.float32) * s, 'bq': jax.random.normal(ks[4], (EMB,), jnp.float32) * s, 'Wk': jax.random.normal(ks[5], (EMB, EMB), jnp.float32) * s, 'bk': jax.random.normal(ks[6], (EMB,), jnp.float32) * s, 'Wv': jax.random.normal(ks[7], (EMB, EMB), jnp.float32) * s, 'bv': jax.random.normal(ks[8], (EMB,), jnp.float32) * s, 'Wo': jax.random.normal(ks[9], (EMB, EMB), jnp.float32) * s, 'bo': jax.random.normal(ks[10], (EMB,), jnp.float32) * s}
    _L1_xattn_all = _L1_xattn_setup()
    _L1_xattn_in = {k: v for k, v in _L1_xattn_all.items() if k in ('Wq', 'bq', 'Wk', 'bk', 'Wv', 'bv', 'Wo', 'bo')}
    del _L1_xattn_all

    def _L1_ffn_setup():
        import jax, jax.numpy as jnp
        import numpy as np
        CAPACITY = 2
        B, S, D, E, I = (4, 1024, 256, 8, 1024)
        key = jax.random.key(seed)
        k0, k1, k2, k3, k4 = jax.random.split(key, 5)
        x = jax.random.normal(k0, (B, S, D), dtype=jnp.float32)
        gate_w = jax.random.normal(k1, (E, D), dtype=jnp.float32) * 0.006
        w_gate = jax.random.normal(k2, (E, I, D), dtype=jnp.float32) * (1.0 / np.sqrt(D))
        w_up = jax.random.normal(k3, (E, I, D), dtype=jnp.float32) * (1.0 / np.sqrt(D))
        w_down = jax.random.normal(k4, (E, D, I), dtype=jnp.float32) * (1.0 / np.sqrt(I))
        return {'x': x, 'gate_w': gate_w, 'w_gate': w_gate, 'w_up': w_up, 'w_down': w_down}
    _L1_ffn_all = _L1_ffn_setup()
    _L1_ffn_in = {k: v for k, v in _L1_ffn_all.items() if k in ('gate_w', 'w_gate', 'w_up', 'w_down')}
    del _L1_ffn_all
    return {'x': x, 'ctx_1024': ctx_1024, 'L0_xattn_ln1_w': _L0_xattn_in['ln1_w'], 'L0_xattn_ln1_b': _L0_xattn_in['ln1_b'], 'L0_xattn_ln2_w': _L0_xattn_in['ln2_w'], 'L0_xattn_ln2_b': _L0_xattn_in['ln2_b'], 'L0_xattn_Wq': _L0_xattn_in['Wq'], 'L0_xattn_Wkv': _L0_xattn_in['Wkv'], 'L0_xattn_Wo': _L0_xattn_in['Wo'], 'L0_ffn_w_router': _L0_ffn_in['w_router'], 'L0_ffn_gate_up_proj': _L0_ffn_in['gate_up_proj'], 'L0_ffn_down_proj': _L0_ffn_in['down_proj'], 'L0_ffn_w_gate': _L0_ffn_in['w_gate'], 'L0_ffn_w_up': _L0_ffn_in['w_up'], 'L0_ffn_w_down': _L0_ffn_in['w_down'], 'L1_xattn_Wq': _L1_xattn_in['Wq'], 'L1_xattn_bq': _L1_xattn_in['bq'], 'L1_xattn_Wk': _L1_xattn_in['Wk'], 'L1_xattn_bk': _L1_xattn_in['bk'], 'L1_xattn_Wv': _L1_xattn_in['Wv'], 'L1_xattn_bv': _L1_xattn_in['bv'], 'L1_xattn_Wo': _L1_xattn_in['Wo'], 'L1_xattn_bo': _L1_xattn_in['bo'], 'L1_ffn_gate_w': _L1_ffn_in['gate_w'], 'L1_ffn_w_gate': _L1_ffn_in['w_gate'], 'L1_ffn_w_up': _L1_ffn_in['w_up'], 'L1_ffn_w_down': _L1_ffn_in['w_down']}

def reference(x, ctx_1024, L0_xattn_ln1_w, L0_xattn_ln1_b, L0_xattn_ln2_w, L0_xattn_ln2_b, L0_xattn_Wq, L0_xattn_Wkv, L0_xattn_Wo, L0_ffn_w_router, L0_ffn_gate_up_proj, L0_ffn_down_proj, L0_ffn_w_gate, L0_ffn_w_up, L0_ffn_w_down, L1_xattn_Wq, L1_xattn_bq, L1_xattn_Wk, L1_xattn_bk, L1_xattn_Wv, L1_xattn_bv, L1_xattn_Wo, L1_xattn_bo, L1_ffn_gate_w, L1_ffn_w_gate, L1_ffn_w_up, L1_ffn_w_down):
    import jax
    import jax.numpy as jnp

    def _L0_xattn_ref(x, latents, ln1_w, ln1_b, ln2_w, ln2_b, Wq, Wkv, Wo):
        import jax, jax.numpy as jnp
        import numpy as np
        DIM = 256
        HEADS = 16
        DIM_HEAD = 64
        INNER = HEADS * DIM_HEAD
        EPS = 1e-05

        def _layernorm(t, w, b):
            mu = jnp.mean(t, axis=-1, keepdims=True)
            var = jnp.mean(jnp.square(t - mu), axis=-1, keepdims=True)
            return (t - mu) * jax.lax.rsqrt(var + EPS) * w + b
        xn = _layernorm(x, ln1_w, ln1_b)
        latn = _layernorm(latents, ln2_w, ln2_b)
        b, l, _ = latn.shape
        q = latn @ Wq
        kv_input = jnp.concatenate([xn, latn], axis=1)
        kv = kv_input @ Wkv
        k, v = jnp.split(kv, 2, axis=-1)

        def heads(t):
            return t.reshape(t.shape[0], t.shape[1], HEADS, DIM_HEAD).transpose(0, 2, 1, 3)
        q, k, v = (heads(q), heads(k), heads(v))
        scale = 1.0 / np.sqrt(np.sqrt(DIM_HEAD))
        weight = jnp.einsum('bhld,bhnd->bhln', q * scale, k * scale)
        weight = jax.nn.softmax(weight.astype(jnp.float32), axis=-1).astype(weight.dtype)
        out = jnp.einsum('bhln,bhnd->bhld', weight, v)
        out = out.transpose(0, 2, 1, 3).reshape(b, l, INNER)
        return out @ Wo

    def _L0_ffn_ref(hidden_states, w_router, gate_up_proj, down_proj, w_gate, w_up, w_down):
        import jax, jax.numpy as jnp
        import numpy as np
        E = 16
        H = 256
        F = 512
        TOP_K = 1
        B, S = (2, 256)
        b, s, h = hidden_states.shape
        x = hidden_states.reshape(-1, h)
        logits = x @ w_router.T
        _, top_idx = jax.lax.top_k(logits, TOP_K)
        mask = jax.nn.one_hot(top_idx, E, dtype=logits.dtype).sum(axis=1)
        scores = jax.nn.sigmoid(logits) * mask
        masked_inputs = scores.T[:, :, None] * x[None, :, :]
        gate_up = jnp.einsum('eth,ehf->etf', masked_inputs, gate_up_proj)
        gate, up = jnp.split(gate_up, 2, axis=-1)
        expert_out = jnp.einsum('etf,efh->eth', up * jax.nn.silu(gate), down_proj)
        shared = jax.nn.silu(x @ w_gate.T) * (x @ w_up.T) @ w_down.T
        out = shared + expert_out.sum(axis=0)
        return out.reshape(b, s, h)

    def _L1_xattn_ref(query, key, value, Wq, bq, Wk, bk, Wv, bv, Wo, bo):
        import jax, jax.numpy as jnp
        import numpy as np
        import math
        EMB = 256
        HEADS = 16
        HEAD_DIM = EMB // HEADS
        B, S, _ = query.shape
        q = query @ Wq.T + bq
        k = key @ Wk.T + bk
        v = value @ Wv.T + bv
        q = q.reshape(B, S, HEADS, HEAD_DIM).transpose(0, 2, 1, 3)
        k = k.reshape(B, S, HEADS, HEAD_DIM).transpose(0, 2, 1, 3)
        v = v.reshape(B, S, HEADS, HEAD_DIM).transpose(0, 2, 1, 3)
        scale = 1.0 / math.sqrt(EMB)
        scores = jnp.einsum('bhqd,bhkd->bhqk', q, k) * scale
        probs = jax.nn.softmax(scores, axis=-1)
        out = jnp.einsum('bhqk,bhkd->bhqd', probs, v)
        out = out.transpose(0, 2, 1, 3).reshape(B, S, EMB)
        return out @ Wo.T + bo

    def _L1_ffn_ref(x, gate_w, w_gate, w_up, w_down):
        import jax, jax.numpy as jnp
        import numpy as np
        CAPACITY = 2
        B, S, D = x.shape
        E = gate_w.shape[0]
        k = S // E * CAPACITY
        logits = jnp.einsum('bsd,ed->bse', x, gate_w)
        affinity = jax.nn.softmax(logits, axis=-1)
        affinity = jnp.transpose(affinity, (0, 2, 1))
        gating, idx = jax.lax.top_k(affinity, k)
        bidx = jnp.arange(B)[:, None, None]
        x_in = x[bidx, idx]
        h = jax.nn.silu(jnp.einsum('bekd,eid->beki', x_in, w_gate)) * jnp.einsum('bekd,eid->beki', x_in, w_up)
        x_e = jnp.einsum('beki,edi->bekd', h, w_down)
        out = jnp.zeros_like(x).at[bidx, idx].add(gating[..., None] * x_e)
        return out
    x = x + _L0_xattn_ref(ctx_1024, _layernorm(x, axis=-1), L0_xattn_ln1_w, L0_xattn_ln1_b, L0_xattn_ln2_w, L0_xattn_ln2_b, L0_xattn_Wq, L0_xattn_Wkv, L0_xattn_Wo)
    x = x + _L0_ffn_ref(_layernorm(x, axis=-1), L0_ffn_w_router, L0_ffn_gate_up_proj, L0_ffn_down_proj, L0_ffn_w_gate, L0_ffn_w_up, L0_ffn_w_down)
    x = x + _L1_xattn_ref(_layernorm(x, axis=-1), ctx_1024, ctx_1024, L1_xattn_Wq, L1_xattn_bq, L1_xattn_Wk, L1_xattn_bk, L1_xattn_Wv, L1_xattn_bv, L1_xattn_Wo, L1_xattn_bo)
    x = x + _L1_ffn_ref(_layernorm(x, axis=-1), L1_ffn_gate_w, L1_ffn_w_gate, L1_ffn_w_up, L1_ffn_w_down)
    return x

_drawn_inputs = setup_inputs


def setup_inputs(seed=0):
    import zlib

    import numpy as np

    out = dict(_drawn_inputs(seed))
    spreads = {'L0_xattn_ln1_w': (1.0, 0.2),
     'L0_xattn_ln1_b': (0.0, 0.1),
     'L0_xattn_ln2_w': (1.0, 0.2),
     'L0_xattn_ln2_b': (0.0, 0.1)}
    factors = {'L0_ffn_w_router': 4.522,
     'L0_ffn_gate_up_proj': 4.514,
     'L0_ffn_down_proj': 4.621,
     'L1_xattn_bq': 49.495,
     'L1_xattn_bk': 200.0,
     'L0_ffn_w_gate': 5.691,
     'L0_ffn_w_up': 5.597,
     'L0_ffn_w_down': 5.566,
     'L1_xattn_Wq': 3.03,
     'L1_xattn_Wk': 2.696,
     'L1_xattn_bv': 5.771,
     'L1_xattn_bo': 5.305,
     'L1_ffn_gate_w': 3.335,
     'L1_ffn_w_gate': 3.086,
     'L1_ffn_w_up': 2.91,
     'L1_ffn_w_down': 2.9}
    for name, (base, spread) in spreads.items():
        noise = np.random.default_rng([zlib.crc32(name.encode()), seed]).standard_normal(out[name].shape)
        drawn = base * np.exp(spread * noise) if base else spread * noise
        out[name] = jnp.asarray(drawn.astype(out[name].dtype))
    for name, factor in factors.items():
        out[name] = (out[name] * factor).astype(out[name].dtype)
    return out
```

```python
import math
from contextlib import ExitStack

import concourse.bass as bass
from concourse import mybir

F32 = mybir.dt.float32
F32R = mybir.dt.float32r
BF16 = mybir.dt.bfloat16
I32 = mybir.dt.int32
U32 = mybir.dt.uint32
ALU = mybir.AluOpType
ACT = mybir.ActivationFunctionType
AX = mybir.AxisListType

P = 128
EPS = 1e-5


class Shared:
    pass


class Chain:

    def __init__(self, eng, sem):
        self.eng, self.sem, self.n = eng, sem, 0

    def restart(self):
        self.eng.sem_clear(self.sem)
        self.n = 0

    def __call__(self, ins):
        self.n += 1
        ins.then_inc(self.sem, 1)
        self.eng.wait_ge(self.sem, self.n)


def wait(eng, sem, value):
    if not isinstance(value, int) or value > 0:
        eng.wait_ge(sem, value)


def unrolled(eng, steps, body):
    body(0, True, steps == 1)
    if steps > 2:
        with eng.Fori(1, steps - 1) as i:
            body(i, False, False)
    if steps > 1:
        body(steps - 1, False, True)


def inverse_root(dve, link, rstd, std, var, tmp):
    link(dve.reciprocal(rstd, std))
    link(dve.tensor_tensor(tmp, rstd, rstd, ALU.mult))
    link(dve.scalar_tensor_tensor(tmp, var, EPS, tmp, ALU.add, ALU.mult))
    link(dve.tensor_scalar(tmp, tmp, -0.5, 1.5, ALU.mult, ALU.add))
    link(dve.tensor_tensor(rstd, rstd, tmp, ALU.mult))


def normalise_inputs(nc, g, io):
    NB, S, D, KC = g.NB, g.S, g.D, g.KC
    with ExitStack() as ctx:
        def sb(name, shape, dt):
            return ctx.enter_context(nc.sbuf_tensor(name, shape, dt))

        def sem(name):
            return ctx.enter_context(nc.semaphore(name))

        ctx_in = [sb(f"n_ctx{i}", [P, 2, D], F32) for i in range(2)]
        xn = [sb(f"n_xn{i}", [P, 4, D], F32) for i in range(2)]
        lat = sb("n_lat", [P, 2, D], F32)
        full = [sb(f"n_full{i}", [P, KC, 2 * S], F32) for i in range(2)]
        stats = sb("n_stats", [P, 6, 6], F32)
        mv = sb("n_mv", [P, 6, 2], F32)
        std = sb("n_std", [P, 6], F32)
        rstd = sb("n_rstd", [P, 6], F32)
        tmp = sb("n_tmp", [P, 6], F32)
        affine = sb("n_affine", [P, 4, KC], F32)
        ps = [ctx.enter_context(nc.psum_tensor(f"n_ps{i}", [P, KC, 2 * S], F32)) for i in range(2)]
        x_in, c_in = [sem(f"n_x_in{i}") for i in range(2)], [sem(f"n_c_in{i}") for i in range(2)]
        eps_set, zeros_set, zeroed = sem("n_eps_set"), sem("n_zeros_set"), sem("n_zeroed")
        ZEROS = g.BLOCKS * D
        const_in, ident_set = sem("n_const_in"), sem("n_ident")
        normed, turned, filled = sem("n_normed"), sem("n_turned"), sem("n_filled")
        have_var, have_std = sem("n_have_var"), sem("n_have_std")
        high, low, chain = sem("n_high"), sem("n_low"), sem("n_chain")
        x_dram = io["x"].rearrange("b (h p) d -> p b h d", p=P)
        c_dram = io["ctx_1024"].rearrange("b (h p) d -> p b h d", p=P)

        with nc.Block() as block:
            @block.sync
            def _(sp):
                for b in range(NB):
                    wait(sp, x_in[b % 2], 16 * (b // 2))
                    wait(sp, c_in[b % 2], 16 * (b // 2))
                    wait(sp, normed, b - 1)
                    sp.dma_start(g.x[:, 2 * b:2 * b + 2, :], x_dram[:, b]).then_inc(x_in[b % 2], 16)
                    sp.dma_start(ctx_in[b % 2][:, :, :], c_dram[:, b]).then_inc(c_in[b % 2], 16)
                    if b == 0:
                        for i, name in enumerate(("L0_xattn_ln1_w", "L0_xattn_ln1_b",
                                                  "L0_xattn_ln2_w", "L0_xattn_ln2_b")):
                            sp.dma_start(affine[:, i, :], io[name]).then_inc(const_in, 16)
                sp.wait_ge(zeros_set, 1)
                sp.dma_start(g.rows_in.rearrange("(p r) d -> p (r d)", p=P), g.big[:, 0:ZEROS]).then_inc(zeroed, 16)
                sp.wait_ge(zeroed, 16)

            @block.gpsimd
            def _(pool):
                nc.gpsimd.memset(g.ident[:, :], 0.0).then_inc(ident_set, 1)
                pool.wait_ge(ident_set, 1)
                nc.gpsimd.affine_select(out=g.ident[:, :], in_=g.ident[:, :], compare_op=ALU.not_equal, fill=1.0,
                                        base=0, pattern=[[-1, P]], channel_multiplier=1).then_inc(ident_set, 1)
                nc.gpsimd.memset(g.big[:, 0:ZEROS], 0.0).then_inc(zeros_set, 1)

                def part(b, par):
                    at = bass.ds(b * 2 * S, 2 * S)
                    pool.wait_ge(high, b + 1)
                    for kc in range(KC):
                        ins = pool.tensor_tensor(g.kvT_l[:, kc, at], full[par][:, kc, :],
                                                 g.kvT_h[:, kc, at], ALU.subtract)
                    ins.then_inc(low, 1)

                with pool.Fori(0, NB // 2) as i:
                    for par in range(2):
                        part(2 * i + par, par)

            @block.scalar
            def _(act):
                def roots(b):
                    act.wait_ge(have_var, 2 * b + 1)
                    act.activation(std[:, 0:4], mv[:, 0:4, 1], ACT.Sqrt, bias=g.eps[:, 0:1]).then_inc(have_std, 1)
                    act.wait_ge(have_var, 2 * b + 2)
                    act.activation(std[:, 4:6], mv[:, 4:6, 1], ACT.Sqrt, bias=g.eps[:, 0:1]).then_inc(have_std, 1)

                def step(i, first, last):
                    for par in range(2):
                        at = bass.ds((2 * i + par) * 2 * S, 2 * S)
                        act.wait_ge(filled, 2 * i + par + 1)
                        for kc in range(KC):
                            ins = act.activation(g.kvT_h[:, kc, at], full[par][:, kc, :], ACT.Copy)
                        ins.then_inc(high, 1)
                        if not (last and par == 1):
                            roots(2 * i + par + 1)

                act.wait_ge(eps_set, 1)
                roots(0)
                unrolled(act, NB // 2, step)

            @block.tensor
            def _(pe):
                def turn(i, first, last):
                    for par in range(2):
                        pe.wait_ge(normed, 2 * i + par + 1)
                        if first and par == 0:
                            pe.wait_ge(ident_set, 2)
                        wait(pe, filled, 2 * i + par - 1)
                        for kc in range(KC):
                            for t in range(4):
                                ins = pe.transpose(ps[par][:, kc, t * P:(t + 1) * P],
                                                   xn[par][:, t, kc * P:(kc + 1) * P], g.ident[:, :])
                        ins.then_inc(turned, 1)

                unrolled(pe, NB // 2, turn)

            @block.vector
            def _(dve):
                link = Chain(dve, chain)

                def moments(i, par):
                    link.restart()
                    dve.wait_ge(x_in[par], i * 16 + 16)
                    for t in range(2):
                        dve.bn_stats(stats[:, t, :], g.x[:, bass.ds((2 * i + par) * 2 + t, 1), :])
                    dve.wait_ge(c_in[par], i * 16 + 16)
                    for t in range(2, 4):
                        ins = dve.bn_stats(stats[:, t, :], ctx_in[par][:, t - 2, :])
                    link(ins)
                    for t in range(4):
                        ins = dve.bn_aggr(mv[:, t, :], stats[:, t, :])
                    ins.then_inc(have_var, 1)

                def norm(i, par):
                    b = 2 * i + par
                    dve.wait_ge(have_std, 2 * b + 1)
                    inverse_root(dve, link, rstd[:, 0:4], std[:, 0:4], mv[:, 0:4, 1], tmp[:, 0:4])
                    for t in range(2):
                        ins = dve.tensor_scalar(lat[:, t, :], g.x[:, bass.ds(b * 2 + t, 1), :], mv[:, t, 0:1],
                                                rstd[:, t:t + 1], ALU.subtract, ALU.mult)
                    link(ins)
                    wait(dve, turned, b - 1)
                    for t in range(2):
                        dve.tensor_scalar(xn[par][:, t, :], ctx_in[par][:, t, :], mv[:, 2 + t, 0:1],
                                          rstd[:, 2 + t:3 + t], ALU.subtract, ALU.mult)
                    for t in range(2):
                        ins = dve.bn_stats(stats[:, 4 + t, :], lat[:, t, :])
                    link(ins)
                    for t in range(2):
                        ins = dve.bn_aggr(mv[:, 4 + t, :], stats[:, 4 + t, :])
                    ins.then_inc(have_var, 1)
                    dve.wait_ge(have_std, 2 * b + 2)
                    inverse_root(dve, link, rstd[:, 4:6], std[:, 4:6], mv[:, 4:6, 1], tmp[:, 4:6])
                    for t in range(2):
                        ins = dve.tensor_scalar(xn[par][:, 2 + t, :], lat[:, t, :], mv[:, 4 + t, 0:1],
                                                rstd[:, 4 + t:5 + t], ALU.subtract, ALU.mult)
                    ins.then_inc(normed, 1)

                def fill(i, par):
                    b = 2 * i + par
                    dve.wait_ge(turned, b + 1)
                    wait(dve, low, b - 1)
                    for kc in range(KC):
                        for which in range(2):
                            ins = dve.tensor_scalar(full[par][:, kc, which * S:(which + 1) * S],
                                                    ps[par][:, kc, which * S:(which + 1) * S],
                                                    affine[:, 2 * which, kc:kc + 1],
                                                    affine[:, 2 * which + 1, kc:kc + 1], ALU.mult, ALU.add)
                    ins.then_inc(filled, 1)

                def step(i, first, last):
                    moments(i, 1)
                    fill(i, 0)
                    norm(i, 1)
                    if not last:
                        moments(i + 1, 0)
                    fill(i, 1)
                    if not last:
                        norm(i + 1, 0)

                dve.memset(g.eps[:, :], EPS).then_inc(eps_set, 1)
                moments(0, 0)
                dve.wait_ge(const_in, 64)
                norm(0, 0)
                unrolled(dve, NB // 2, step)


def attend_latents(nc, g, io):
    NB, S, KC = g.NB, g.S, g.KC
    N = 2 * S
    NC = N // P
    DH = 64
    PAIRS = 8
    STEPS = PAIRS * NB
    INNER = PAIRS * P
    QSCALE = 1.0 / DH ** 0.5
    with ExitStack() as ctx:
        def sb(name, shape, dt):
            return ctx.enter_context(nc.sbuf_tensor(name, shape, dt))

        def psum(name, shape):
            return ctx.enter_context(nc.psum_tensor(name, shape, F32))

        def sem(name):
            return ctx.enter_context(nc.semaphore(name))

        w_raw = sb("a_w_raw", [P, KC, 3, P], F32)
        w_h, w_l = sb("a_w_h", [P, KC, 3, P], F32R), sb("a_w_l", [P, KC, 3, P], F32R)
        q_h = [sb(f"a_q_h{i}", [P, 2, S], F32R) for i in range(2)]
        q_l = [sb(f"a_q_l{i}", [P, 2, S], F32R) for i in range(2)]
        k_h = [sb(f"a_k_h{i}", [P, N], F32R) for i in range(2)]
        k_l = [sb(f"a_k_l{i}", [P, N], F32R) for i in range(2)]
        vT = sb("a_vT", [P, N], F32)
        v = [sb(f"a_v{i}", [P, NC, P], F32) for i in range(2)]
        probs = [sb(f"a_p{i}", [P, N], F32) for i in range(4)]
        probsT = [[sb(f"a_pT{i}{h}", [P, NC, S], F32) for h in range(2)] for i in range(2)]
        negmax, total, inverse = sb("a_negmax", [P, 4], F32), sb("a_total", [P, 4], F32), sb("a_inverse", [P, 4], F32)

        scores = [psum(f"a_s{i}", [P, N]) for i in range(2)]
        turned_p = [psum(f"a_t{i}", [P, NC, P]) for i in range(2)]
        out_p = psum("a_o", [P, S])
        proj_qv, proj_k, turned_v = psum("a_qv", [P, N]), psum("a_k", [P, N]), psum("a_tv", [P, NC, P])

        w_in, wh_set, w_ready = sem("a_w_in"), sem("a_wh_set"), sem("a_w_ready")
        zeroed = sem("a_zeroed")
        q_done, k_done, v_done, vt_done = sem("a_q_done"), sem("a_k_done"), sem("a_v_done"), sem("a_vt_done")
        qh_set, ql_set, kh_set, kl_set = sem("a_qh_set"), sem("a_ql_set"), sem("a_kh_set"), sem("a_kl_set")
        vT_set, v_set = sem("a_vT_set"), sem("a_v_set")
        s_done, t_done, o_done = sem("a_s_done"), sem("a_t_done"), sem("a_o_done")
        max_set, exp_set, inv_set, norm_set = sem("a_max_set"), sem("a_exp_set"), sem("a_inv_set"), sem("a_norm_set")
        even_set, odd_set, o_set = sem("a_even_set"), sem("a_odd_set"), sem("a_o_set")
        wq_dram = io["L0_xattn_Wq"].rearrange("(c p) n -> p c n", p=P)
        wkv_dram = io["L0_xattn_Wkv"].rearrange("(c p) n -> p c n", p=P)

        def steps(eng, step):
            def body(i, first, last):
                step(2 * i, 0, first, False)
                step(2 * i + 1, 1, False, last)

            unrolled(eng, STEPS // 2, body)

        with nc.Block() as block:
            @block.sync
            def _(sp):
                for p in range(PAIRS):
                    wait(sp, w_ready, p)
                    for i, src in enumerate((wq_dram[:, :, p * P:(p + 1) * P], wkv_dram[:, :, p * P:(p + 1) * P],
                                             wkv_dram[:, :, INNER + p * P:INNER + (p + 1) * P])):
                        sp.dma_start(w_raw[:, :, i, :], src).then_inc(w_in, 16)

            @block.gpsimd
            def _(pool):
                for par in range(2):
                    for q in (q_h, q_l):
                        pool.memset(q[par][:, :, :].bitcast(F32), 0.0).then_inc(zeroed, 1)

                for p in range(PAIRS):
                    pool.wait_ge(w_in, 48 * p + 48)
                    wait(pool, v_done, NB * p)
                    pool.tensor_copy(w_h[:, :, :, :], w_raw[:, :, :, :]).then_inc(wh_set, 1)
                    pool.wait_ge(wh_set, p + 1)
                    pool.tensor_tensor(w_l[:, :, :, :], w_raw[:, :, :, :], w_h[:, :, :, :],
                                       ALU.subtract).then_inc(w_ready, 1)

            @block.tensor
            def _(pe):
                def project(out, which, s, done):
                    n = S if which == 0 else N
                    at = bass.ds((s % NB) * N + (N - n), n)
                    passes = [(w, x, kc) for kc in range(KC)
                              for w, x in ((w_h, g.kvT_h), (w_h, g.kvT_l), (w_l, g.kvT_h))]
                    for i, (w, x, kc) in enumerate(passes):
                        ins = pe.matmul(out[:, 0:n], w[:, kc, which, :], x[:, kc, at],
                                        start=(i == 0), stop=(i == len(passes) - 1))
                    ins.then_inc(done, 1)

                def project_q(s):
                    pe.wait_ge(w_ready, s // NB + 1)
                    wait(pe, vT_set, s)
                    project(proj_qv, 0, s, q_done)

                def project_k(s):
                    wait(pe, kl_set, s)
                    project(proj_k, 1, s, k_done)

                def project_v(s):
                    pe.wait_ge(ql_set, s + 1)
                    project(proj_qv, 2, s, v_done)

                def turn_v(s):
                    pe.wait_ge(vT_set, s + 1)
                    wait(pe, v_set, s)
                    for c in range(NC):
                        ins = pe.transpose(turned_v[:, c, :], vT[:, c * P:(c + 1) * P], g.ident[:, :])
                    ins.then_inc(vt_done, 1)

                def score(s, par, j):
                    h, rows = j // 2, slice(j % 2 * P, (j % 2 + 1) * P)
                    if j == 0:
                        pe.wait_ge(ql_set, s + 1)
                        pe.wait_ge(kl_set, s + 1)
                    wait(pe, exp_set, 4 * s + j - 1)
                    bank = scores[j % 2]
                    pe.matmul(bank[:, :], q_h[par][:, h, rows], k_h[par][:, :], start=True, stop=False)
                    pe.matmul(bank[:, :], q_h[par][:, h, rows], k_l[par][:, :], start=False, stop=False)
                    pe.matmul(bank[:, :], q_l[par][:, h, rows], k_h[par][:, :],
                              start=False, stop=True).then_inc(s_done, 1)

                def turn(s, j):
                    pe.wait_ge(norm_set, 4 * s + j + 1)
                    wait(pe, odd_set if j % 2 else even_set, 2 * s + j // 2)
                    for c in range(NC):
                        ins = pe.transpose(turned_p[j % 2][:, c, :], probs[j][:, c * P:(c + 1) * P], g.ident[:, :])
                    ins.then_inc(t_done, 1)

                def attend(s, par):
                    pe.wait_ge(even_set, 2 * s + 2)
                    pe.wait_ge(odd_set, 2 * s + 2)
                    pe.wait_ge(v_set, s + 1)
                    wait(pe, o_set, s)
                    for c in range(NC):
                        for h in range(2):
                            ins = pe.matmul(out_p[h * DH:(h + 1) * DH, :], v[par][:, c, h * DH:(h + 1) * DH],
                                            probsT[par][h][:, c, :], start=(c == 0), stop=(c == NC - 1))
                    ins.then_inc(o_done, 1)

                def step(s, par, first, last):
                    score(s, par, 0)
                    if not first:
                        turn(s - 1, 2)
                    if not last:
                        project_q(s + 1)
                    score(s, par, 1)
                    if not first:
                        turn(s - 1, 3)
                    if not last:
                        project_k(s + 1)
                    score(s, par, 2)
                    turn(s, 0)
                    if not last:
                        project_v(s + 1)
                    score(s, par, 3)
                    if not first:
                        attend(s - 1, 1 - par)
                    turn(s, 1)
                    if not last:
                        turn_v(s + 1)

                pe.wait_ge(zeroed, 4)
                project_q(0)
                project_k(0)
                project_v(0)
                turn_v(0)
                steps(pe, step)
                turn(STEPS - 1, 2)
                turn(STEPS - 1, 3)
                attend(STEPS - 1, (STEPS - 1) % 2)

            @block.scalar
            def _(act):
                def set_q(s, par):
                    act.wait_ge(q_done, s + 1)
                    wait(act, s_done, 4 * s - 4)
                    for h in range(2):
                        half = slice(h * DH, (h + 1) * DH)
                        ins = act.activation(q_h[par][half, h, :], proj_qv[half, 0:S], ACT.Copy, scale=QSCALE)
                    ins.then_inc(qh_set, 1)

                def set_k(s, par):
                    act.wait_ge(k_done, s + 1)
                    act.activation(k_h[par][:, :], proj_k[:, :], ACT.Copy).then_inc(kh_set, 1)

                def set_vT(s):
                    act.wait_ge(v_done, s + 1)
                    wait(act, vt_done, s)
                    act.activation(vT[:, :], proj_qv[:, :], ACT.Copy).then_inc(vT_set, 1)

                def set_v(s, par):
                    act.wait_ge(vt_done, s + 1)
                    wait(act, o_done, s - 1)
                    act.activation(v[par][:, :, :], turned_v[:, :, :], ACT.Copy).then_inc(v_set, 1)

                def exponent(s, j):
                    act.wait_ge(max_set, 4 * s + j + 1)
                    wait(act, t_done, 4 * s + j - 3)
                    act.activation(probs[j][:, :], scores[j % 2][:, :], ACT.Exp, bias=negmax[:, j:j + 1],
                                   accum_out=total[:, j:j + 1]).then_inc(exp_set, 1)

                def set_even(s, par, j):
                    act.wait_ge(t_done, 4 * s + j + 1)
                    wait(act, o_done, s - 1)
                    act.activation(probsT[par][j // 2][:, :, 0:P], turned_p[0][:, :, :], ACT.Copy).then_inc(even_set, 1)

                def step(s, par, first, last):
                    exponent(s, 0)
                    if not first:
                        set_even(s - 1, 1 - par, 2)
                    if not last:
                        set_q(s + 1, 1 - par)
                    exponent(s, 1)
                    if not last:
                        set_k(s + 1, 1 - par)
                    exponent(s, 2)
                    set_even(s, par, 0)
                    if not last:
                        set_vT(s + 1)
                    exponent(s, 3)
                    if not last:
                        set_v(s + 1, 1 - par)

                act.wait_ge(zeroed, 4)
                set_q(0, 0)
                set_k(0, 0)
                set_vT(0)
                set_v(0, 0)
                steps(act, step)
                set_even(STEPS - 1, (STEPS - 1) % 2, 2)

            @block.vector
            def _(dve):
                def part_q(s, par):
                    dve.wait_ge(qh_set, s + 1)
                    for h in range(2):
                        half = slice(h * DH, (h + 1) * DH)
                        ins = dve.scalar_tensor_tensor(q_l[par][half, h, :], proj_qv[half, 0:S], QSCALE,
                                                       q_h[par][half, h, :], ALU.mult, ALU.subtract)
                    ins.then_inc(ql_set, 1)

                def part_k(s, par):
                    dve.wait_ge(kh_set, s + 1)
                    dve.tensor_tensor(k_l[par][:, :], proj_k[:, :], k_h[par][:, :], ALU.subtract).then_inc(kl_set, 1)

                def maximum(s, j):
                    dve.wait_ge(s_done, 4 * s + j + 1)
                    dve.tensor_reduce(negmax[:, j:j + 1], scores[j % 2][:, :], AX.X, ALU.max,
                                      negate=True).then_inc(max_set, 1)

                def normalise(s, j):
                    dve.wait_ge(exp_set, 4 * s + j + 1)
                    dve.reciprocal(inverse[:, j:j + 1], total[:, j:j + 1]).then_inc(inv_set, 1)
                    dve.wait_ge(inv_set, 4 * s + j + 1)
                    dve.tensor_scalar(probs[j][:, :], probs[j][:, :], inverse[:, j:j + 1], None,
                                      ALU.mult).then_inc(norm_set, 1)

                def set_odd(s, par, j):
                    dve.wait_ge(t_done, 4 * s + j + 1)
                    wait(dve, o_done, s - 1)
                    dve.tensor_copy(probsT[par][j // 2][:, :, P:2 * P], turned_p[1][:, :, :]).then_inc(odd_set, 1)

                def set_out(s):
                    dve.wait_ge(o_done, s + 1)
                    dve.tensor_copy(g.big[:, bass.ds(s * S, S)], out_p[:, :]).then_inc(o_set, 1)

                def step(s, par, first, last):
                    maximum(s, 0)
                    if not first:
                        normalise(s - 1, 3)
                    if not last:
                        part_q(s + 1, 1 - par)
                    maximum(s, 1)
                    normalise(s, 0)
                    if not first:
                        set_odd(s - 1, 1 - par, 3)
                    if not last:
                        part_k(s + 1, 1 - par)
                    maximum(s, 2)
                    normalise(s, 1)
                    maximum(s, 3)
                    normalise(s, 2)
                    if not first:
                        set_out(s - 1)
                    set_odd(s, par, 1)

                dve.wait_ge(zeroed, 4)
                part_q(0, 0)
                part_k(0, 0)
                steps(dve, step)
                normalise(STEPS - 1, 3)
                set_odd(STEPS - 1, (STEPS - 1) % 2, 3)
                set_out(STEPS - 1)


class Norm:

    def __init__(self, ctx, nc, g, name):
        def sb(what, shape, dt):
            return [ctx.enter_context(nc.sbuf_tensor(f"{name}_{what}{i}", shape, dt)) for i in range(2)]

        def sem(what):
            return ctx.enter_context(nc.semaphore(f"{name}_{what}"))

        self.g = g
        self.stats, self.mv = sb("stats", [P, 2, 6], F32), sb("mv", [P, 2, 2], F32)
        self.std, self.rstd, self.tmp = sb("std", [P, 2], F32), sb("rstd", [P, 2], F32), sb("tmp", [P, 2], F32)
        self.xn = sb("xn", [P, 2, g.D], F32)
        self.full = sb("full", [P, g.KC, g.S], F32)
        self.have_var, self.have_std, self.normed = sem("have_var"), sem("have_std"), sem("normed")
        self.turned, self.filled = sem("turned"), sem("filled")
        self.high, self.low, self.chain = sem("high"), sem("low"), sem("chain")
        self.ps = [ctx.enter_context(nc.psum_tensor(f"{name}_ps{i}", [P, g.KC, g.S], F32)) for i in range(2)]

    def moments(self, dve, link, b, par):
        for t in range(2):
            ins = dve.bn_stats(self.stats[par][:, t, :], self.g.x[:, bass.ds(2 * b + t, 1), :])
        link(ins)
        for t in range(2):
            ins = dve.bn_aggr(self.mv[par][:, t, :], self.stats[par][:, t, :])
        ins.then_inc(self.have_var, 1)

    def root(self, act, b, par):
        act.wait_ge(self.have_var, b + 1)
        act.activation(self.std[par][:, :], self.mv[par][:, :, 1], ACT.Sqrt,
                       bias=self.g.eps[:, 0:1]).then_inc(self.have_std, 1)

    def apply(self, dve, link, b, par):
        dve.wait_ge(self.have_std, b + 1)
        inverse_root(dve, link, self.rstd[par][:, :], self.std[par][:, :], self.mv[par][:, :, 1], self.tmp[par][:, :])
        wait(dve, self.turned, b - 1)
        for t in range(2):
            ins = dve.tensor_scalar(self.xn[par][:, t, :], self.g.x[:, bass.ds(2 * b + t, 1), :],
                                    self.mv[par][:, t, 0:1], self.rstd[par][:, t:t + 1], ALU.subtract, ALU.mult)
        ins.then_inc(self.normed, 1)

    def turn(self, pe, b, par):
        pe.wait_ge(self.normed, b + 1)
        wait(pe, self.filled, b - 1)
        for kc in range(self.g.KC):
            for t in range(2):
                ins = pe.transpose(self.ps[par][:, kc, t * P:(t + 1) * P],
                                   self.xn[par][:, t, kc * P:(kc + 1) * P], self.g.ident[:, :])
        ins.then_inc(self.turned, 1)

    def fill(self, dve, b, par):
        dve.wait_ge(self.turned, b + 1)
        dve.tensor_copy(self.full[par][:, :, :], self.ps[par][:, :, :]).then_inc(self.filled, 1)

    def take_high(self, act, b, par):
        act.wait_ge(self.filled, b + 1)
        act.activation(self.g.xT_h[:, :, bass.ds(b * self.g.S, self.g.S)], self.full[par][:, :, :],
                       ACT.Copy).then_inc(self.high, 1)

    def take_low(self, pool, b, par):
        at = bass.ds(b * self.g.S, self.g.S)
        pool.wait_ge(self.high, b + 1)
        pool.tensor_tensor(self.g.xT_l[:, :, at], self.full[par][:, :, :], self.g.xT_h[:, :, at],
                           ALU.subtract).then_inc(self.low, 1)


def batches(eng, NB, step):
    def body(i, first, last):
        step(2 * i, 0, first, 1 if last else 0)
        step(2 * i + 1, 1, False, 2 if last else 0)

    unrolled(eng, NB // 2, body)


def add_attention(nc, g, io):
    NB, S, D, KC, E = g.NB, g.S, g.D, g.KC, g.E
    PAIRS = 8
    with ExitStack() as ctx:
        def sb(name, shape, dt):
            return ctx.enter_context(nc.sbuf_tensor(name, shape, dt))

        def sem(name):
            return ctx.enter_context(nc.semaphore(name))

        w_raw = sb("c_w_raw", [P, PAIRS, D], F32)
        w_h, w_l = sb("c_w_h", [P, PAIRS, D], F32R), sb("c_w_l", [P, PAIRS, D], F32R)
        router = sb("c_router", [P, KC, E], F32)
        o_h = [sb(f"c_o_h{i}", [P, PAIRS, S], F32R) for i in range(2)]
        o_l = [sb(f"c_o_l{i}", [P, PAIRS, S], F32R) for i in range(2)]
        sum_ps = [ctx.enter_context(nc.psum_tensor(f"c_sum{i}", [P, 2, D], F32)) for i in range(2)]
        logit_ps = [ctx.enter_context(nc.psum_tensor(f"c_logit{i}", [P, 2, E], F32)) for i in range(2)]
        w_in, r_in, wh_set, wl_set = sem("c_w_in"), sem("c_r_in"), sem("c_wh_set"), sem("c_wl_set")
        oh_set, ol_set, summed = sem("c_oh_set"), sem("c_ol_set"), sem("c_summed")
        logit_done, logit_set, kept = sem("c_logit_done"), sem("c_logit_set"), sem("c_kept")
        norm = Norm(ctx, nc, g, "c")
        o_of = g.big[:, :].rearrange("p (r b s) -> p r b s", r=PAIRS, b=NB)

        def o_batch(b):
            return o_of[:, :, bass.ds(b, 1), :].rearrange("p r a s -> p r (a s)")

        with nc.Block() as block:
            @block.sync
            def _(sp):
                sp.dma_start(w_raw[:, :, :], io["L0_xattn_Wo"].rearrange("(r p) n -> p r n", p=P)).then_inc(w_in, 16)
                sp.dma_start(router[:, :, :], io["L0_ffn_w_router_T"].rearrange("(c p) e -> p c e", p=P)).then_inc(r_in, 16)

            @block.gpsimd
            def _(pool):
                pool.wait_ge(wh_set, 1)
                pool.tensor_tensor(w_l[:, :, :], w_raw[:, :, :], w_h[:, :, :], ALU.subtract).then_inc(wl_set, 1)
                batches(pool, NB, lambda b, par, first, last: norm.take_low(pool, b, par))

            @block.scalar
            def _(act):
                def high_o(b, par):
                    wait(act, summed, b - 1)
                    act.activation(o_h[par][:, :, :], o_batch(b), ACT.Copy).then_inc(oh_set, 1)

                def keep(b, par):
                    act.wait_ge(norm.normed, b + 1)
                    act.activation(g.xn[:, bass.ds(2 * b, 2), :], norm.xn[par][:, :, :], ACT.Copy).then_inc(kept, 1)

                def take_logits(b, par):
                    act.wait_ge(logit_done, b + 1)
                    act.activation(g.logits[:, bass.ds(2 * b, 2), :], logit_ps[par][:, :, :],
                                   ACT.Copy).then_inc(logit_set, 1)

                def step(b, par, first, last):
                    norm.root(act, b, par)
                    if not last:
                        high_o(b + 2, par)
                    if not first:
                        norm.take_high(act, b - 1, 1 - par)
                        take_logits(b - 1, 1 - par)
                    keep(b, par)

                act.wait_ge(w_in, 16)
                act.activation(w_h[:, :, :], w_raw[:, :, :], ACT.Copy).then_inc(wh_set, 1)
                high_o(0, 0)
                high_o(1, 1)
                batches(act, NB, step)
                norm.take_high(act, NB - 1, 1)
                take_logits(NB - 1, 1)

            @block.tensor
            def _(pe):
                def add_up(b, par):
                    pe.wait_ge(ol_set, b + 1)
                    wait(pe, norm.have_var, b - 1)
                    passes = [(o, w, r) for r in range(PAIRS)
                              for o, w in ((o_h[par], w_h), (o_h[par], w_l), (o_l[par], w_h))]
                    for t in range(2):
                        for i, (o, w, r) in enumerate(passes):
                            ins = pe.matmul(sum_ps[par][:, t, :], o[:, r, t * P:(t + 1) * P], w[:, r, :],
                                            start=(i == 0), stop=(i == len(passes) - 1))
                    ins.then_inc(summed, 1)

                def route(b, par):
                    pe.wait_ge(norm.filled, b + 1)
                    wait(pe, logit_set, b - 1)
                    for t in range(2):
                        for kc in range(KC):
                            ins = pe.matmul(logit_ps[par][:, t, :], norm.full[par][:, kc, t * P:(t + 1) * P],
                                            router[:, kc, :], start=(kc == 0), stop=(kc == KC - 1))
                    ins.then_inc(logit_done, 1)

                def step(b, par, first, last):
                    if last < 2:
                        add_up(b + 1, 1 - par)
                    if not first:
                        route(b - 1, 1 - par)
                    norm.turn(pe, b, par)

                pe.wait_ge(wl_set, 1)
                pe.wait_ge(r_in, 16)
                add_up(0, 0)
                batches(pe, NB, step)
                route(NB - 1, 1)

            @block.vector
            def _(dve):
                link = Chain(dve, norm.chain)

                def low_o(b, par):
                    dve.wait_ge(oh_set, b + 1)
                    dve.tensor_tensor(o_l[par][:, :, :], o_batch(b), o_h[par][:, :, :], ALU.subtract).then_inc(ol_set, 1)

                def fill(b, par):
                    wait(dve, norm.low, b - 1)
                    wait(dve, logit_done, b - 1)
                    norm.fill(dve, b, par)

                def step(b, par, first, last):
                    link.restart()
                    if not first:
                        fill(b - 1, 1 - par)
                    dve.wait_ge(summed, b + 1)
                    rows = g.x[:, bass.ds(2 * b, 2), :]
                    link(dve.tensor_tensor(rows, rows, sum_ps[par][:, :, :], ALU.add))
                    norm.moments(dve, link, b, par)
                    if not last:
                        low_o(b + 2, par)
                    wait(dve, kept, b - 1)
                    norm.apply(dve, link, b, par)

                low_o(0, 0)
                low_o(1, 1)
                batches(dve, NB, step)
                fill(NB - 1, 1)


def route_tokens(nc, g, io):
    NT, E, D, BLOCKS = g.NT, g.E, g.D, g.BLOCKS
    with ExitStack() as ctx:
        def sb(name, shape, dt=F32):
            return ctx.enter_context(nc.sbuf_tensor(name, shape, dt))

        def sem(name):
            return ctx.enter_context(nc.semaphore(name))

        top, score = sb("r_top", [P, NT]), sb("r_score", [P, NT])
        order, first = sb("r_order", [P, E]), sb("r_first", [P, NT])
        hot, hot_b = sb("r_hot", [P, NT, E]), sb("r_hot_b", [P, NT, E], BF16)
        before_w, ones_w = sb("r_before_w", [P, P], BF16), sb("r_ones_w", [P, P], BF16)
        within, sums = sb("r_within", [P, NT, E]), [sb(f"r_sums{i}", [P, NT, E]) for i in range(2)]
        tile_sum = sb("r_tile_sum", [P, NT, E])
        padded_i, padded = sb("r_padded_i", [P, E], I32), sb("r_padded", [P, E])
        ends = [sb(f"r_ends{i}", [P, E]) for i in range(2)]
        starts, row = sb("r_starts", [P, E]), sb("r_row", [P, NT])
        block_start, past = sb("r_block_start", [P, BLOCKS]), sb("r_past", [P, BLOCKS, E])
        block_f = sb("r_block_f", [P, BLOCKS])
        count_ps = ctx.enter_context(nc.psum_tensor("r_count_ps", [P, NT, E], F32))
        total_ps = ctx.enter_context(nc.psum_tensor("r_total_ps", [P, NT, E], F32))
        const_set, ones_set, hot_set, counted = sem("r_const_set"), sem("r_ones_set"), sem("r_hot_set"), sem("r_counted")
        top_set, score_set, scaled = sem("r_top_set"), sem("r_score_set"), sem("r_scaled")
        row_set, scattered, chain = sem("r_row_set"), sem("r_scattered"), sem("r_chain")

        with nc.Block() as block:
            @block.gpsimd
            def _(pool):
                pool.iota(order[:, :], [[-1, E]], base=E, channel_multiplier=0,
                          allow_small_or_imprecise_dtypes=True).then_inc(const_set, 1)
                pool.iota(block_start[:, :], [[P, BLOCKS]], base=0, channel_multiplier=0,
                          allow_small_or_imprecise_dtypes=True).then_inc(const_set, 1)
                pool.memset(ones_w[:, :], 1.0).then_inc(ones_set, 1)
                pool.wait_ge(ones_set, 1)
                pool.affine_select(out=before_w[:, :], in_=ones_w[:, :], compare_op=ALU.is_gt, fill=0.0,
                                   base=0, pattern=[[1, P]], channel_multiplier=-1).then_inc(const_set, 1)
                pool.wait_ge(row_set, 1)
                pool.wait_ge(scaled, 1)
                for t in range(NT):
                    pool.indirect_dma_start(g.rows_in[:, :], bass.IndirectOffsetOnAxis(ap=g.row_of[:, t:t + 1], axis=0),
                                            g.xn[:, t, :], None).then_inc(scattered, 16)
                pool.wait_ge(scattered, 16 * NT)

            @block.scalar
            def _(act):
                act.wait_ge(top_set, 1)
                act.activation(score[:, :], top[:, :], ACT.Sigmoid).then_inc(score_set, 1)

            @block.tensor
            def _(pe):
                pe.wait_ge(const_set, 3)
                pe.wait_ge(hot_set, 1)
                pe.matmul(count_ps[:, :, :], before_w[:, :], hot_b[:, :, :], start=True, stop=True)
                pe.matmul(total_ps[:, :, :], ones_w[:, :], hot_b[:, :, :], start=True, stop=True).then_inc(counted, 1)

            @block.vector
            def _(dve):
                link = Chain(dve, chain)

                def over(ap, n):
                    return ap.unsqueeze(1).to_broadcast([P, n, ap.shape[-1]])

                def along(ap, n):
                    return ap.unsqueeze(2).to_broadcast([P, ap.shape[-1], n])

                def running(bufs, at, n):
                    src, k = 0, 1
                    while k < n:
                        a, b = bufs[src], bufs[1 - src]
                        dve.tensor_copy(at(b, 0, k), at(a, 0, k))
                        link(dve.tensor_tensor(at(b, k, n), at(a, k, n), at(a, 0, n - k), ALU.add))
                        src, k = 1 - src, 2 * k
                    return bufs[src]

                dve.tensor_reduce(top[:, :], g.logits[:, :, :], AX.X, ALU.max).then_inc(top_set, 1)
                dve.wait_ge(top_set, 1)
                link(dve.tensor_tensor(hot[:, :, :], g.logits[:, :, :], along(top[:, :], E), ALU.is_equal))
                dve.wait_ge(const_set, 3)
                link(dve.tensor_tensor(hot[:, :, :], hot[:, :, :], over(order[:, :], NT), ALU.mult))
                link(dve.tensor_reduce(first[:, :], hot[:, :, :], AX.X, ALU.max))
                link(dve.tensor_tensor(hot[:, :, :], hot[:, :, :], along(first[:, :], E), ALU.is_equal))
                dve.tensor_copy(hot_b[:, :, :], hot[:, :, :]).then_inc(hot_set, 1)
                dve.wait_ge(score_set, 1)
                for t in range(NT):
                    ins = dve.tensor_scalar(g.xn[:, t, :], g.xn[:, t, :], score[:, t:t + 1], None, ALU.mult)
                ins.then_inc(scaled, 1)
                dve.wait_ge(counted, 1)
                dve.tensor_copy(within[:, :, :], count_ps[:, :, :])
                dve.tensor_copy(tile_sum[:, :, :], total_ps[:, :, :])
                link(dve.tensor_copy(sums[0][:, :, :], total_ps[:, :, :]))
                upto = running(sums, lambda a, i, j: a[:, i:j, :], NT)
                link(dve.tensor_tensor(within[:, :, :], within[:, :, :], tile_sum[:, :, :], ALU.subtract))
                link(dve.tensor_tensor(within[:, :, :], within[:, :, :], upto[:, :, :], ALU.add))
                link(dve.tensor_scalar(padded[:, :], upto[:, NT - 1, :], float(P - 1), None, ALU.add))
                link(dve.tensor_copy(padded_i[:, :], padded[:, :]))
                shift = P.bit_length() - 1
                link(dve.tensor_scalar(padded_i[:, :], padded_i[:, :], shift, shift,
                                       ALU.logical_shift_right, ALU.logical_shift_left))
                dve.tensor_copy(padded[:, :], padded_i[:, :])
                link(dve.tensor_copy(ends[0][:, :], padded_i[:, :]))
                end = running(ends, lambda a, i, j: a[:, i:j], E)
                link(dve.tensor_tensor(starts[:, :], end[:, :], padded[:, :], ALU.subtract))
                link(dve.tensor_tensor(within[:, :, :], within[:, :, :], over(starts[:, :], NT), ALU.add))
                link(dve.tensor_tensor(within[:, :, :], within[:, :, :], hot[:, :, :], ALU.mult))
                link(dve.tensor_reduce(row[:, :], within[:, :, :], AX.X, ALU.add))
                dve.tensor_copy(g.row_of[:, :], row[:, :]).then_inc(row_set, 1)
                link(dve.tensor_tensor(past[:, :, :], along(block_start[:, :], E), over(end[:, :], BLOCKS), ALU.is_ge))
                link(dve.tensor_reduce(block_f[:, :], past[:, :, :], AX.X, ALU.add))
                link(dve.tensor_scalar(block_f[:, :], block_f[:, :], float(E - 1), None, ALU.min))
                link(dve.tensor_copy(g.block_expert[:, :], block_f[:, :]))


def run_experts(nc, g, io):
    D, KC, F, BLOCKS = g.D, g.KC, g.F, g.BLOCKS
    FC = F // P
    AHEAD = 4
    with ExitStack() as ctx:
        def sb(name, shape, dt=F32, n=2):
            return [ctx.enter_context(nc.sbuf_tensor(f"{name}{i}", shape, dt)) for i in range(n)]

        def psum(name, shape):
            return ctx.enter_context(nc.psum_tensor(name, shape, F32))

        def sem(name):
            return ctx.enter_context(nc.semaphore(name))

        rows, rowsT = sb("e_rows", [P, D], n=AHEAD), sb("e_rowsT", [P, KC, P])
        w_in, w_out = sb("e_w_in", [P, KC, 2 * F], n=AHEAD), sb("e_w_out", [P, FC, D], n=AHEAD)
        silu, hidden, hiddenT = sb("e_silu", [P, F]), sb("e_hidden", [P, F]), sb("e_hiddenT", [P, FC, P])
        result = sb("e_result", [P, D])
        gate_ps = [psum(f"e_gate{i}", [P, F]) for i in range(2)]
        up_ps = [psum(f"e_up{i}", [P, F]) for i in range(2)]
        rowsT_ps, hiddenT_ps, result_ps = psum("e_rowsT_ps", [P, KC, P]), psum("e_hiddenT_ps", [P, FC, P]), psum("e_result_ps", [P, D])
        rows_in = [sem(f"e_rows_in{i}") for i in range(AHEAD)]
        w_in_in = [sem(f"e_w_in_in{i}") for i in range(AHEAD)]
        w_out_in = [sem(f"e_w_out_in{i}") for i in range(AHEAD)]
        rows_turned, rowsT_set, gated, upped = sem("e_rows_turned"), sem("e_rowsT_set"), sem("e_gated"), sem("e_upped")
        silu_set, hidden_set, hidden_turned, hiddenT_set = sem("e_silu_set"), sem("e_hidden_set"), sem("e_hidden_turned"), sem("e_hiddenT_set")
        summed, result_set = sem("e_summed"), sem("e_result_set")
        stored = [sem(f"e_stored{i}") for i in range(2)]
        in_dram = io["L0_ffn_gate_up_proj"].rearrange("e (c p) f -> p e c f", p=P)
        out_dram = io["L0_ffn_down_proj"].rearrange("e (c p) d -> p e c d", p=P)
        rows_dram = g.rows_in[:, :].rearrange("(j p) d -> p j d", p=P)
        results_dram = g.rows_out[:, :].rearrange("(j p) d -> p j d", p=P)

        ROUNDS = -(-BLOCKS // AHEAD)
        LAST = (BLOCKS - 1) % AHEAD

        def blocks(eng, step):
            def body(i, first, last):
                n = BLOCKS - AHEAD * (ROUNDS - 1) if last else AHEAD
                for q in range(n):
                    step(AHEAD * i + q, q, i, first and q == 0, last and q == n - 1)

            unrolled(eng, ROUNDS, body)

        with nc.Block() as block:
            @block.sync
            def _(sp):
                def load(j, q, i, first, last):
                    wait(sp, rows_turned, j - AHEAD + 1)
                    sp.dma_start(rows[q][:, :], rows_dram[:, bass.ds(j, 1), :]).then_inc(rows_in[q], 16)
                    expert = sp.value_load(g.block_expert[0:1, bass.ds(j, 1)], min_val=0, max_val=g.E - 1)
                    wait(sp, upped, j - AHEAD + 1)
                    sp.dma_start(w_in[q][:, :, :], in_dram[:, bass.ds(expert, 1), :, :]).then_inc(w_in_in[q], 16)
                    wait(sp, summed, j - AHEAD + 1)
                    sp.dma_start(w_out[q][:, :, :], out_dram[:, bass.ds(expert, 1), :, :]).then_inc(w_out_in[q], 16)

                blocks(sp, load)

            @block.gpsimd
            def _(pool):
                def store(j, q, i, first, last):
                    pool.wait_ge(result_set, j + 1)
                    pool.dma_start(results_dram[:, bass.ds(j, 1), :], result[q % 2][:, :]).then_inc(stored[q % 2], 16)

                blocks(pool, store)
                for par in range(2):
                    pool.wait_ge(stored[par], 16 * len(range(par, BLOCKS, 2)))

            @block.tensor
            def _(pe):
                def turn_rows(j, q, i):
                    pe.wait_ge(rows_in[q], 16 * i + 16)
                    wait(pe, rowsT_set, j)
                    for c in range(KC):
                        ins = pe.transpose(rowsT_ps[:, c, :], rows[q][:, c * P:(c + 1) * P], g.ident[:, :])
                    ins.then_inc(rows_turned, 1)

                def product(out, q, half, done):
                    for c in range(KC):
                        ins = pe.matmul(out[q % 2][:, :], rowsT[q % 2][:, c, :], w_in[q][:, c, half * F:(half + 1) * F],
                                        start=(c == 0), stop=(c == KC - 1))
                    ins.then_inc(done, 1)

                def turn_hidden(j, q):
                    pe.wait_ge(hidden_set, j + 1)
                    wait(pe, hiddenT_set, j)
                    for c in range(FC):
                        ins = pe.transpose(hiddenT_ps[:, c, :], hidden[q % 2][:, c * P:(c + 1) * P], g.ident[:, :])
                    ins.then_inc(hidden_turned, 1)

                def down(j, q, i):
                    pe.wait_ge(hiddenT_set, j + 1)
                    pe.wait_ge(w_out_in[q], 16 * i + 16)
                    wait(pe, result_set, j)
                    for c in range(FC):
                        ins = pe.matmul(result_ps[:, :], hiddenT[q % 2][:, c, :], w_out[q][:, c, :],
                                        start=(c == 0), stop=(c == FC - 1))
                    ins.then_inc(summed, 1)

                def step(j, q, i, first, last):
                    if not last:
                        turn_rows(j + 1, (q + 1) % AHEAD, i + (q + 1) // AHEAD)
                    pe.wait_ge(rowsT_set, j + 1)
                    pe.wait_ge(w_in_in[q], 16 * i + 16)
                    wait(pe, hidden_set, j - 1)
                    product(gate_ps, q, 0, gated)
                    if not first:
                        turn_hidden(j - 1, (q - 1) % AHEAD)
                    product(up_ps, q, 1, upped)
                    if not first:
                        down(j - 1, (q - 1) % AHEAD, i if q else i - 1)

                turn_rows(0, 0, 0)
                blocks(pe, step)
                turn_hidden(BLOCKS - 1, LAST)
                down(BLOCKS - 1, LAST, ROUNDS - 1)

            @block.scalar
            def _(act):
                def take_result(j, q, i):
                    act.wait_ge(summed, j + 1)
                    wait(act, stored[q % 2], 16 * ((AHEAD // 2) * i + q // 2))
                    act.activation(result[q % 2][:, :], result_ps[:, :], ACT.Copy).then_inc(result_set, 1)

                def step(j, q, i, first, last):
                    act.wait_ge(gated, j + 1)
                    wait(act, hidden_set, j - 1)
                    act.activation(silu[q % 2][:, :], gate_ps[q % 2][:, :], ACT.Silu).then_inc(silu_set, 1)
                    if not first:
                        take_result(j - 1, (q - 1) % AHEAD, i if q else i - 1)

                blocks(act, step)
                take_result(BLOCKS - 1, LAST, ROUNDS - 1)

            @block.vector
            def _(dve):
                def set_rowsT(j, q):
                    dve.wait_ge(rows_turned, j + 1)
                    wait(dve, upped, j - 1)
                    dve.tensor_copy(rowsT[q % 2][:, :, :], rowsT_ps[:, :, :]).then_inc(rowsT_set, 1)

                def set_hiddenT(j, q):
                    dve.wait_ge(hidden_turned, j + 1)
                    wait(dve, summed, j - 1)
                    dve.tensor_copy(hiddenT[q % 2][:, :, :], hiddenT_ps[:, :, :]).then_inc(hiddenT_set, 1)

                def step(j, q, i, first, last):
                    if not last:
                        set_rowsT(j + 1, (q + 1) % AHEAD)
                    if not first:
                        set_hiddenT(j - 1, (q - 1) % AHEAD)
                    dve.wait_ge(silu_set, j + 1)
                    dve.wait_ge(upped, j + 1)
                    wait(dve, hidden_turned, j - 1)
                    dve.tensor_tensor(hidden[q % 2][:, :], up_ps[q % 2][:, :], silu[q % 2][:, :], ALU.mult).then_inc(hidden_set, 1)

                set_rowsT(0, 0)
                blocks(dve, step)
                set_hiddenT(BLOCKS - 1, LAST)


def shared_expert(nc, g, io):
    D, KC, F, NT = g.D, g.KC, g.F, g.NT
    FC = F // P
    N = 512
    TILES = N // P
    GROUPS = NT // TILES
    with ExitStack() as ctx:
        def sb(name, shape, dt=F32):
            return ctx.enter_context(nc.sbuf_tensor(name, shape, dt))

        def psum(name, shape):
            return ctx.enter_context(nc.psum_tensor(name, shape, F32))

        def sem(name):
            return ctx.enter_context(nc.semaphore(name))

        names = ("L0_ffn_w_gate_T", "L0_ffn_w_up_T", "L0_ffn_w_down_T")
        raw = [sb("s_raw_g", [P, KC, F]), sb("s_raw_u", [P, KC, F]), sb("s_raw_d", [P, FC, D])]
        w_h = [sb("s_h_g", [P, KC, F], F32R), sb("s_h_u", [P, KC, F], F32R), sb("s_h_d", [P, FC, D], F32R)]
        w_l = [sb("s_l_g", [P, KC, F], F32R), sb("s_l_u", [P, KC, F], F32R), sb("s_l_d", [P, FC, D], F32R)]
        silu, hidden = [sb(f"s_silu{i}", [P, N]) for i in range(2)], [sb(f"s_hidden{i}", [P, N]) for i in range(2)]
        hid_h, hid_l = sb("s_hid_h", [P, FC, N], F32R), sb("s_hid_l", [P, FC, N], F32R)
        gate_ps = [psum(f"s_gate{i}", [P, N]) for i in range(2)]
        up_ps = [psum(f"s_up{i}", [P, N]) for i in range(2)]
        sum_ps = [psum(f"s_sum{i}", [P, 2, D]) for i in range(2)]
        w_in, wh_set, wl_set = sem("s_w_in"), sem("s_wh_set"), sem("s_wl_set")
        gated, upped, silu_set, hidden_set = sem("s_gated"), sem("s_upped"), sem("s_silu_set"), sem("s_hidden_set")
        high, low, summed, added = sem("s_high"), sem("s_low"), sem("s_summed"), sem("s_added")

        with nc.Block() as block:
            @block.sync
            def _(sp):
                for dst, name in zip(raw, names):
                    sp.dma_start(dst[:, :, :], io[name].rearrange("(c p) n -> p c n", p=P)).then_inc(w_in, 16)

            @block.scalar
            def _(act):
                act.wait_ge(w_in, 48)
                for i in range(3):
                    act.activation(w_h[i][:, :, :], raw[i][:, :, :], ACT.Copy).then_inc(wh_set, 1)

                def silu_of(s, n):
                    act.wait_ge(gated, n + 1)
                    wait(act, hidden_set, n - 1)
                    act.activation(silu[s % 2][:, :], gate_ps[s % 2][:, :], ACT.Silu).then_inc(silu_set, 1)

                def high_of(s, n, grp):
                    act.wait_ge(hidden_set, n + 1)
                    wait(act, summed, grp)
                    act.activation(hid_h[:, s, :], hidden[s % 2][:, :], ACT.Copy).then_inc(high, 1)

                for grp in range(GROUPS):
                    for s in range(FC):
                        silu_of(s, FC * grp + s)
                        high_of(s, FC * grp + s, grp)

            @block.gpsimd
            def _(pool):
                for i in range(3):
                    pool.wait_ge(wh_set, i + 1)
                    pool.tensor_tensor(w_l[i][:, :, :], raw[i][:, :, :], w_h[i][:, :, :], ALU.subtract).then_inc(wl_set, 1)
                for n in range(GROUPS * FC):
                    pool.wait_ge(high, n + 1)
                    pool.tensor_tensor(hid_l[:, n % FC, :], hidden[n % 2][:, :], hid_h[:, n % FC, :],
                                       ALU.subtract).then_inc(low, 1)

            @block.tensor
            def _(pe):
                def product(out, i, c, grp, done):
                    at = slice(grp * N, (grp + 1) * N)
                    passes = [(w, x, kc) for kc in range(KC)
                              for w, x in ((w_h, g.xT_h), (w_h, g.xT_l), (w_l, g.xT_h))]
                    for k, (w, x, kc) in enumerate(passes):
                        ins = pe.matmul(out[:, :], w[i][:, kc, c * P:(c + 1) * P], x[:, kc, at],
                                        start=(k == 0), stop=(k == len(passes) - 1))
                    ins.then_inc(done, 1)

                pe.wait_ge(wl_set, 2)
                for grp in range(GROUPS):
                    for c in range(FC):
                        n = FC * grp + c
                        wait(pe, hidden_set, n - 1)
                        product(gate_ps[n % 2], 0, c, grp, gated)
                        product(up_ps[n % 2], 1, c, grp, upped)
                    pe.wait_ge(wl_set, 3)
                    pe.wait_ge(low, FC * (grp + 1))
                    wait(pe, added, grp)
                    passes = [(h, w, c) for c in range(FC)
                              for h, w in ((hid_h, w_h), (hid_h, w_l), (hid_l, w_h))]
                    for t in range(TILES):
                        for k, (h, w, c) in enumerate(passes):
                            ins = pe.matmul(sum_ps[t // 2][:, t % 2, :], h[:, c, t * P:(t + 1) * P], w[2][:, c, :],
                                            start=(k == 0), stop=(k == len(passes) - 1))
                    ins.then_inc(summed, 1)

            @block.vector
            def _(dve):
                def add(grp):
                    dve.wait_ge(summed, grp + 1)
                    for i in range(2):
                        rows = g.x[:, grp * TILES + 2 * i:grp * TILES + 2 * i + 2, :]
                        ins = dve.tensor_tensor(rows, rows, sum_ps[i][:, :, :], ALU.add)
                    ins.then_inc(added, 1)

                for grp in range(GROUPS):
                    for c in range(FC):
                        n = FC * grp + c
                        dve.wait_ge(silu_set, n + 1)
                        dve.wait_ge(upped, n + 1)
                        wait(dve, low, n - 1)
                        dve.tensor_tensor(hidden[c % 2][:, :], up_ps[c % 2][:, :], silu[c % 2][:, :],
                                          ALU.mult).then_inc(hidden_set, 1)
                    add(grp)


def gather_rows(nc, g, io):
    NB, NT = g.NB, g.NT
    with ExitStack() as ctx:
        gathered = [ctx.enter_context(nc.semaphore(f"g_gathered{i}")) for i in range(NB)]
        all_added = ctx.enter_context(nc.semaphore("g_added"))
        norm = Norm(ctx, nc, g, "g")
        with nc.Block() as block:
            @block.gpsimd
            def _(pool):
                for t in range(NT):
                    pool.indirect_dma_start(g.xn[:, t, :], None, g.rows_out[:, :],
                                            bass.IndirectOffsetOnAxis(ap=g.row_of[:, t:t + 1], axis=0)
                                            ).then_inc(gathered[t // 2], 16)
                batches(pool, NB, lambda b, par, first, last: norm.take_low(pool, b, par))

            @block.scalar
            def _(act):
                def step(b, par, first, last):
                    norm.root(act, b, par)
                    if not first:
                        norm.take_high(act, b - 1, 1 - par)

                batches(act, NB, step)
                norm.take_high(act, NB - 1, 1)

            @block.tensor
            def _(pe):
                batches(pe, NB, lambda b, par, first, last: norm.turn(pe, b, par))

            @block.vector
            def _(dve):
                for b in range(NB):
                    dve.wait_ge(gathered[b], 32)
                    rows = g.x[:, 2 * b:2 * b + 2, :]
                    ins = dve.tensor_tensor(rows, rows, g.xn[:, 2 * b:2 * b + 2, :], ALU.add)
                ins.then_inc(all_added, 1)
                dve.wait_ge(all_added, 1)
                link = Chain(dve, norm.chain)

                def fill(b, par):
                    wait(dve, norm.low, b - 1)
                    norm.fill(dve, b, par)

                def step(b, par, first, last):
                    link.restart()
                    norm.moments(dve, link, b, par)
                    if not first:
                        fill(b - 1, 1 - par)
                    norm.apply(dve, link, b, par)

                batches(dve, NB, step)
                fill(NB - 1, 1)


def attend_context(nc, g, io):
    NB, S, D, KC = g.NB, g.S, g.D, g.KC
    HEADS, DH = 16, 16
    SCALE = 1.0 / D ** 0.5
    PER = P // DH
    UNITS, GROUPS, PAD = 16, 4, 32
    with ExitStack() as ctx:
        def sb(name, shape, dt=F32):
            return ctx.enter_context(nc.sbuf_tensor(name, shape, dt))

        def psum(name, shape):
            return ctx.enter_context(nc.psum_tensor(name, shape, F32))

        def sem(name):
            return ctx.enter_context(nc.semaphore(name))

        raw = [sb(f"h_raw{i}", [P, KC, D]) for i in range(3)]
        w_h = [sb(f"h_w_h{i}", [P, KC, D], F32R) for i in range(3)]
        w_l = [sb(f"h_w_l{i}", [P, KC, D], F32R) for i in range(3)]
        WQ, WK, WV = range(3)
        out_raw = sb("h_out_raw", [P, GROUPS, D])
        out_h, out_l = sb("h_out_h", [P, GROUPS, D], F32R), sb("h_out_l", [P, GROUPS, D], F32R)
        bias_q, bias_k = sb("h_bias_q", [P, KC]), sb("h_bias_k", [P, KC])
        bias_v, bias_o = sb("h_bias_v", [P, D]), sb("h_bias_o", [P, D])
        mask = sb("h_mask", [P, PER])
        ctx_raw = sb("h_ctx", [P, KC, S])
        ctx_h, ctx_l = sb("h_ctx_h", [P, KC, S], F32R), sb("h_ctx_l", [P, KC, S], F32R)
        q_h = [sb(f"h_q_h{i}", [P, KC, S], F32R) for i in range(2)]
        q_l = [sb(f"h_q_l{i}", [P, KC, S], F32R) for i in range(2)]
        k_full = sb("h_k", [P, KC, S])
        k_h, k_l = sb("h_k_h", [P, KC, S], F32R), sb("h_k_l", [P, KC, S], F32R)
        kz_h, kz_l = sb("h_kz_h", [P, KC, PER, S], F32R), sb("h_kz_l", [P, KC, PER, S], F32R)
        probsT = [sb(f"h_probsT{i}", [P, 4, 2, S]) for i in range(2)]
        probs = [sb(f"h_probs{i}", [P, 2, S]) for i in range(4)]
        v = [sb(f"h_v{i}", [P, 2, HEADS, PAD]) for i in range(2)]
        negmax, total = sb("h_negmax", [P, 4, 2]), sb("h_total", [P, 2, 2, 4])
        one_inverse = sb("h_one_inverse", [P, 2, 4])
        inverse = [sb(f"h_inverse{i}", [P, 2, 4, PAD]) for i in range(2)]
        scale_T, o_full = sb("h_scale_T", [P, 2, S]), [sb(f"h_o{i}", [P, S]) for i in range(2)]
        o_h, o_l = sb("h_o_h", [P, GROUPS, S], F32R), sb("h_o_l", [P, GROUPS, S], F32R)
        scores = [psum(f"h_scores{i}", [P, 2, S]) for i in range(2)]
        turned_p = [psum(f"h_turned{i}", [P, 2, 2, P]) for i in range(2)]
        proj, out_p, y_p = psum("h_proj", [P, 2, S]), psum("h_out", [P, 2, S]), psum("h_y", [P, 2, D])
        loaded, ctx_in, zeroed, mask_set = sem("h_loaded"), sem("h_ctx_in"), sem("h_zeroed"), sem("h_mask_set")
        wh_set, wl_set, raw_set, chain = sem("h_wh_set"), sem("h_wl_set"), sem("h_raw_set"), sem("h_chain")
        ctxh_set, ctxl_set = sem("h_ctxh_set"), sem("h_ctxl_set")
        q_done, qh_set, ql_set = sem("h_q_done"), sem("h_qh_set"), sem("h_ql_set")
        k_done, k_set, kh_set, kl_set, kz_set = sem("h_k_done"), sem("h_k_set"), sem("h_kh_set"), sem("h_kl_set"), sem("h_kz_set")
        v_done, v_set = sem("h_v_done"), sem("h_v_set")
        scored, max_set, exp_set, turned = sem("h_scored"), sem("h_max_set"), sem("h_exp_set"), sem("h_turned")
        even_set, odd_set = sem("h_even_set"), sem("h_odd_set")
        recip_set, inv_set = sem("h_recip_set"), sem("h_inv_set")
        o_done, scaleT_set, o_set, oh_set, ol_set = sem("h_o_done"), sem("h_scaleT_set"), sem("h_o_set"), sem("h_oh_set"), sem("h_ol_set")
        y_done, added, biased = sem("h_y_done"), sem("h_added"), sem("h_biased")
        LOADS = 3 + 4 + 4
        ctx_dram = io["ctx_T"].rearrange("(c p) t -> p c t", p=P)

        with nc.Block() as block:
            @block.sync
            def _(sp):
                sp.dma_start(ctx_raw[:, :, :], ctx_dram[:, :, 0:S]).then_inc(ctx_in, 16)
                for i, name in enumerate(("Wq", "Wk", "Wv")):
                    sp.dma_start(raw[i][:, :, :], io[f"L1_xattn_{name}_T"].rearrange("(c p) n -> p c n", p=P)).then_inc(loaded, 16)
                sp.dma_start(bias_q[:, :], io["L1_xattn_bq"]).then_inc(loaded, 16)
                sp.dma_start(bias_k[:, :], io["L1_xattn_bk"]).then_inc(loaded, 16)
                sp.dma_start(bias_v[:, :], io["L1_xattn_bv"].partition_broadcast(P)).then_inc(loaded, 16)
                sp.dma_start(bias_o[:, :], io["L1_xattn_bo"].partition_broadcast(P)).then_inc(loaded, 16)
                sp.wait_ge(zeroed, 1)
                rows = io["L1_xattn_Wo_T"].rearrange("(r j p) n -> j p r n", j=4, p=DH)
                for j in range(4):
                    sp.dma_start(out_raw[PAD * j:PAD * j + DH, :, :], rows[j]).then_inc(loaded, 16)

                def load(b):
                    sp.wait_ge(ctxl_set, b)
                    sp.dma_start(ctx_raw[:, :, :], ctx_dram[:, :, bass.ds(b * S, S)]).then_inc(ctx_in, 16)

                with sp.Fori(1, NB) as b:
                    load(b)

            @block.gpsimd
            def _(pool):
                def pad(m, b):
                    def heads(part):
                        return part[:, m, :].unsqueeze(1).to_broadcast([P, PER, S])

                    own = mask[:, :].unsqueeze(2).to_broadcast([P, PER, S])
                    pool.wait_ge(kl_set, b + 1)
                    wait(pool, scored, UNITS * (b - 1) + (m + 1) * UNITS // 2)
                    pool.tensor_tensor(kz_h[:, m, :, :], heads(k_h), own, ALU.mult)
                    pool.tensor_tensor(kz_l[:, m, :, :], heads(k_l), own, ALU.mult).then_inc(kz_set, 1)

                def low_k(b):
                    pool.wait_ge(kh_set, b + 1)
                    pool.tensor_tensor(k_l[:, :, :], k_full[:, :, :], k_h[:, :, :], ALU.subtract).then_inc(kl_set, 1)

                def low_ctx(b):
                    pool.wait_ge(ctxh_set, b + 1)
                    pool.tensor_tensor(ctx_l[:, :, :], ctx_raw[:, :, :], ctx_h[:, :, :], ALU.subtract).then_inc(ctxl_set, 1)

                def low_o(b, grp):
                    pool.wait_ge(oh_set, GROUPS * b + grp + 1)
                    pool.tensor_tensor(o_l[:, grp, :], o_full[grp % 2][:, :], o_h[:, grp, :], ALU.subtract).then_inc(ol_set, 1)

                def add_bias(b):
                    rows = g.x[:, bass.ds(2 * b, 2), :]
                    pool.tensor_tensor(rows, rows, bias_o[:, :].unsqueeze(1).to_broadcast([P, 2, D]),
                                       ALU.add).then_inc(biased, 1)

                def step(b, par, first, last):
                    pad(1, b)
                    add_bias(b)
                    if not first:
                        low_o(b - 1, 2)
                        low_o(b - 1, 3)
                    if last < 2:
                        low_k(b + 1)
                        pad(0, b + 1)
                    low_o(b, 0)
                    low_o(b, 1)
                    if not last:
                        low_ctx(b + 2)

                pool.memset(out_raw[:, :, :], 0.0).then_inc(zeroed, 1)
                for i in range(2):
                    pool.memset(v[i][:, :, :, :], 0.0).then_inc(zeroed, 1)
                link = Chain(pool, chain)
                link(pool.memset(mask[:, :], 1.0))
                link(pool.affine_select(out=mask[:, :], in_=mask[:, :], compare_op=ALU.is_ge, fill=0.0,
                                        base=0, pattern=[[-DH, PER]], channel_multiplier=1))
                link(pool.affine_select(out=mask[:, :], in_=mask[:, :], compare_op=ALU.is_ge, fill=0.0,
                                        base=DH - 1, pattern=[[DH, PER]], channel_multiplier=-1))
                low_ctx(0)
                for n, (low, full, high) in enumerate([(w_l[i], raw[i], w_h[i]) for i in range(3)] + [(out_l, out_raw, out_h)]):
                    pool.wait_ge(wh_set, n + 1)
                    pool.tensor_tensor(low[:, :, :], full[:, :, :], high[:, :, :], ALU.subtract).then_inc(wl_set, 1)
                low_k(0)
                pad(0, 0)
                low_ctx(1)
                batches(pool, NB, step)
                low_o(NB - 1, 2)
                low_o(NB - 1, 3)

            @block.scalar
            def _(act):
                def high_ctx(b):
                    act.wait_ge(ctx_in, 16 * b + 16)
                    wait(act, v_done, b)
                    act.activation(ctx_h[:, :, :], ctx_raw[:, :, :], ACT.Copy).then_inc(ctxh_set, 1)

                def set_q(b, par):
                    act.wait_ge(q_done, b + 1)
                    for m in range(KC):
                        ins = act.activation(q_h[par][:, m, :], proj[:, m, :], ACT.Identity, bias=bias_q[:, m:m + 1])
                    ins.then_inc(qh_set, 1)

                def set_k(b):
                    act.wait_ge(k_done, b + 1)
                    wait(act, kz_set, 2 * b)
                    for m in range(KC):
                        ins = act.activation(k_full[:, m, :], proj[:, m, :], ACT.Identity, bias=bias_k[:, m:m + 1])
                    ins.then_inc(k_set, 1)
                    act.wait_ge(k_set, b + 1)
                    act.activation(k_h[:, :, :], k_full[:, :, :], ACT.Copy).then_inc(kh_set, 1)

                def exponent(b, u):
                    n = UNITS * b + u
                    pair, half = (u // 2) % 2, u % 2
                    act.wait_ge(max_set, n + 1)
                    wait(act, turned, n - 3)
                    if u % 4 == 0:
                        wait(act, inv_set, GROUPS * b + u // 4 - 1)
                    for h in range(2):
                        ins = act.activation(probs[u % 4][:, h, :], scores[u % 2][:, h, :], ACT.Exp,
                                             bias=negmax[:, u % 4, h:h + 1],
                                             accum_out=total[:, (u // 4) % 2, half, 2 * pair + h:2 * pair + h + 1])
                    ins.then_inc(exp_set, 1)

                def set_even(b, u):
                    n = UNITS * b + u
                    act.wait_ge(turned, n + 1)
                    wait(act, o_done, GROUPS * b + u // 4 - 1)
                    pair = (u // 2) % 2
                    act.activation(probsT[(u // 4) % 2][:, 2 * pair:2 * pair + 2, :, 0:P], turned_p[0][:, :, :, :],
                                   ACT.Copy).then_inc(even_set, 1)

                def high_o(b, grp):
                    act.wait_ge(o_set, GROUPS * b + grp + 1)
                    if grp == 0:
                        wait(act, y_done, b)
                    act.activation(o_h[:, grp, :], o_full[grp % 2][:, :], ACT.Copy).then_inc(oh_set, 1)

                def step(b, par, first, last):
                    for u in range(UNITS):
                        exponent(b, u)
                        if u == 1 and not first:
                            high_o(b - 1, 2)
                        if u == 5 and not first:
                            high_o(b - 1, 3)
                        if u == 6 and last < 2:
                            set_k(b + 1)
                        if u == 9:
                            high_o(b, 0)
                        if u == 10 and last < 2:
                            set_q(b + 1, 1 - par)
                        if u == 13:
                            high_o(b, 1)
                        if u == 14 and not last:
                            high_ctx(b + 2)
                        if u % 2 == 0 and u >= 2:
                            set_even(b, u - 2)
                        if u == 0 and not first:
                            set_even(b - 1, UNITS - 2)

                high_ctx(0)
                act.wait_ge(loaded, 16 * LOADS)
                act.wait_ge(raw_set, 1)
                for n in range(3):
                    act.activation(w_h[n][:, :, :], raw[n][:, :, :], ACT.Copy).then_inc(wh_set, 1)
                act.activation(out_h[:, :, :], out_raw[:, :, :], ACT.Copy).then_inc(wh_set, 1)
                set_k(0)
                set_q(0, 0)
                high_ctx(1)
                batches(act, NB, step)
                set_even(NB - 1, UNITS - 2)
                high_o(NB - 1, 2)
                high_o(NB - 1, 3)

            @block.tensor
            def _(pe):
                def threefold(out, stationary, moving, kcs):
                    passes = [(s, m) for kc in kcs
                              for s, m in ((stationary(kc)[0], moving(kc)[0]), (stationary(kc)[0], moving(kc)[1]),
                                           (stationary(kc)[1], moving(kc)[0]))]
                    for i, (s, m) in enumerate(passes):
                        ins = pe.matmul(out, s, m, start=(i == 0), stop=(i == len(passes) - 1))
                    return ins

                def project_k(b):
                    wait(pe, v_set, b)
                    pe.wait_ge(ctxl_set, b + 1)
                    for m in range(KC):
                        ins = threefold(proj[:, m, :],
                                        lambda kc: (w_h[WK][:, kc, m * P:(m + 1) * P], w_l[WK][:, kc, m * P:(m + 1) * P]),
                                        lambda kc: (ctx_h[:, kc, :], ctx_l[:, kc, :]), range(KC))
                    ins.then_inc(k_done, 1)

                def project_q(b):
                    at = bass.ds(b * S, S)
                    pe.wait_ge(k_set, b + 1)
                    for m in range(KC):
                        ins = threefold(proj[:, m, :],
                                        lambda kc: (w_h[WQ][:, kc, m * P:(m + 1) * P], w_l[WQ][:, kc, m * P:(m + 1) * P]),
                                        lambda kc: (g.xT_h[:, kc, at], g.xT_l[:, kc, at]), range(KC))
                    ins.then_inc(q_done, 1)

                def project_v(b):
                    pe.wait_ge(ql_set, b + 1)
                    for c in range(2):
                        ins = threefold(proj[:, c, :],
                                        lambda kc: (ctx_h[:, kc, c * P:(c + 1) * P], ctx_l[:, kc, c * P:(c + 1) * P]),
                                        lambda kc: (w_h[WV][:, kc, :], w_l[WV][:, kc, :]), range(KC))
                    ins.then_inc(v_done, 1)

                def score(b, par, u):
                    n = UNITS * b + u
                    m, pair, half = u // 8, (u % 8) // 2, u % 2
                    if u == 0:
                        pe.wait_ge(ql_set, b + 1)
                    if u % 8 == 0:
                        pe.wait_ge(kz_set, 2 * b + m + 1)
                    wait(pe, exp_set, n - 1)
                    at, heads = slice(half * P, (half + 1) * P), slice(2 * pair, 2 * pair + 2)
                    threefold(scores[u % 2][:, :, :], lambda kc: (q_h[par][:, m, at], q_l[par][:, m, at]),
                              lambda kc: (kz_h[:, m, heads, :], kz_l[:, m, heads, :]), range(1)).then_inc(scored, 1)

                def turn(b, u):
                    n = UNITS * b + u
                    pe.wait_ge(exp_set, n + 1)
                    if u % 2:
                        wait(pe, odd_set, UNITS // 2 * b + u // 2)
                    else:
                        wait(pe, even_set, UNITS // 2 * b + u // 2)
                    for h in range(2):
                        for c in range(2):
                            ins = pe.transpose(turned_p[u % 2][:, h, c, :], probs[u % 4][:, h, c * P:(c + 1) * P],
                                               g.ident[:, :])
                    ins.then_inc(turned, 1)

                def weigh(b, par, grp):
                    n = GROUPS * b + grp
                    if grp == 0:
                        pe.wait_ge(v_set, b + 1)
                    pe.wait_ge(even_set, 2 * n + 2)
                    pe.wait_ge(odd_set, 2 * n + 2)
                    pe.wait_ge(inv_set, n + 1)
                    wait(pe, o_set, n)
                    for half in range(2):
                        pe.transpose(out_p[:, 1, half * P:(half + 1) * P],
                                     inverse[grp % 2][:, half, :, :], g.ident[:, :])
                    for c in range(2):
                        for j in range(4):
                            ins = pe.matmul(out_p[PAD * j:PAD * (j + 1), 0, :], v[par][:, c, 4 * grp + j, :],
                                            probsT[grp % 2][:, j, c, :], start=(c == 0), stop=(c == 1))
                    ins.then_inc(o_done, 1)

                def project_out(b):
                    pe.wait_ge(ol_set, GROUPS * b + GROUPS)
                    wait(pe, added, b)
                    for t in range(2):
                        at = slice(t * P, (t + 1) * P)
                        ins = threefold(y_p[:, t, :], lambda r: (o_h[:, r, at], o_l[:, r, at]),
                                        lambda r: (out_h[:, r, :], out_l[:, r, :]), range(GROUPS))
                    ins.then_inc(y_done, 1)

                def step(b, par, first, last):
                    for u in range(UNITS):
                        score(b, par, u)
                        if u >= 2:
                            turn(b, u - 2)
                        elif not first:
                            turn(b - 1, UNITS + u - 2)
                        if u == 3 and not first:
                            weigh(b - 1, 1 - par, 3)
                        if u in (7, 11, 15):
                            weigh(b, par, (u - 7) // 4)
                        if u == 5 and last < 2:
                            project_k(b + 1)
                        if u == 8 and not first:
                            project_out(b - 1)
                        if u == 9 and last < 2:
                            project_q(b + 1)
                        if u == 12 and last < 2:
                            project_v(b + 1)

                pe.wait_ge(wl_set, 4)
                project_k(0)
                project_q(0)
                project_v(0)
                batches(pe, NB, step)
                turn(NB - 1, UNITS - 2)
                turn(NB - 1, UNITS - 1)
                weigh(NB - 1, 1, 3)
                project_out(NB - 1)

            @block.vector
            def _(dve):
                def part_q(b, par):
                    dve.wait_ge(qh_set, b + 1)
                    for m in range(KC):
                        ins = dve.scalar_tensor_tensor(q_l[par][:, m, :], proj[:, m, :], bias_q[:, m:m + 1],
                                                       q_h[par][:, m, :], ALU.add, ALU.subtract)
                    ins.then_inc(ql_set, 1)

                def set_v(b, par):
                    dve.wait_ge(v_done, b + 1)
                    dve.tensor_tensor(v[par][:, :, :, 0:DH], proj[:, :, :].rearrange("p c (h d) -> p c h d", h=HEADS),
                                      bias_v[:, :].rearrange("p (h d) -> p h d", h=HEADS).unsqueeze(1)
                                      .to_broadcast([P, 2, HEADS, DH]), ALU.add).then_inc(v_set, 1)

                def maximum(b, u):
                    dve.wait_ge(scored, UNITS * b + u + 1)
                    dve.tensor_reduce(negmax[:, u % 4, :], scores[u % 2][:, :, :], AX.X, ALU.max,
                                      negate=True).then_inc(max_set, 1)

                def set_odd(b, u):
                    dve.wait_ge(turned, UNITS * b + u + 1)
                    wait(dve, o_done, GROUPS * b + u // 4 - 1)
                    pair = (u // 2) % 2
                    dve.tensor_copy(probsT[(u // 4) % 2][:, 2 * pair:2 * pair + 2, :, P:2 * P],
                                    turned_p[1][:, :, :, :]).then_inc(odd_set, 1)

                def invert(b, grp):
                    n = GROUPS * b + grp
                    dve.wait_ge(exp_set, 4 * n + 4)
                    wait(dve, o_done, n - 1)
                    dve.reciprocal(one_inverse[:, :, :], total[:, grp % 2, :, :]).then_inc(recip_set, 1)
                    dve.wait_ge(recip_set, n + 1)
                    dve.tensor_copy(inverse[grp % 2][:, :, :, :],
                                    one_inverse[:, :, :].unsqueeze(3).to_broadcast([P, 2, 4, PAD])).then_inc(inv_set, 1)

                def set_out(b, grp):
                    n = GROUPS * b + grp
                    dve.wait_ge(o_done, n + 1)
                    dve.tensor_copy(scale_T[:, grp % 2, :], out_p[:, 1, :]).then_inc(scaleT_set, 1)
                    dve.wait_ge(scaleT_set, n + 1)
                    wait(dve, ol_set, n - 1)
                    dve.tensor_tensor(o_full[grp % 2][:, :], out_p[:, 0, :], scale_T[:, grp % 2, :],
                                      ALU.mult).then_inc(o_set, 1)

                def add(b):
                    dve.wait_ge(y_done, b + 1)
                    dve.wait_ge(biased, b + 1)
                    rows = g.x[:, bass.ds(2 * b, 2), :]
                    dve.tensor_tensor(rows, rows, y_p[:, :, :], ALU.add).then_inc(added, 1)

                def step(b, par, first, last):
                    for u in range(UNITS):
                        maximum(b, u)
                        if u % 4 == 1:
                            if u > 1:
                                invert(b, u // 4 - 1)
                            elif not first:
                                invert(b - 1, 3)
                        if u % 2 == 1 and u >= 3:
                            set_odd(b, u - 2)
                        if u == 1 and not first:
                            set_odd(b - 1, UNITS - 1)
                        if u == 0 and not first:
                            set_out(b - 1, 2)
                        if u == 4 and not first:
                            set_out(b - 1, 3)
                        if u in (8, 12):
                            set_out(b, (u - 8) // 4)
                        if u == 9 and not first:
                            add(b - 1)
                        if u == 10 and last < 2:
                            part_q(b + 1, 1 - par)
                        if u == 13 and last < 2:
                            set_v(b + 1, 1 - par)

                dve.wait_ge(loaded, 16 * LOADS)
                dve.tensor_scalar(raw[WQ][:, :, :], raw[WQ][:, :, :], SCALE, None, ALU.mult)
                dve.tensor_scalar(bias_q[:, :], bias_q[:, :], SCALE, None, ALU.mult).then_inc(raw_set, 1)
                dve.wait_ge(zeroed, 3)
                part_q(0, 0)
                set_v(0, 0)
                batches(dve, NB, step)
                invert(NB - 1, 3)
                set_odd(NB - 1, UNITS - 1)
                set_out(NB - 1, 2)
                set_out(NB - 1, 3)
                add(NB - 1)


def norm_and_gate(nc, g, io):
    NB, S, KC, E = g.NB, g.S, g.KC, g.E2
    with ExitStack() as ctx:
        def sem(name):
            return ctx.enter_context(nc.semaphore(name))

        gate = ctx.enter_context(nc.sbuf_tensor("k_gate", [P, KC, E], F32))
        logit_ps = [ctx.enter_context(nc.psum_tensor(f"k_logit{i}", [P, 2, E], F32)) for i in range(2)]
        gate_in, logit_done, logit_set, kept = sem("k_gate_in"), sem("k_logit_done"), sem("k_logit_set"), sem("k_kept")
        norm = Norm(ctx, nc, g, "k")

        with nc.Block() as block:
            @block.sync
            def _(sp):
                sp.dma_start(gate[:, :, :], io["L1_ffn_gate_w_T"].rearrange("(c p) e -> p c e", p=P)).then_inc(gate_in, 16)

            @block.scalar
            def _(act):
                def take_logits(b, par):
                    act.wait_ge(logit_done, b + 1)
                    act.activation(g.logits2[:, :, bass.ds(b, 1), :].rearrange("p t b e -> p t (b e)"),
                                   logit_ps[par][:, :, :], ACT.Copy).then_inc(logit_set, 1)

                def step(b, par, first, last):
                    norm.root(act, b, par)
                    if not first:
                        take_logits(b - 1, 1 - par)
                    act.wait_ge(norm.normed, b + 1)
                    act.activation(g.xn[:, bass.ds(2 * b, 2), :], norm.xn[par][:, :, :], ACT.Copy).then_inc(kept, 1)

                batches(act, NB, step)
                take_logits(NB - 1, 1)

            @block.tensor
            def _(pe):
                def route(b, par):
                    pe.wait_ge(norm.filled, b + 1)
                    wait(pe, logit_set, b - 1)
                    for t in range(2):
                        for kc in range(KC):
                            ins = pe.matmul(logit_ps[par][:, t, :], norm.full[par][:, kc, t * P:(t + 1) * P],
                                            gate[:, kc, :], start=(kc == 0), stop=(kc == KC - 1))
                    ins.then_inc(logit_done, 1)

                def step(b, par, first, last):
                    if not first:
                        route(b - 1, 1 - par)
                    norm.turn(pe, b, par)

                pe.wait_ge(gate_in, 16)
                batches(pe, NB, step)
                route(NB - 1, 1)

            @block.vector
            def _(dve):
                link = Chain(dve, norm.chain)

                def fill(b, par):
                    wait(dve, logit_done, b - 1)
                    norm.fill(dve, b, par)

                def step(b, par, first, last):
                    link.restart()
                    norm.moments(dve, link, b, par)
                    if not first:
                        fill(b - 1, 1 - par)
                    wait(dve, kept, b - 1)
                    norm.apply(dve, link, b, par)

                batches(dve, NB, step)
                fill(NB - 1, 1)


def exact_exp(dve, link, x, power, power_i, rest, series):
    LN2_HIGH = 0.693359375
    LN2_LOW = math.log(2) - LN2_HIGH
    ROUND = 1.5 * 2.0 ** 23
    TERMS = 8
    link(dve.tensor_scalar(x, x, -87.0, None, ALU.max))
    link(dve.tensor_scalar(power, x, 1 / math.log(2), ROUND, ALU.mult, ALU.add))
    link(dve.tensor_scalar(power, power, ROUND, None, ALU.subtract))
    link(dve.scalar_tensor_tensor(rest, power, -LN2_HIGH, x, ALU.mult, ALU.add))
    link(dve.scalar_tensor_tensor(rest, power, -LN2_LOW, rest, ALU.mult, ALU.add))
    link(dve.tensor_scalar(series, rest, 1 / math.factorial(TERMS), None, ALU.mult))
    for n in range(TERMS - 1, 0, -1):
        link(dve.scalar_tensor_tensor(series, series, 1 / math.factorial(n), rest, ALU.add, ALU.mult))
    link(dve.tensor_scalar(power, power, 127.0, None, ALU.add))
    link(dve.tensor_copy(power_i, power))
    link(dve.tensor_scalar(power_i, power_i, 23, None, ALU.logical_shift_left))
    link(dve.scalar_tensor_tensor(x, series, 1.0, power_i.bitcast(F32), ALU.add, ALU.mult))


def choose_tokens(nc, g, io):
    NB, S, E, SLOTS = g.NB, g.S, g.E2, g.SLOTS
    ROWS = NB * E
    with ExitStack() as ctx:
        def sb(name, shape, dt=F32):
            return ctx.enter_context(nc.sbuf_tensor(name, shape, dt))

        def sem(name):
            return ctx.enter_context(nc.semaphore(name))

        peak, total = sb("t_peak", [P, 2 * NB]), sb("t_total", [P, 2 * NB])
        inverse = sb("t_inverse", [P, 2 * NB])
        work = [sb(f"t_work{i}", [ROWS, S]) for i in range(2)]
        top = sb("t_top", [ROWS, 8])
        chosen, rank, none = sb("t_chosen", [ROWS, S]), sb("t_rank", [ROWS, S]), sb("t_none", [ROWS, S])
        rows_ps = ctx.enter_context(nc.psum_tensor("t_rows_ps", [ROWS, 2, P], F32))
        place_ps = ctx.enter_context(nc.psum_tensor("t_place_ps", [P, 2, ROWS], F32))
        power, rest, series = (sb(f"t_{name}", [P, 2 * NB, E]) for name in ("power", "rest", "series"))
        power_i = sb("t_power_i", [P, 2 * NB, E], I32)
        ready, turned = sem("t_ready"), sem("t_turned")
        ranked, returned, chain, none_set = sem("t_ranked"), sem("t_returned"), sem("t_chain"), sem("t_none_set")
        by_token = g.logits2[:, :, :, :].rearrange("p t b e -> p (t b) e")
        affinity = g.affinity[:, :, :].rearrange("p t (b e) -> p (t b) e", e=E)

        def along(ap):
            return ap.unsqueeze(2).to_broadcast([P, 2 * NB, E])

        with nc.Block() as block:
            @block.gpsimd
            def _(pool):
                pool.memset(none[:, :], 0.0).then_inc(none_set, 1)
                pool.iota(g.slot[:, :], [[1, SLOTS]], base=1, channel_multiplier=0,
                          allow_small_or_imprecise_dtypes=True).then_inc(none_set, 1)

            @block.tensor
            def _(pe):
                pe.wait_ge(ready, 1)
                for t in range(2):
                    ins = pe.transpose(rows_ps[:, t, :], g.affinity[:, t, :], g.ident[:, :])
                ins.then_inc(turned, 1)
                pe.wait_ge(ranked, 1)
                for t in range(2):
                    ins = pe.transpose(place_ps[:, t, :], rank[:, t * P:(t + 1) * P], g.ident[0:ROWS, 0:ROWS])
                ins.then_inc(returned, 1)

            @block.vector
            def _(dve):
                link = Chain(dve, chain)
                link(dve.tensor_reduce(peak[:, :], by_token, AX.X, ALU.max))
                link(dve.tensor_tensor(by_token, by_token, along(peak[:, :]), ALU.subtract))
                exact_exp(dve, link, by_token, power[:, :, :], power_i[:, :, :], rest[:, :, :], series[:, :, :])
                link(dve.tensor_reduce(total[:, :], by_token, AX.X, ALU.add))
                link(dve.reciprocal(inverse[:, :], total[:, :]))
                dve.tensor_tensor(affinity, by_token, along(inverse[:, :]), ALU.mult).then_inc(ready, 1)
                dve.wait_ge(turned, 1)
                link(dve.tensor_copy(work[0][:, :], rows_ps[:, :, :].rearrange("r t p -> r (t p)")))
                for i in range(SLOTS // 8):
                    link(dve.max(top[:, :], work[i % 2][:, :]))
                    link(dve.match_replace(work[1 - i % 2][:, :], top[:, :], work[i % 2][:, :], -1.0))
                link(dve.tensor_scalar(chosen[:, :], work[SLOTS // 8 % 2][:, :], 0.0, None, ALU.is_lt))
                dve.wait_ge(none_set, 2)
                link(dve.tensor_tensor_scan(rank[:, :], chosen[:, :], none[:, :], 0.0, ALU.add, ALU.add))
                dve.tensor_tensor(rank[:, :], rank[:, :], chosen[:, :], ALU.mult).then_inc(ranked, 1)
                dve.wait_ge(returned, 1)
                dve.tensor_copy(g.place[:, :, :], place_ps[:, :, :])


def chosen_slots(dve, g, out, b):
    E, SLOTS = g.E2, g.SLOTS
    for t in range(2):
        ins = dve.tensor_tensor(out[:, t, :, :],
                                g.place[:, t, bass.ds(b * E, E)].unsqueeze(2).to_broadcast([P, E, SLOTS]),
                                g.slot[:, :].unsqueeze(1).to_broadcast([P, E, SLOTS]), ALU.is_equal)
    return ins


def collect_tokens(nc, g, io):
    NB, D, KC, E, SLOTS = g.NB, g.D, g.KC, g.E2, g.SLOTS
    with ExitStack() as ctx:
        def sem(name):
            return ctx.enter_context(nc.semaphore(name))

        x_h = [ctx.enter_context(nc.sbuf_tensor(f"l_x_h{i}", [P, 2, D], F32R)) for i in range(2)]
        x_l = [ctx.enter_context(nc.sbuf_tensor(f"l_x_l{i}", [P, 2, D], F32R)) for i in range(2)]
        slots = [ctx.enter_context(nc.sbuf_tensor(f"l_slots{i}", [P, 2, E, SLOTS], F32R)) for i in range(2)]
        ps = [[ctx.enter_context(nc.psum_tensor(f"l_ps{i}{kc}", [P, E, SLOTS], F32)) for kc in range(KC)] for i in range(2)]
        xh_set, xl_set, slots_set, collected = sem("l_xh_set"), sem("l_xl_set"), sem("l_slots_set"), sem("l_collected")
        high, low = sem("l_high"), sem("l_low")

        def place_of(part, kc, b):
            return part[:, kc, :, bass.ds(b, 1), :].rearrange("p e b s -> p e (b s)")

        with nc.Block() as block:
            @block.gpsimd
            def _(pool):
                def step(b, par, first, last):
                    pool.wait_ge(xh_set, b + 1)
                    pool.tensor_tensor(x_l[par][:, :, :], g.xn[:, bass.ds(2 * b, 2), :], x_h[par][:, :, :],
                                       ALU.subtract).then_inc(xl_set, 1)

                batches(pool, NB, step)

            @block.scalar
            def _(act):
                def high_x(b, par):
                    wait(act, collected, b - 1)
                    act.activation(x_h[par][:, :, :], g.xn[:, bass.ds(2 * b, 2), :], ACT.Copy).then_inc(xh_set, 1)

                def step(b, par, first, last):
                    if last < 2:
                        high_x(b + 1, 1 - par)
                    act.wait_ge(collected, b + 1)
                    for kc in range(KC):
                        ins = act.activation(place_of(g.xin_h, kc, b), ps[par][kc][:, :, :], ACT.Copy)
                    ins.then_inc(high, 1)

                high_x(0, 0)
                batches(act, NB, step)

            @block.tensor
            def _(pe):
                def step(b, par, first, last):
                    pe.wait_ge(slots_set, b + 1)
                    pe.wait_ge(xl_set, b + 1)
                    wait(pe, low, b - 1)
                    for kc in range(KC):
                        passes = [(x, t) for t in range(2) for x in (x_h[par], x_l[par])]
                        for i, (x, t) in enumerate(passes):
                            ins = pe.matmul(ps[par][kc][:, :, :], x[:, t, kc * P:(kc + 1) * P], slots[par][:, t, :, :],
                                            start=(i == 0), stop=(i == len(passes) - 1))
                    ins.then_inc(collected, 1)

                batches(pe, NB, step)

            @block.vector
            def _(dve):
                def choose(b, par):
                    wait(dve, collected, b - 1)
                    chosen_slots(dve, g, slots[par], b).then_inc(slots_set, 1)

                def step(b, par, first, last):
                    if last < 2:
                        choose(b + 1, 1 - par)
                    dve.wait_ge(high, b + 1)
                    for kc in range(KC):
                        ins = dve.tensor_tensor(place_of(g.xin_l, kc, b), ps[par][kc][:, :, :],
                                                place_of(g.xin_h, kc, b), ALU.subtract)
                    ins.then_inc(low, 1)

                choose(0, 0)
                batches(dve, NB, step)


def run_choosing_experts(nc, g, io):
    NB, D, KC, E, SLOTS = g.NB, g.D, g.KC, g.E2, g.SLOTS
    CHUNKS = g.I // P
    N = NB * SLOTS
    TILES = N // P
    W = 2 * KC * P + D
    RAWS = 4
    with ExitStack() as ctx:
        def sb(name, shape, dt=F32):
            return ctx.enter_context(nc.sbuf_tensor(name, shape, dt))

        def sem(name):
            return ctx.enter_context(nc.semaphore(name))

        raw = [sb(f"n_raw{i}", [P, W]) for i in range(RAWS)]
        w_h, w_l = [sb(f"n_w_h{i}", [P, W], F32R) for i in range(RAWS)], [sb(f"n_w_l{i}", [P, W], F32R) for i in range(RAWS)]
        silu, hidden = [sb(f"n_silu{i}", [P, N]) for i in range(2)], [sb(f"n_hidden{i}", [P, N]) for i in range(2)]
        hid_h = [sb(f"n_hid_h{i}", [P, N], F32R) for i in range(2)]
        hid_l = [sb(f"n_hid_l{i}", [P, N], F32R) for i in range(2)]
        result = sb("n_result", [P, TILES, D])
        gate_ps = [ctx.enter_context(nc.psum_tensor(f"n_gate{i}", [P, N], F32)) for i in range(2)]
        up_ps = [ctx.enter_context(nc.psum_tensor(f"n_up{i}", [P, N], F32)) for i in range(2)]
        sum_ps = [ctx.enter_context(nc.psum_tensor(f"n_sum{i}", [P, D], F32)) for i in range(TILES)]
        raw_in = [sem(f"n_raw_in{i}") for i in range(RAWS)]
        wh_set, wl_set, gated, upped = sem("n_wh_set"), sem("n_wl_set"), sem("n_gated"), sem("n_upped")
        silu_set, hidden_set, high, low = sem("n_silu_set"), sem("n_hidden_set"), sem("n_high"), sem("n_low")
        downed, taken, stored = sem("n_downed"), sem("n_taken"), sem("n_stored")
        store = g.chosen_out.rearrange("(q r) (e s) d -> r s e q d", r=2, e=E)

        def chunk_before(e, m):
            return (e - 1, CHUNKS - 1) if m == 0 else (e, m - 1)

        with nc.Block() as block:
            @block.sync
            def _(sp):
                def step(e, first, last):
                    for m in range(CHUNKS):
                        if not first or m >= RAWS:
                            sp.wait_ge(wl_set, CHUNKS * e + m - RAWS + 1)
                        sp.dma_start(raw[m % RAWS][:, :], io["L1_ffn_w"][bass.ds(e, 1), m, :, :]
                                     .rearrange("e p w -> p (e w)")).then_inc(raw_in[m % RAWS], 16)

                unrolled(sp, E, step)

            @block.scalar
            def _(act):
                def high_w(e, m):
                    act.wait_ge(raw_in[m % RAWS], 16 * ((CHUNKS // RAWS) * e + m // RAWS + 1))
                    wait(act, downed, CHUNKS * e + m - RAWS + 1)
                    act.activation(w_h[m % RAWS][:, :], raw[m % RAWS][:, :], ACT.Copy).then_inc(wh_set, 1)

                def step(e, first, last):
                    for m in range(CHUNKS):
                        c = CHUNKS * e + m
                        act.wait_ge(gated, c + 1)
                        if not first or m >= 2:
                            act.wait_ge(hidden_set, c - 1)
                        act.activation(silu[m % 2][:, :], gate_ps[m % 2][:, :], ACT.Silu).then_inc(silu_set, 1)
                        if m + 2 < CHUNKS:
                            high_w(e, m + 2)
                        elif not last:
                            high_w(e + 1, m + 2 - CHUNKS)
                        act.wait_ge(hidden_set, c + 1)
                        if not first or m >= 2:
                            act.wait_ge(downed, c - 1)
                        act.activation(hid_h[m % 2][:, :], hidden[m % 2][:, :], ACT.Copy).then_inc(high, 1)

                high_w(0, 0)
                high_w(0, 1)
                unrolled(act, E, step)

            @block.gpsimd
            def _(pool):
                def step(e, first, last):
                    for m in range(CHUNKS):
                        c = CHUNKS * e + m
                        pool.wait_ge(wh_set, c + 1)
                        pool.tensor_tensor(w_l[m % RAWS][:, :], raw[m % RAWS][:, :], w_h[m % RAWS][:, :],
                                           ALU.subtract).then_inc(wl_set, 1)
                        if m == 1 and not first:
                            keep(e - 1)

                def keep(e):
                    pool.wait_ge(taken, e + 1)
                    for r in range(2):
                        pool.dma_start(store[r, :, bass.ds(e, 1), :, :].rearrange("s e q d -> s (e q) d"),
                                       result[r * SLOTS:(r + 1) * SLOTS, :, :]).then_inc(stored, 16)

                unrolled(pool, E, step)
                keep(E - 1)
                pool.wait_ge(stored, 32 * E)

            @block.tensor
            def _(pe):
                def product(out, e, m, at, done):
                    passes = [(w, x, kc) for kc in range(KC)
                              for w, x in ((w_h, g.xin_h), (w_h, g.xin_l), (w_l, g.xin_h))]
                    for i, (w, x, kc) in enumerate(passes):
                        ins = pe.matmul(out[:, :], w[m % RAWS][:, at + kc * P:at + (kc + 1) * P],
                                        x[:, kc, bass.ds(e, 1), :, :].rearrange("p e b s -> p (e b s)"),
                                        start=(i == 0), stop=(i == len(passes) - 1))
                    ins.then_inc(done, 1)

                def down(e, m):
                    pe.wait_ge(low, CHUNKS * e + m + 1)
                    if m == 0:
                        wait(pe, taken, e)
                    at = slice(2 * KC * P, W)
                    for t in range(TILES):
                        of = slice(t * P, (t + 1) * P)
                        passes = ((hid_h, w_h), (hid_h, w_l), (hid_l, w_h))
                        for i, (h, w) in enumerate(passes):
                            ins = pe.matmul(sum_ps[t][:, :], h[m % 2][:, of], w[m % RAWS][:, at],
                                            start=(m == 0 and i == 0), stop=(m == CHUNKS - 1 and i == len(passes) - 1))
                    ins.then_inc(downed, 1)

                def step(e, first, last):
                    for m in range(CHUNKS):
                        c = CHUNKS * e + m
                        pe.wait_ge(wl_set, c + 1)
                        if not first or m >= 2:
                            pe.wait_ge(hidden_set, c - 1)
                        product(gate_ps[m % 2], e, m, 0, gated)
                        product(up_ps[m % 2], e, m, KC * P, upped)
                        if not first or m:
                            down(*chunk_before(e, m))

                unrolled(pe, E, step)
                down(E - 1, CHUNKS - 1)

            @block.vector
            def _(dve):
                def take(e):
                    dve.wait_ge(downed, CHUNKS * (e + 1))
                    wait(dve, stored, 32 * e)
                    for t in range(TILES):
                        ins = dve.tensor_copy(result[:, t, :], sum_ps[t][:, :])
                    ins.then_inc(taken, 1)

                def step(e, first, last):
                    for m in range(CHUNKS):
                        c = CHUNKS * e + m
                        dve.wait_ge(silu_set, c + 1)
                        dve.wait_ge(upped, c + 1)
                        if not first or m >= 2:
                            dve.wait_ge(low, c - 1)
                        dve.tensor_tensor(hidden[m % 2][:, :], up_ps[m % 2][:, :], silu[m % 2][:, :],
                                          ALU.mult).then_inc(hidden_set, 1)
                        dve.wait_ge(high, c + 1)
                        dve.tensor_tensor(hid_l[m % 2][:, :], hidden[m % 2][:, :], hid_h[m % 2][:, :],
                                          ALU.subtract).then_inc(low, 1)
                        if m == 0 and not first:
                            take(e - 1)

                unrolled(dve, E, step)
                take(E - 1)


def return_tokens(nc, g, io):
    NB, D, E, SLOTS = g.NB, g.D, g.E2, g.SLOTS
    PAIRS = E * SLOTS // P
    with ExitStack() as ctx:
        def sb(name, shape, dt=F32):
            return [ctx.enter_context(nc.sbuf_tensor(f"{name}{i}", shape, dt)) for i in range(2)]

        def sem(name):
            return ctx.enter_context(nc.semaphore(name))

        y, y_h, y_l = sb("u_y", [P, PAIRS, D]), sb("u_y_h", [P, PAIRS, D], F32R), sb("u_y_l", [P, PAIRS, D], F32R)
        slots, gates = sb("u_slots", [P, 2, E, SLOTS]), sb("u_gates", [P, 2, E, SLOTS])
        gate_h, gate_l = sb("u_gate_h", [P, 2, PAIRS, P], F32R), sb("u_gate_l", [P, 2, PAIRS, P], F32R)
        turn_ps = [[ctx.enter_context(nc.psum_tensor(f"u_turn{i}{t}", [P, PAIRS, P], F32)) for t in range(2)] for i in range(2)]
        sum_ps = [ctx.enter_context(nc.psum_tensor(f"u_sum{i}", [P, 2, D], F32)) for i in range(2)]
        y_in = [sem(f"u_y_in{i}") for i in range(2)]
        yh_set, yl_set, chosen, weighed, turned = sem("u_yh_set"), sem("u_yl_set"), sem("u_chosen"), sem("u_weighed"), sem("u_turned")
        high, low, summed, added, stored = sem("u_high"), sem("u_low"), sem("u_summed"), sem("u_added"), sem("u_stored")
        results = g.chosen_out.rearrange("b (c p) d -> p b c d", p=P)
        out = io["out"].rearrange("b (t p) d -> p b t d", p=P)

        def halves(eng, step):
            def body(i, first, last):
                step(2 * i, 0, first, 1 if last else 0, i)
                step(2 * i + 1, 1, False, 2 if last else 0, i)

            unrolled(eng, NB // 2, body)

        with nc.Block() as block:
            @block.sync
            def _(sp):
                def step(b, par, first, last):
                    wait(sp, yl_set, b - 1)
                    sp.dma_start(y[par][:, :, :], results[:, bass.ds(b, 1), :, :]).then_inc(y_in[par], 16)
                    if not first:
                        store(b - 1)

                def store(b):
                    sp.wait_ge(added, b + 1)
                    sp.dma_start(out[:, bass.ds(b, 1), :, :], g.x[:, bass.ds(2 * b, 2), :]).then_inc(stored, 16)

                batches(sp, NB, step)
                store(NB - 1)
                sp.wait_ge(stored, 16 * NB)

            @block.gpsimd
            def _(pool):
                def step(b, par, first, last):
                    pool.wait_ge(yh_set, b + 1)
                    pool.tensor_tensor(y_l[par][:, :, :], y[par][:, :, :], y_h[par][:, :, :], ALU.subtract).then_inc(yl_set, 1)

                batches(pool, NB, step)

            @block.scalar
            def _(act):
                def high_y(b, par, i):
                    act.wait_ge(y_in[par], 16 * i + 16)
                    wait(act, summed, b - 1)
                    act.activation(y_h[par][:, :, :], y[par][:, :, :], ACT.Copy).then_inc(yh_set, 1)

                def step(b, par, first, last, i):
                    high_y(b, par, i)
                    act.wait_ge(turned, b + 1)
                    for t in range(2):
                        ins = act.activation(gate_h[par][:, t, :, :], turn_ps[par][t][:, :, :], ACT.Copy)
                    ins.then_inc(high, 1)

                halves(act, step)

            @block.tensor
            def _(pe):
                def turn(b, par):
                    pe.wait_ge(weighed, b + 1)
                    wait(pe, low, b - 1)
                    for t in range(2):
                        for c in range(PAIRS):
                            ins = pe.transpose(turn_ps[par][t][:, c, :], gates[par][:, t, 2 * c:2 * c + 2, :], g.ident[:, :])
                    ins.then_inc(turned, 1)

                def step(b, par, first, last):
                    if last < 2:
                        turn(b + 1, 1 - par)
                    pe.wait_ge(low, b + 1)
                    pe.wait_ge(yl_set, b + 1)
                    wait(pe, added, b - 1)
                    for t in range(2):
                        passes = [(s, m, c) for c in range(PAIRS)
                                  for s, m in ((gate_h, y_h), (gate_h, y_l), (gate_l, y_h))]
                        for i, (s, m, c) in enumerate(passes):
                            ins = pe.matmul(sum_ps[par][:, t, :], s[par][:, t, c, :], m[par][:, c, :],
                                            start=(i == 0), stop=(i == len(passes) - 1))
                    ins.then_inc(summed, 1)

                turn(0, 0)
                batches(pe, NB, step)

            @block.vector
            def _(dve):
                def weigh(b, par):
                    chosen_slots(dve, g, slots[par], b).then_inc(chosen, 1)
                    dve.wait_ge(chosen, b + 1)
                    wait(dve, turned, b - 1)
                    for t in range(2):
                        ins = dve.tensor_tensor(gates[par][:, t, :, :], slots[par][:, t, :, :],
                                                g.affinity[:, t, bass.ds(b * E, E)].unsqueeze(2).to_broadcast([P, E, SLOTS]),
                                                ALU.mult)
                    ins.then_inc(weighed, 1)

                def take_low(b, par):
                    dve.wait_ge(high, b + 1)
                    for t in range(2):
                        ins = dve.tensor_tensor(gate_l[par][:, t, :, :], turn_ps[par][t][:, :, :],
                                                gate_h[par][:, t, :, :], ALU.subtract)
                    ins.then_inc(low, 1)

                def step(b, par, first, last):
                    if last < 2:
                        weigh(b + 1, 1 - par)
                    take_low(b, par)
                    dve.wait_ge(summed, b + 1)
                    rows = g.x[:, bass.ds(2 * b, 2), :]
                    dve.tensor_tensor(rows, rows, sum_ps[par][:, :, :], ALU.add).then_inc(added, 1)

                weigh(0, 0)
                batches(dve, NB, step)


def clear_semaphores(nc):
    numbers = sorted(nc.free_semaphores)
    runs = [[numbers[0], numbers[0]]]
    for number in numbers[1:]:
        if number == runs[-1][1] + 1:
            runs[-1][1] = number
        else:
            runs.append([number, number])
    with nc.Block() as block:
        @block.sync
        def _(sp):
            for first, last in runs:
                sp.sem_clear(range(first, last + 1))


def program(nc, io):
    g = Shared()
    g.NB, g.S, g.D = io["x"].shape
    g.KC, g.NT = g.D // P, g.NB * g.S // P
    g.E, _, two_f = io["L0_ffn_gate_up_proj"].shape
    g.F = two_f // 2
    g.BLOCKS = g.NT + g.E - 1
    g.E2, chunks = io["L1_ffn_w"].shape[:2]
    g.I, g.SLOTS = chunks * P, g.S // g.E2 * 2
    g.rows_in = nc.dram_tensor("rows_in", [g.BLOCKS * P, g.D], F32, kind="Internal").ap()
    g.rows_out = nc.dram_tensor("rows_out", [g.BLOCKS * P, g.D], F32, kind="Internal").ap()
    g.chosen_out = nc.dram_tensor("chosen_out", [g.NB, g.E2 * g.SLOTS, g.D], F32, kind="Internal").ap()
    with ExitStack() as whole:
        def keep(ctx, name, shape, dt=F32):
            return ctx.enter_context(nc.sbuf_tensor(name, shape, dt))

        g.x = keep(whole, "x", [P, g.NT, g.D])
        g.ident, g.eps = keep(whole, "ident", [P, P]), keep(whole, "eps", [P, 1])
        g.row_of = keep(whole, "row_of", [P, g.NT], U32)
        g.block_expert = keep(whole, "block_expert", [P, g.BLOCKS], I32)
        with ExitStack() as ctx:
            g.big = keep(ctx, "big", [P, 64 * g.S])
            with ExitStack() as inner:
                g.kvT_h = keep(inner, "kvT_h", [P, g.KC, 2 * g.NB * g.S], F32R)
                g.kvT_l = keep(inner, "kvT_l", [P, g.KC, 2 * g.NB * g.S], F32R)
                normalise_inputs(nc, g, io)
                clear_semaphores(nc)
                attend_latents(nc, g, io)
                clear_semaphores(nc)
            g.xn = keep(ctx, "xn", [P, g.NT, g.D])
            g.xT_h = keep(ctx, "xT_h", [P, g.KC, g.NB * g.S], F32R)
            g.xT_l = keep(ctx, "xT_l", [P, g.KC, g.NB * g.S], F32R)
            g.logits = keep(ctx, "logits", [P, g.NT, g.E])
            add_attention(nc, g, io)
            clear_semaphores(nc)
            route_tokens(nc, g, io)
            clear_semaphores(nc)
            shared_expert(nc, g, io)
            clear_semaphores(nc)
            run_experts(nc, g, io)
            clear_semaphores(nc)
        with ExitStack() as ctx:
            g.xT_h = keep(ctx, "xT2_h", [P, g.KC, g.NB * g.S], F32R)
            g.xT_l = keep(ctx, "xT2_l", [P, g.KC, g.NB * g.S], F32R)
            with ExitStack() as inner:
                g.xn = keep(inner, "xn2", [P, g.NT, g.D])
                gather_rows(nc, g, io)
                clear_semaphores(nc)
            attend_context(nc, g, io)
            clear_semaphores(nc)
        g.logits2 = keep(whole, "logits2", [P, 2, g.NB, g.E2])
        g.affinity, g.place = keep(whole, "affinity", [P, 2, g.NB * g.E2]), keep(whole, "place", [P, 2, g.NB * g.E2])
        g.slot = keep(whole, "slot", [P, g.SLOTS])
        g.xin_h = keep(whole, "xin_h", [P, g.KC, g.E2, g.NB, g.SLOTS], F32R)
        g.xin_l = keep(whole, "xin_l", [P, g.KC, g.E2, g.NB, g.SLOTS], F32R)
        with ExitStack() as ctx:
            g.xn = keep(ctx, "xn3", [P, g.NT, g.D])
            norm_and_gate(nc, g, io)
            clear_semaphores(nc)
            choose_tokens(nc, g, io)
            clear_semaphores(nc)
            collect_tokens(nc, g, io)
            clear_semaphores(nc)
        run_choosing_experts(nc, g, io)
        clear_semaphores(nc)
        return_tokens(nc, g, io)


def lay_out(inputs):
    import numpy as np

    same = ("x", "ctx_1024", "L0_xattn_Wq", "L0_xattn_Wkv", "L0_xattn_Wo", "L0_ffn_gate_up_proj",
            "L0_ffn_down_proj", "L1_xattn_bv", "L1_xattn_bo")
    transposed = ("L0_ffn_w_gate", "L0_ffn_w_up", "L0_ffn_w_down", "L1_xattn_Wq", "L1_xattn_Wk",
                  "L1_xattn_Wv", "L1_xattn_Wo", "L1_ffn_gate_w")
    by_partition = ("L0_xattn_ln1_w", "L0_xattn_ln1_b", "L0_xattn_ln2_w", "L0_xattn_ln2_b",
                    "L1_xattn_bq", "L1_xattn_bk")
    a = {name: np.asarray(value) for name, value in inputs.items()}
    out = {name: a[name] for name in same}
    out["L0_ffn_w_router_T"] = a["L0_ffn_w_router"].T
    out["ctx_T"] = a["ctx_1024"].reshape(-1, a["ctx_1024"].shape[-1]).T
    for name in transposed:
        out[f"{name}_T"] = a[name].T
    for name in by_partition:
        out[name] = a[name].reshape(-1, P).T
    e, i, d = a["L1_ffn_w_gate"].shape

    def of_inputs(w):
        return w.reshape(e, i // P, P, d // P, P).transpose(0, 1, 4, 3, 2).reshape(e, i // P, P, d)

    down = a["L1_ffn_w_down"].reshape(e, d, i // P, P).transpose(0, 2, 3, 1)
    out["L1_ffn_w"] = np.concatenate([of_inputs(a["L1_ffn_w_gate"]), of_inputs(a["L1_ffn_w_up"]), down], axis=-1)
    return {name: np.ascontiguousarray(value) for name, value in out.items()}


def kernel(**inputs):
    import numpy as np
    import concourse.bacc as bacc
    from concourse import mybir
    from concourse.bass_utils import run_bass_kernel_spmd as run

    nc = bacc.Bacc("TRN2", target_bir_lowering=False, num_devices=1)
    arrays, io = {}, {}
    for name, a in lay_out(inputs).items():
        arrays[f"in_{name}"] = a
        io[name] = nc.dram_tensor(f"in_{name}", a.shape, mybir.dt.from_np(a.dtype), kind="ExternalInput").ap()
    io["out"] = nc.dram_tensor("out_x", io["x"].shape, mybir.dt.from_np(np.dtype("float32")), kind="ExternalOutput").ap()
    program(nc, io)
    return run(nc, [arrays], core_ids=[0]).results[0]["out_x"]
```

```python
import math
from contextlib import ExitStack

import concourse.bass as bass
from concourse import mybir

F32 = mybir.dt.float32
F32R = mybir.dt.float32r
BF16 = mybir.dt.bfloat16
I32 = mybir.dt.int32
U32 = mybir.dt.uint32
ALU = mybir.AluOpType
ACT = mybir.ActivationFunctionType
AX = mybir.AxisListType

P = 128
EPS = 1e-5


class Shared:
    pass


class Chain:

    def __init__(self, eng, sem):
        self.eng, self.sem, self.n = eng, sem, 0

    def restart(self):
        self.eng.sem_clear(self.sem)
        self.n = 0

    def __call__(self, ins):
        self.n += 1
        ins.then_inc(self.sem, 1)
        self.eng.wait_ge(self.sem, self.n)


def wait(eng, sem, value):
    if not isinstance(value, int) or value > 0:
        eng.wait_ge(sem, value)


def unrolled(eng, steps, body):
    body(0, True, steps == 1)
    if steps > 2:
        with eng.Fori(1, steps - 1) as i:
            body(i, False, False)
    if steps > 1:
        body(steps - 1, False, True)


def inverse_root(dve, link, rstd, std, var, tmp):
    link(dve.reciprocal(rstd, std))
    link(dve.tensor_tensor(tmp, rstd, rstd, ALU.mult))
    link(dve.scalar_tensor_tensor(tmp, var, EPS, tmp, ALU.add, ALU.mult))
    link(dve.tensor_scalar(tmp, tmp, -0.5, 1.5, ALU.mult, ALU.add))
    link(dve.tensor_tensor(rstd, rstd, tmp, ALU.mult))


def attend_latents(nc, g, io):
    NB, S, D, KC = g.NB, g.S, g.D, g.KC
    N = 2 * S
    NC = N // P
    DH = 64
    PAIRS, GROUPS = 8, 4
    INNER = PAIRS * P
    QSCALE = 1.0 / DH ** 0.5
    with ExitStack() as ctx:
        def sb(name, shape, dt=F32):
            return ctx.enter_context(nc.sbuf_tensor(name, shape, dt))

        def psum(name, shape):
            return ctx.enter_context(nc.psum_tensor(name, shape, F32))

        def sem(name):
            return ctx.enter_context(nc.semaphore(name))

        ctx_in, lat, xn = sb("a_ctx_in", [P, 2, D]), sb("a_lat", [P, 2, D]), sb("a_xn", [P, 4, D])
        stats, mv, rstd = sb("a_stats", [P, 6, 6]), sb("a_mv", [P, 6, 2]), sb("a_rstd", [P, 6])
        var, tmp, guess = sb("a_var", [P, 4]), sb("a_tmp", [P, 4]), sb("a_guess", [P, 4], I32)
        affine, zeros = sb("a_affine", [P, 4, KC]), sb("a_zeros", [P, D])
        full = sb("a_full", [P, KC, N])
        kvT_h = [sb(f"a_kvT_h{i}", [P, KC, N], F32R) for i in range(2)]
        kvT_l = [sb(f"a_kvT_l{i}", [P, KC, N], F32R) for i in range(2)]
        PIECES, OUT_PIECES = GROUPS, 2
        raw = [sb(f"a_raw{i}", [P, 3 * KC * N // 2]) for i in range(2)]
        w_h, w_l = sb("a_w_h", [P, 3, KC, INNER], F32R), sb("a_w_l", [P, 3, KC, INNER], F32R)
        out_h, out_l = sb("a_out_h", [P, PAIRS, D], F32R), sb("a_out_l", [P, PAIRS, D], F32R)
        k_hl = [[sb(f"a_k_hl{i}{h}", [P, N], F32R) for h in range(2)] for i in range(2)]
        q_hh = [sb(f"a_q_hh{i}", [P, 2, S], F32R) for i in range(2)]
        q_l = [sb(f"a_q_l{i}", [P, 2, S], F32R) for i in range(2)]
        halves = [slice(0, DH), slice(DH, P)]
        v = [sb(f"a_v{i}", [P, NC, 2 * P]) for i in range(2)]
        probs = [sb(f"a_p{i}", [P, N]) for i in range(4)]
        probsT = [[sb(f"a_pT{i}{h}", [P, NC, S]) for h in range(2)] for i in range(2)]
        negmax, total, inverse = sb("a_negmax", [P, 4]), sb("a_total", [P, 2, 2, 2]), sb("a_inverse", [P, 2, 2, 2])
        inverses = [sb(f"a_inverses{i}", [P, 2, 2, DH]) for i in range(2)]
        inverse_T, o_full = sb("a_inverse_T", [P, S]), [sb(f"a_o{i}", [P, S]) for i in range(4)]
        o_h, o_l = sb("a_o_h", [P, PAIRS, S], F32R), sb("a_o_l", [P, PAIRS, S], F32R)

        scores = [psum(f"a_s{i}", [P, N]) for i in range(2)]
        turned_p = [psum(f"a_t{i}", [P, NC, P]) for i in range(2)]
        out_p, k_p, v_p = psum("a_out_p", [P, 2, S]), psum("a_k_p", [P, N]), psum("a_v_p", [P, 2, 2 * P])
        q_p = psum("a_q_p", [P, N])

        loaded, const_in, zeroed, stored = sem("a_loaded"), sem("a_const_in"), sem("a_zeroed"), sem("a_stored")
        w_in = [sem(f"a_w_in{i}") for i in range(2)]
        wh_set, w_ready, ident_set, chain = sem("a_wh_set"), sem("a_w_ready"), sem("a_ident_set"), sem("a_chain")
        normed, inputs_turned, filled = sem("a_normed"), sem("a_inputs_turned"), sem("a_filled")
        kvh_set, kvl_set = sem("a_kvh_set"), sem("a_kvl_set")
        q_done, k_done, v_done = sem("a_q_done"), sem("a_k_done"), sem("a_v_done")
        qh_set, ql_set, kh_set, kl_set, v_set = sem("a_qh_set"), sem("a_ql_set"), sem("a_kh_set"), sem("a_kl_set"), sem("a_v_set")
        s_done, t_done, o_done = sem("a_s_done"), sem("a_t_done"), sem("a_o_done")
        max_set, exp_set, inv_set, spread_set = sem("a_max_set"), sem("a_exp_set"), sem("a_inv_set"), sem("a_spread_set")
        even_set, odd_set, o_set = sem("a_even_set"), sem("a_odd_set"), sem("a_o_set")
        invT_set, oh_set, ol_set = sem("a_invT_set"), sem("a_oh_set"), sem("a_ol_set")
        y_done, added = sem("a_y_done"), sem("a_added")
        x_dram = io["x"].rearrange("b (h p) d -> p b h d", p=P)
        c_dram = io["ctx_1024"].rearrange("b (h p) d -> p b h d", p=P)

        def after(b, r, bp, last):
            if r < PAIRS - 1:
                return b, r + 1, bp
            return None if last == 2 else (b + 1, 0, 1 - bp)

        def before(b, r, first):
            if r:
                return b, r - 1
            return None if first else (b - 1, PAIRS - 1)

        with nc.Block() as block:
            @block.sync
            def _(sp):
                def load(b):
                    wait(sp, loaded, 32 * b)
                    wait(sp, normed, b)
                    sp.dma_start(g.x[:, bass.ds(2 * b, 2), :], x_dram[:, bass.ds(b, 1)]).then_inc(loaded, 16)
                    sp.dma_start(ctx_in[:, :, :], c_dram[:, bass.ds(b, 1)]).then_inc(loaded, 16)

                def load_piece(i):
                    wait(sp, w_ready, i - 1)
                    if i < PIECES:
                        part = raw[i % 2][:, :].rearrange("p (w c n) -> p w c n", w=3, c=KC)
                        wq, wkv = io["L0_xattn_Wq"], io["L0_xattn_Wkv"]
                        for w, (src, at) in enumerate(((wq, 0), (wkv, 0), (wkv, INNER))):
                            at += 2 * P * i
                            sp.dma_start(part[:, w, :, :], src[:, at:at + 2 * P].rearrange("(c p) n -> p c n", p=P)
                                         ).then_inc(w_in[i % 2], 16)
                    else:
                        rows = slice((i - PIECES) * INNER // 2, (i - PIECES + 1) * INNER // 2)
                        sp.dma_start(raw[i % 2][:, 0:PAIRS * D // 2].rearrange("p (r n) -> p r n", r=PAIRS // 2),
                                     io["L0_xattn_Wo"][rows, :].rearrange("(r p) n -> p r n", p=P)
                                     ).then_inc(w_in[i % 2], 16)

                load(0)
                for i, name in enumerate(("L0_xattn_ln1_w", "L0_xattn_ln1_b", "L0_xattn_ln2_w", "L0_xattn_ln2_b")):
                    sp.dma_start(affine[:, i, :], io[name]).then_inc(const_in, 16)
                load_piece(0)
                load_piece(1)
                load(1)
                for i in range(2, PIECES + OUT_PIECES):
                    load_piece(i)
                sp.wait_ge(zeroed, 3)
                sp.dma_start(g.rows_in.rearrange("(j p) d -> p j d", p=P),
                             zeros[:, :].unsqueeze(1).to_broadcast([P, g.BLOCKS, D])).then_inc(stored, 16)
                with sp.Fori(2, NB) as b:
                    load(b)
                sp.wait_ge(stored, 16)

            @block.gpsimd
            def _(pool):
                def low_kv(b, bp, kc):
                    pool.wait_ge(kvh_set, KC * b + kc + 1)
                    pool.tensor_tensor(kvT_l[bp][:, kc, :], full[:, kc, :], kvT_h[bp][:, kc, :],
                                       ALU.subtract).then_inc(kvl_set, 1)

                def low_o(b, r):
                    pool.wait_ge(oh_set, PAIRS * b + r + 1)
                    pool.tensor_tensor(o_l[:, r, :], o_full[r % 4][:, :], o_h[:, r, :], ALU.subtract).then_inc(ol_set, 1)

                def split_piece(i):
                    pool.wait_ge(w_in[i % 2], 16 * sum(3 if n < PIECES else 1 for n in range(i % 2, i + 1, 2)))
                    if i < PIECES:
                        full_w = raw[i % 2][:, :].rearrange("p (w n) -> p w n", w=3 * KC)
                        high, low = (w[:, :, :, :].rearrange("p w c n -> p (w c) n")[:, :, 2 * P * i:2 * P * (i + 1)]
                                     for w in (w_h, w_l))
                    else:
                        full_w = raw[i % 2][:, 0:PAIRS * D // 2].rearrange("p (r n) -> p r n", r=PAIRS // 2)
                        rows = slice((i - PIECES) * PAIRS // 2, (i - PIECES + 1) * PAIRS // 2)
                        high, low = out_h[:, rows, :], out_l[:, rows, :]
                    pool.tensor_copy(high, full_w).then_inc(wh_set, 1)
                    pool.wait_ge(wh_set, i + 1)
                    pool.tensor_tensor(low, full_w, high, ALU.subtract).then_inc(w_ready, 1)

                def step(b, bp, first, last):
                    for r in range(PAIRS):
                        if r in (5, 6) and last < 2:
                            low_kv(b + 1, 1 - bp, r - 5)
                        if r >= 2:
                            low_o(b, r - 2)
                        elif not first:
                            low_o(b - 1, PAIRS + r - 2)

                pool.memset(g.ident[:, :], 0.0).then_inc(ident_set, 1)
                pool.wait_ge(ident_set, 1)
                pool.affine_select(out=g.ident[:, :], in_=g.ident[:, :], compare_op=ALU.not_equal, fill=1.0,
                                   base=0, pattern=[[-1, P]], channel_multiplier=1).then_inc(ident_set, 1)
                for par in range(2):
                    pool.memset(q_l[par][:, :, :].bitcast(F32), 0.0).then_inc(zeroed, 1)
                pool.memset(zeros[:, :], 0.0).then_inc(zeroed, 1)
                split_piece(0)
                for kc in range(KC):
                    low_kv(0, 0, kc)
                for i in range(1, PIECES + OUT_PIECES):
                    split_piece(i)
                batches(pool, NB, step)
                for r in range(PAIRS - 2, PAIRS):
                    low_o(NB - 1, r)

            @block.tensor
            def _(pe):
                def threefold(out, pairs):
                    passes = [(s, m) for (sh, sl), (mh, ml) in pairs for s, m in ((sh, mh), (sh, ml), (sl, mh))]
                    for i, (s, m) in enumerate(passes):
                        ins = pe.matmul(out, s, m, start=(i == 0), stop=(i == len(passes) - 1))
                    return ins

                def project(out, which, r, bp, at):
                    cols = slice(r * P, (r + 1) * P)
                    return threefold(out, [((w_h[:, which, kc, cols], w_l[:, which, kc, cols]),
                                            (kvT_h[bp][:, kc, at], kvT_l[bp][:, kc, at])) for kc in range(KC)])

                def project_q(b, r, bp):
                    project(q_p[:, 0:S], 0, r, bp, slice(S, N)).then_inc(q_done, 1)

                def project_k(b, r, bp, starting):
                    if starting:
                        pe.wait_ge(w_ready, r // 2 + 1)
                    wait(pe, kl_set, PAIRS * b + r)
                    project(k_p[:, :], 1, r, bp, slice(0, N)).then_inc(k_done, 1)

                def project_v(b, group, half, bp, starting):
                    m = PAIRS * b + 2 * group + half
                    if starting:
                        pe.wait_ge(w_ready, group + 1)
                    if group == 0:
                        pe.wait_ge(kvl_set, KC * b + KC)
                    wait(pe, v_set, m)
                    cols = slice(2 * P * group, 2 * P * (group + 1))
                    for c2 in range(2):
                        keys = slice((2 * half + c2) * P, (2 * half + c2 + 1) * P)
                        ins = threefold(v_p[:, c2, :], [((kvT_h[bp][:, kc, keys], kvT_l[bp][:, kc, keys]),
                                                         (w_h[:, 2, kc, cols], w_l[:, 2, kc, cols])) for kc in range(KC)])
                    ins.then_inc(v_done, 1)

                def score(b, r, j):
                    h, rows = j // 2, slice(j % 2 * P, (j % 2 + 1) * P)
                    if j == 0:
                        pe.wait_ge(ql_set, PAIRS * b + r + 1)
                        pe.wait_ge(kl_set, PAIRS * b + r + 1)
                    wait(pe, exp_set, 4 * (PAIRS * b + r) + j - 1)
                    pe.matmul(scores[j % 2][:, :], q_hh[r % 2][:, h, rows], k_hl[r % 2][h][:, :], start=True, stop=False)
                    pe.matmul(scores[j % 2][:, :], q_l[r % 2][:, h, rows], k_hl[r % 2][h][:, :],
                              start=False, stop=True).then_inc(s_done, 1)

                def turn(b, r, j):
                    s = PAIRS * b + r
                    pe.wait_ge(exp_set, 4 * s + j + 1)
                    wait(pe, odd_set if j % 2 else even_set, 2 * s + j // 2)
                    for c in range(NC):
                        ins = pe.transpose(turned_p[j % 2][:, c, :], probs[j][:, c * P:(c + 1) * P], g.ident[:, :])
                    ins.then_inc(t_done, 1)

                def attend(b, r):
                    s = PAIRS * b + r
                    pe.wait_ge(even_set, 2 * s + 2)
                    pe.wait_ge(odd_set, 2 * s + 2)
                    pe.wait_ge(v_set, s + 2 - r % 2)
                    pe.wait_ge(spread_set, s + 1)
                    wait(pe, o_set, s)
                    for half in range(2):
                        pe.transpose(out_p[:, 1, half * P:(half + 1) * P], inverses[r % 2][:, half, :, :], g.ident[:, :])
                    for c in range(NC):
                        for h in range(2):
                            at = r % 2 * P + h * DH
                            ins = pe.matmul(out_p[h * DH:(h + 1) * DH, 0, :], v[r // 2 % 2][:, c, at:at + DH],
                                            probsT[r % 2][h][:, c, :], start=(c == 0), stop=(c == NC - 1))
                    ins.then_inc(o_done, 1)

                def turn_inputs(b, kc):
                    pe.wait_ge(normed, b + 1)
                    for t in range(4):
                        ins = pe.transpose(q_p[:, t * P:(t + 1) * P], xn[:, t, kc * P:(kc + 1) * P], g.ident[:, :])
                    ins.then_inc(inputs_turned, 1)

                def project_out(b):
                    pe.wait_ge(w_ready, PIECES + OUT_PIECES)
                    pe.wait_ge(ol_set, PAIRS * (b + 1))
                    for t in range(2):
                        at = slice(t * P, (t + 1) * P)
                        ins = threefold(q_p[:, t * D:(t + 1) * D], [((o_h[:, r, at], o_l[:, r, at]),
                                                                     (out_h[:, r, :], out_l[:, r, :])) for r in range(PAIRS)])
                    ins.then_inc(y_done, 1)

                def step(b, bp, first, last):
                    for r in range(PAIRS):
                        prev, nxt = before(b, r, first), after(b, r, bp, last)
                        score(b, r, 0)
                        if prev:
                            turn(*prev, 2)
                        if nxt:
                            project_k(*nxt, first and bp == 0)
                        score(b, r, 1)
                        if prev:
                            turn(*prev, 3)
                        if nxt:
                            if r == 3:
                                wait(pe, added, b)
                            if r in (5, 6) and last < 2:
                                pe.wait_ge(filled, KC * (b + 1) + r - 4)
                            project_q(*nxt)
                        score(b, r, 2)
                        turn(b, r, 0)
                        group = r // 2 + 1
                        if group < GROUPS:
                            project_v(b, group, r % 2, bp, first and bp == 0)
                        elif last < 2:
                            project_v(b + 1, 0, r % 2, 1 - bp, False)
                        score(b, r, 3)
                        if prev:
                            attend(*prev)
                        turn(b, r, 1)
                        if r == 2 and not first:
                            pe.wait_ge(ql_set, PAIRS * b + r + 2)
                            project_out(b - 1)
                        if r in (4, 5) and last < 2:
                            pe.wait_ge(ql_set, PAIRS * b + r + 2)
                            turn_inputs(b + 1, r - 4)

                pe.wait_ge(ident_set, 2)
                for kc in range(KC):
                    wait(pe, filled, kc)
                    turn_inputs(0, kc)
                pe.wait_ge(zeroed, 2)
                pe.wait_ge(kvl_set, KC)
                project_k(0, 0, 0, True)
                project_q(0, 0, 0)
                project_v(0, 0, 0, 0, True)
                project_v(0, 0, 1, 0, True)
                batches(pe, NB, step)
                turn(NB - 1, PAIRS - 1, 2)
                turn(NB - 1, PAIRS - 1, 3)
                attend(NB - 1, PAIRS - 1)
                project_out(NB - 1)

            @block.scalar
            def _(act):
                def high_kv(b, bp, kc):
                    act.wait_ge(filled, KC * b + kc + 1)
                    act.activation(kvT_h[bp][:, kc, :], full[:, kc, :], ACT.Copy).then_inc(kvh_set, 1)

                def set_q(b, r):
                    s = PAIRS * b + r
                    act.wait_ge(q_done, s + 1)
                    wait(act, s_done, 4 * s - 4)
                    for h in range(2):
                        for half in halves:
                            ins = act.activation(q_hh[r % 2][half, h, :], q_p[halves[h], 0:S], ACT.Copy, scale=QSCALE)
                    ins.then_inc(qh_set, 1)

                def set_k(b, r):
                    act.wait_ge(k_done, PAIRS * b + r + 1)
                    for h, half in enumerate(halves):
                        ins = act.activation(k_hl[r % 2][h][half, :], k_p[half, :], ACT.Copy)
                    ins.then_inc(kh_set, 1)

                def set_v(b, group, half):
                    m = PAIRS * b + 2 * group + half
                    act.wait_ge(v_done, m + 1)
                    wait(act, o_done, m - half - 2)
                    act.activation(v[group % 2][:, 2 * half:2 * half + 2, :], v_p[:, :, :], ACT.Copy).then_inc(v_set, 1)

                def exponent(b, r, j):
                    n = 4 * (PAIRS * b + r) + j
                    act.wait_ge(max_set, n + 1)
                    wait(act, t_done, n - 3)
                    wait(act, inv_set, PAIRS * b + r - 1)
                    act.activation(probs[j][:, :], scores[j % 2][:, :], ACT.Exp, bias=negmax[:, j:j + 1],
                                   accum_out=total[:, r % 2, j % 2, j // 2:j // 2 + 1]).then_inc(exp_set, 1)

                def spread(b, r):
                    s = PAIRS * b + r
                    act.wait_ge(inv_set, s + 1)
                    wait(act, o_done, s - 1)
                    act.activation(inverses[r % 2][:, :, :, :],
                                   inverse[:, r % 2, :, :].unsqueeze(3).to_broadcast([P, 2, 2, DH]),
                                   ACT.Copy).then_inc(spread_set, 1)

                def set_even(b, r, j):
                    s = PAIRS * b + r
                    act.wait_ge(t_done, 4 * s + j + 1)
                    wait(act, o_done, s - 1)
                    act.activation(probsT[r % 2][j // 2][:, :, 0:P], turned_p[0][:, :, :], ACT.Copy).then_inc(even_set, 1)

                def high_o(b, r):
                    act.wait_ge(o_set, PAIRS * b + r + 1)
                    if r == 0:
                        wait(act, y_done, b)
                    act.activation(o_h[:, r, :], o_full[r % 4][:, :], ACT.Copy).then_inc(oh_set, 1)

                def step(b, bp, first, last):
                    for r in range(PAIRS):
                        prev, nxt = before(b, r, first), after(b, r, bp, last)
                        exponent(b, r, 0)
                        if prev:
                            set_even(*prev, 2)
                        if r == 6 and last < 2:
                            high_kv(b + 1, 1 - bp, 1)
                        if nxt:
                            set_k(*nxt[:2])
                        exponent(b, r, 1)
                        if prev:
                            spread(*prev)
                        if r == 5 and last < 2:
                            high_kv(b + 1, 1 - bp, 0)
                        if nxt:
                            set_q(*nxt[:2])
                        exponent(b, r, 2)
                        set_even(b, r, 0)
                        exponent(b, r, 3)
                        group = r // 2 + 1
                        if group < GROUPS:
                            set_v(b, group, r % 2)
                        elif last < 2:
                            set_v(b + 1, 0, r % 2)
                        if r >= 2:
                            high_o(b, r - 2)
                        elif not first:
                            high_o(b - 1, PAIRS + r - 2)

                for kc in range(KC):
                    high_kv(0, 0, kc)
                act.wait_ge(zeroed, 2)
                set_k(0, 0)
                set_q(0, 0)
                set_v(0, 0, 0)
                set_v(0, 0, 1)
                batches(act, NB, step)
                set_even(NB - 1, PAIRS - 1, 2)
                spread(NB - 1, PAIRS - 1)
                high_o(NB - 1, PAIRS - 2)
                high_o(NB - 1, PAIRS - 1)

            @block.vector
            def _(dve):
                link = Chain(dve, chain)
                PARTS = 19

                def seed_root(n):
                    link(dve.tensor_scalar(var[:, 0:n], mv[:, 0:4, 1] if n == 4 else mv[:, 4:6, 1], EPS, None, ALU.add))
                    link(dve.tensor_scalar(guess[:, 0:n], var[:, 0:n].bitcast(I32), 1, None, ALU.logical_shift_right))
                    link(dve.tensor_scalar(guess[:, 0:n], guess[:, 0:n], -1, 0x5f3759df, ALU.mult, ALU.add))

                def newton(n, src, dst, half):
                    if half == 0:
                        link(dve.tensor_tensor(tmp[:, 0:n], src, src, ALU.mult))
                        link(dve.tensor_tensor(tmp[:, 0:n], tmp[:, 0:n], var[:, 0:n], ALU.mult))
                    else:
                        link(dve.tensor_scalar(tmp[:, 0:n], tmp[:, 0:n], -0.5, 1.5, ALU.mult, ALU.add))
                        link(dve.tensor_tensor(dst, src, tmp[:, 0:n], ALU.mult))

                def prepare(b, part):
                    def rows(t):
                        return g.x[:, bass.ds(2 * b + t, 1), :]

                    if part == 0:
                        link.restart()
                        dve.wait_ge(loaded, 32 * (b + 1))
                        for t in range(2):
                            dve.bn_stats(stats[:, t, :], rows(t))
                    elif part == 1:
                        for t in range(2, 4):
                            ins = dve.bn_stats(stats[:, t, :], ctx_in[:, t - 2, :])
                        link(ins)
                    elif part == 2:
                        for t in range(4):
                            ins = dve.bn_aggr(mv[:, t, :], stats[:, t, :])
                        link(ins)
                        seed_root(4)
                    elif part in range(3, 9):
                        newton(4, guess[:, :].bitcast(F32) if part < 5 else rstd[:, 0:4], rstd[:, 0:4], (part - 3) % 2)
                    elif part == 9:
                        for t in range(2):
                            ins = dve.tensor_scalar(lat[:, t, :], rows(t), mv[:, t, 0:1], rstd[:, t:t + 1],
                                                    ALU.subtract, ALU.mult)
                        link(ins)
                    elif part == 10:
                        wait(dve, inputs_turned, KC * b)
                        for t in range(2):
                            dve.tensor_scalar(xn[:, t, :], ctx_in[:, t, :], mv[:, 2 + t, 0:1],
                                              rstd[:, 2 + t:3 + t], ALU.subtract, ALU.mult)
                    elif part == 11:
                        for t in range(2):
                            ins = dve.bn_stats(stats[:, 4 + t, :], lat[:, t, :])
                        link(ins)
                        for t in range(2):
                            ins = dve.bn_aggr(mv[:, 4 + t, :], stats[:, 4 + t, :])
                        link(ins)
                        seed_root(2)
                    elif part in range(12, 18):
                        newton(2, guess[:, 0:2].bitcast(F32) if part < 14 else rstd[:, 4:6], rstd[:, 4:6], part % 2)
                    elif part == 18:
                        for t in range(2):
                            ins = dve.tensor_scalar(xn[:, 2 + t, :], lat[:, t, :], mv[:, 4 + t, 0:1],
                                                    rstd[:, 4 + t:5 + t], ALU.subtract, ALU.mult)
                        ins.then_inc(normed, 1)

                def fill(b, kc):
                    dve.wait_ge(inputs_turned, KC * b + kc + 1)
                    wait(dve, kvl_set, KC * (b - 1) + kc + 1)
                    for which in range(2):
                        at = slice(which * S, (which + 1) * S)
                        ins = dve.tensor_scalar(full[:, kc, at], q_p[:, at], affine[:, 2 * which, kc:kc + 1],
                                                affine[:, 2 * which + 1, kc:kc + 1], ALU.mult, ALU.add)
                    ins.then_inc(filled, 1)

                def low_q(b, r):
                    dve.wait_ge(qh_set, PAIRS * b + r + 1)
                    for h, half in enumerate(halves):
                        ins = dve.scalar_tensor_tensor(q_l[r % 2][half, h, :], q_p[half, 0:S], QSCALE,
                                                       q_hh[r % 2][half, h, :], ALU.mult, ALU.subtract)
                    ins.then_inc(ql_set, 1)

                def low_k(b, r):
                    dve.wait_ge(kh_set, PAIRS * b + r + 1)
                    for h, half in enumerate(halves):
                        ins = dve.tensor_tensor(k_hl[r % 2][h][halves[1 - h], :], k_p[half, :],
                                                k_hl[r % 2][h][half, :], ALU.subtract)
                    ins.then_inc(kl_set, 1)

                def maximum(b, r, j):
                    dve.wait_ge(s_done, 4 * (PAIRS * b + r) + j + 1)
                    dve.tensor_reduce(negmax[:, j:j + 1], scores[j % 2][:, :], AX.X, ALU.max,
                                      negate=True).then_inc(max_set, 1)

                def invert(b, r):
                    s = PAIRS * b + r
                    dve.wait_ge(exp_set, 4 * s + 4)
                    wait(dve, spread_set, s - 1)
                    dve.reciprocal(inverse[:, r % 2, :, :], total[:, r % 2, :, :]).then_inc(inv_set, 1)

                def set_odd(b, r, j):
                    s = PAIRS * b + r
                    dve.wait_ge(t_done, 4 * s + j + 1)
                    wait(dve, o_done, s - 1)
                    dve.tensor_copy(probsT[r % 2][j // 2][:, :, P:2 * P], turned_p[1][:, :, :]).then_inc(odd_set, 1)

                def set_out(b, r):
                    s = PAIRS * b + r
                    dve.wait_ge(o_done, s + 1)
                    wait(dve, ol_set, s - 3)
                    dve.tensor_copy(inverse_T[:, :], out_p[:, 1, :]).then_inc(invT_set, 1)
                    dve.wait_ge(invT_set, s + 1)
                    dve.tensor_tensor(o_full[r % 4][:, :], out_p[:, 0, :], inverse_T[:, :], ALU.mult).then_inc(o_set, 1)

                def add(b):
                    dve.wait_ge(y_done, b + 1)
                    rows = g.x[:, bass.ds(2 * b, 2), :]
                    dve.tensor_tensor(rows, rows, q_p[:, :].rearrange("p (t d) -> p t d", t=2), ALU.add).then_inc(added, 1)

                def step(b, bp, first, last):
                    def between(r, j):
                        if last < 2 and 4 * r + j < PARTS:
                            prepare(b + 1, 4 * r + j)

                    for r in range(PAIRS):
                        prev, nxt = before(b, r, first), after(b, r, bp, last)
                        maximum(b, r, 0)
                        if prev:
                            invert(*prev)
                        between(r, 0)
                        maximum(b, r, 1)
                        if nxt:
                            low_k(*nxt[:2])
                        if prev:
                            set_odd(*prev, 3)
                        between(r, 1)
                        maximum(b, r, 2)
                        if nxt:
                            low_q(*nxt[:2])
                        between(r, 2)
                        maximum(b, r, 3)
                        if prev:
                            set_out(*prev)
                        set_odd(b, r, 1)
                        between(r, 3)
                        if r == 2 and not first:
                            add(b - 1)
                        if r in (4, 5) and last < 2:
                            fill(b + 1, r - 4)

                dve.memset(g.eps[:, :], EPS)
                for part in range(PARTS):
                    prepare(0, part)
                dve.wait_ge(const_in, 64)
                for kc in range(KC):
                    fill(0, kc)
                dve.wait_ge(zeroed, 2)
                low_k(0, 0)
                low_q(0, 0)
                batches(dve, NB, step)
                invert(NB - 1, PAIRS - 1)
                set_odd(NB - 1, PAIRS - 1, 3)
                set_out(NB - 1, PAIRS - 1)
                add(NB - 1)


class Norm:

    def __init__(self, ctx, nc, g, name):
        def sb(what, shape, dt):
            return [ctx.enter_context(nc.sbuf_tensor(f"{name}_{what}{i}", shape, dt)) for i in range(2)]

        def sem(what):
            return ctx.enter_context(nc.semaphore(f"{name}_{what}"))

        self.g = g
        NT = g.NT

        def of_tiles(what, shape):
            return ctx.enter_context(nc.sbuf_tensor(f"{name}_{what}", shape, F32))

        self.stats, self.mv = of_tiles("stats", [P, NT, 6]), of_tiles("mv", [P, NT, 2])
        self.std, self.rstd, self.tmp = of_tiles("std", [P, NT]), of_tiles("rstd", [P, NT]), of_tiles("tmp", [P, NT])
        self.xn = sb("xn", [P, 2, g.D], F32)
        self.full = sb("full", [P, g.KC, g.S], F32)
        self.have_var, self.have_std, self.normed = sem("have_var"), sem("have_std"), sem("normed")
        self.turned, self.filled = sem("turned"), sem("filled")
        self.high, self.low, self.chain = sem("high"), sem("low"), sem("chain")
        self.ps = [ctx.enter_context(nc.psum_tensor(f"{name}_ps{i}", [P, g.KC, g.S], F32)) for i in range(2)]

    def moments(self, dve, link):
        for t in range(self.g.NT):
            ins = dve.bn_stats(self.stats[:, t, :], self.g.x[:, t, :])
        link(ins)
        for t in range(self.g.NT):
            ins = dve.bn_aggr(self.mv[:, t, :], self.stats[:, t, :])
        ins.then_inc(self.have_var, 1)
        dve.wait_ge(self.have_std, 1)
        inverse_root(dve, link, self.rstd[:, :], self.std[:, :], self.mv[:, :, 1], self.tmp[:, :])

    def root(self, act):
        act.wait_ge(self.have_var, 1)
        act.activation(self.std[:, :], self.mv[:, :, 1], ACT.Sqrt, bias=self.g.eps[:, 0:1]).then_inc(self.have_std, 1)

    def apply(self, dve, b, par):
        wait(dve, self.turned, b - 1)
        for t in range(2):
            ins = dve.tensor_scalar(self.xn[par][:, t, :], self.g.x[:, bass.ds(2 * b + t, 1), :],
                                    self.mv[:, bass.ds(2 * b + t, 1), 0:1], self.rstd[:, bass.ds(2 * b + t, 1)],
                                    ALU.subtract, ALU.mult)
        ins.then_inc(self.normed, 1)

    def turn(self, pe, b, par):
        pe.wait_ge(self.normed, b + 1)
        wait(pe, self.filled, b - 1)
        for kc in range(self.g.KC):
            for t in range(2):
                ins = pe.transpose(self.ps[par][:, kc, t * P:(t + 1) * P],
                                   self.xn[par][:, t, kc * P:(kc + 1) * P], self.g.ident[:, :])
        ins.then_inc(self.turned, 1)

    def fill(self, dve, b, par):
        dve.wait_ge(self.turned, b + 1)
        dve.tensor_copy(self.full[par][:, :, :], self.ps[par][:, :, :]).then_inc(self.filled, 1)

    def take_high(self, act, b, par):
        act.wait_ge(self.filled, b + 1)
        act.activation(self.g.xT_h[:, :, bass.ds(b * self.g.S, self.g.S)], self.full[par][:, :, :],
                       ACT.Copy).then_inc(self.high, 1)

    def take_low(self, pool, b, par):
        at = bass.ds(b * self.g.S, self.g.S)
        pool.wait_ge(self.high, b + 1)
        pool.tensor_tensor(self.g.xT_l[:, :, at], self.full[par][:, :, :], self.g.xT_h[:, :, at],
                           ALU.subtract).then_inc(self.low, 1)


def batches(eng, NB, step):
    def body(i, first, last):
        step(2 * i, 0, first, 1 if last else 0)
        step(2 * i + 1, 1, False, 2 if last else 0)

    unrolled(eng, NB // 2, body)


def norm_and_route(nc, g, io):
    NB, KC, E = g.NB, g.KC, g.E
    with ExitStack() as ctx:
        def sem(name):
            return ctx.enter_context(nc.semaphore(name))

        router = ctx.enter_context(nc.sbuf_tensor("c_router", [P, KC, E], F32))
        logit_ps = [ctx.enter_context(nc.psum_tensor(f"c_logit{i}", [P, 2, E], F32)) for i in range(2)]
        r_in, logit_done, logit_set, kept = sem("c_r_in"), sem("c_logit_done"), sem("c_logit_set"), sem("c_kept")
        norm = Norm(ctx, nc, g, "c")

        with nc.Block() as block:
            @block.sync
            def _(sp):
                sp.dma_start(router[:, :, :], io["L0_ffn_w_router_T"].rearrange("(c p) e -> p c e", p=P)).then_inc(r_in, 16)

            @block.gpsimd
            def _(pool):
                batches(pool, NB, lambda b, par, first, last: norm.take_low(pool, b, par))

            @block.scalar
            def _(act):
                def keep(b, par):
                    act.wait_ge(norm.normed, b + 1)
                    act.activation(g.xn[:, bass.ds(2 * b, 2), :], norm.xn[par][:, :, :], ACT.Copy).then_inc(kept, 1)

                def take_logits(b, par):
                    act.wait_ge(logit_done, b + 1)
                    act.activation(g.logits[:, bass.ds(2 * b, 2), :], logit_ps[par][:, :, :],
                                   ACT.Copy).then_inc(logit_set, 1)

                def step(b, par, first, last):
                    keep(b, par)
                    if not first:
                        norm.take_high(act, b - 1, 1 - par)
                        take_logits(b - 1, 1 - par)

                norm.root(act)
                batches(act, NB, step)
                norm.take_high(act, NB - 1, 1)
                take_logits(NB - 1, 1)

            @block.tensor
            def _(pe):
                def route(b, par):
                    pe.wait_ge(norm.filled, b + 1)
                    wait(pe, logit_set, b - 1)
                    for t in range(2):
                        for kc in range(KC):
                            ins = pe.matmul(logit_ps[par][:, t, :], norm.full[par][:, kc, t * P:(t + 1) * P],
                                            router[:, kc, :], start=(kc == 0), stop=(kc == KC - 1))
                    ins.then_inc(logit_done, 1)

                def step(b, par, first, last):
                    norm.turn(pe, b, par)
                    if not first:
                        route(b - 1, 1 - par)

                pe.wait_ge(r_in, 16)
                batches(pe, NB, step)
                route(NB - 1, 1)

            @block.vector
            def _(dve):
                link = Chain(dve, norm.chain)

                def fill(b, par):
                    wait(dve, norm.low, b - 1)
                    wait(dve, logit_done, b - 1)
                    norm.fill(dve, b, par)

                def step(b, par, first, last):
                    wait(dve, kept, b - 1)
                    norm.apply(dve, b, par)
                    if not first:
                        fill(b - 1, 1 - par)

                norm.moments(dve, link)
                batches(dve, NB, step)
                fill(NB - 1, 1)


def route_tokens(nc, g, io):
    NT, E, D, BLOCKS = g.NT, g.E, g.D, g.BLOCKS
    with ExitStack() as ctx:
        def sb(name, shape, dt=F32):
            return ctx.enter_context(nc.sbuf_tensor(name, shape, dt))

        def sem(name):
            return ctx.enter_context(nc.semaphore(name))

        top, score = sb("r_top", [P, NT]), sb("r_score", [P, NT])
        order, first = sb("r_order", [P, E]), sb("r_first", [P, NT])
        hot, hot_b = sb("r_hot", [P, NT, E]), sb("r_hot_b", [P, NT, E], BF16)
        before_w, ones_w = sb("r_before_w", [P, P], BF16), sb("r_ones_w", [P, P], BF16)
        within, sums = sb("r_within", [P, NT, E]), [sb(f"r_sums{i}", [P, NT, E]) for i in range(2)]
        tile_sum = sb("r_tile_sum", [P, NT, E])
        padded_i, padded = sb("r_padded_i", [P, E], I32), sb("r_padded", [P, E])
        ends = [sb(f"r_ends{i}", [P, E]) for i in range(2)]
        starts, row = sb("r_starts", [P, E]), sb("r_row", [P, NT])
        block_start, past = sb("r_block_start", [P, BLOCKS]), sb("r_past", [P, BLOCKS, E])
        block_f = sb("r_block_f", [P, BLOCKS])
        count_ps = ctx.enter_context(nc.psum_tensor("r_count_ps", [P, NT, E], F32))
        total_ps = ctx.enter_context(nc.psum_tensor("r_total_ps", [P, NT, E], F32))
        const_set, ones_set, hot_set, counted = sem("r_const_set"), sem("r_ones_set"), sem("r_hot_set"), sem("r_counted")
        top_set, score_set, scaled = sem("r_top_set"), sem("r_score_set"), sem("r_scaled")
        row_set, scattered, chain = sem("r_row_set"), sem("r_scattered"), sem("r_chain")

        with nc.Block() as block:
            @block.gpsimd
            def _(pool):
                pool.iota(order[:, :], [[-1, E]], base=E, channel_multiplier=0,
                          allow_small_or_imprecise_dtypes=True).then_inc(const_set, 1)
                pool.iota(block_start[:, :], [[P, BLOCKS]], base=0, channel_multiplier=0,
                          allow_small_or_imprecise_dtypes=True).then_inc(const_set, 1)
                pool.memset(ones_w[:, :], 1.0).then_inc(ones_set, 1)
                pool.wait_ge(ones_set, 1)
                pool.affine_select(out=before_w[:, :], in_=ones_w[:, :], compare_op=ALU.is_gt, fill=0.0,
                                   base=0, pattern=[[1, P]], channel_multiplier=-1).then_inc(const_set, 1)
                pool.wait_ge(row_set, 1)
                pool.wait_ge(scaled, 1)
                for t in range(NT):
                    pool.indirect_dma_start(g.rows_in[:, :], bass.IndirectOffsetOnAxis(ap=g.row_of[:, t:t + 1], axis=0),
                                            g.xn[:, t, :], None).then_inc(scattered, 16)
                pool.wait_ge(scattered, 16 * NT)

            @block.scalar
            def _(act):
                act.wait_ge(top_set, 1)
                act.activation(score[:, :], top[:, :], ACT.Sigmoid).then_inc(score_set, 1)
                act.wait_ge(score_set, 1)
                for t in range(NT):
                    ins = act.activation(g.xn[:, t, :], g.xn[:, t, :], ACT.Copy, scale=score[:, t:t + 1])
                ins.then_inc(scaled, 1)

            @block.tensor
            def _(pe):
                pe.wait_ge(const_set, 3)
                pe.wait_ge(hot_set, 1)
                pe.matmul(count_ps[:, :, :], before_w[:, :], hot_b[:, :, :], start=True, stop=True)
                pe.matmul(total_ps[:, :, :], ones_w[:, :], hot_b[:, :, :], start=True, stop=True).then_inc(counted, 1)

            @block.vector
            def _(dve):
                link = Chain(dve, chain)

                def over(ap, n):
                    return ap.unsqueeze(1).to_broadcast([P, n, ap.shape[-1]])

                def along(ap, n):
                    return ap.unsqueeze(2).to_broadcast([P, ap.shape[-1], n])

                def running(bufs, at, n):
                    src, k = 0, 1
                    while k < n:
                        a, b = bufs[src], bufs[1 - src]
                        dve.tensor_copy(at(b, 0, k), at(a, 0, k))
                        link(dve.tensor_tensor(at(b, k, n), at(a, k, n), at(a, 0, n - k), ALU.add))
                        src, k = 1 - src, 2 * k
                    return bufs[src]

                dve.tensor_reduce(top[:, :], g.logits[:, :, :], AX.X, ALU.max).then_inc(top_set, 1)
                dve.wait_ge(top_set, 1)
                link(dve.tensor_tensor(hot[:, :, :], g.logits[:, :, :], along(top[:, :], E), ALU.is_equal))
                dve.wait_ge(const_set, 3)
                link(dve.tensor_tensor(hot[:, :, :], hot[:, :, :], over(order[:, :], NT), ALU.mult))
                link(dve.tensor_reduce(first[:, :], hot[:, :, :], AX.X, ALU.max))
                link(dve.tensor_tensor(hot[:, :, :], hot[:, :, :], along(first[:, :], E), ALU.is_equal))
                dve.tensor_copy(hot_b[:, :, :], hot[:, :, :]).then_inc(hot_set, 1)
                dve.wait_ge(counted, 1)
                dve.tensor_copy(within[:, :, :], count_ps[:, :, :])
                dve.tensor_copy(tile_sum[:, :, :], total_ps[:, :, :])
                link(dve.tensor_copy(sums[0][:, :, :], total_ps[:, :, :]))
                upto = running(sums, lambda a, i, j: a[:, i:j, :], NT)
                link(dve.tensor_tensor(within[:, :, :], within[:, :, :], tile_sum[:, :, :], ALU.subtract))
                link(dve.tensor_tensor(within[:, :, :], within[:, :, :], upto[:, :, :], ALU.add))
                link(dve.tensor_scalar(padded[:, :], upto[:, NT - 1, :], float(P - 1), None, ALU.add))
                link(dve.tensor_copy(padded_i[:, :], padded[:, :]))
                shift = P.bit_length() - 1
                link(dve.tensor_scalar(padded_i[:, :], padded_i[:, :], shift, shift,
                                       ALU.logical_shift_right, ALU.logical_shift_left))
                dve.tensor_copy(padded[:, :], padded_i[:, :])
                link(dve.tensor_copy(ends[0][:, :], padded_i[:, :]))
                end = running(ends, lambda a, i, j: a[:, i:j], E)
                link(dve.tensor_tensor(starts[:, :], end[:, :], padded[:, :], ALU.subtract))
                link(dve.tensor_tensor(within[:, :, :], within[:, :, :], over(starts[:, :], NT), ALU.add))
                link(dve.tensor_tensor(within[:, :, :], within[:, :, :], hot[:, :, :], ALU.mult))
                link(dve.tensor_reduce(row[:, :], within[:, :, :], AX.X, ALU.add))
                dve.tensor_copy(g.row_of[:, :], row[:, :]).then_inc(row_set, 1)
                link(dve.tensor_tensor(past[:, :, :], along(block_start[:, :], E), over(end[:, :], BLOCKS), ALU.is_ge))
                link(dve.tensor_reduce(block_f[:, :], past[:, :, :], AX.X, ALU.add))
                link(dve.tensor_scalar(block_f[:, :], block_f[:, :], float(E - 1), None, ALU.min))
                link(dve.tensor_copy(g.block_expert[:, :], block_f[:, :]))


def run_experts(nc, g, io):
    D, KC, F, BLOCKS = g.D, g.KC, g.F, g.BLOCKS
    FC = F // P
    AHEAD = 4
    with ExitStack() as ctx:
        def sb(name, shape, dt=F32, n=2):
            return [ctx.enter_context(nc.sbuf_tensor(f"{name}{i}", shape, dt)) for i in range(n)]

        def psum(name, shape):
            return ctx.enter_context(nc.psum_tensor(name, shape, F32))

        def sem(name):
            return ctx.enter_context(nc.semaphore(name))

        rows, rowsT = sb("e_rows", [P, D], n=AHEAD), sb("e_rowsT", [P, KC, P])
        w_in, w_out = sb("e_w_in", [P, KC, 2 * F], n=AHEAD), sb("e_w_out", [P, FC, D], n=AHEAD)
        silu, hidden, hiddenT = sb("e_silu", [P, F]), sb("e_hidden", [P, F]), sb("e_hiddenT", [P, FC, P])
        result = sb("e_result", [P, D])
        gate_ps = [psum(f"e_gate{i}", [P, F]) for i in range(2)]
        up_ps = [psum(f"e_up{i}", [P, F]) for i in range(2)]
        rowsT_ps, hiddenT_ps, result_ps = psum("e_rowsT_ps", [P, KC, P]), psum("e_hiddenT_ps", [P, FC, P]), psum("e_result_ps", [P, D])
        rows_in = [sem(f"e_rows_in{i}") for i in range(AHEAD)]
        w_in_in = [sem(f"e_w_in_in{i}") for i in range(AHEAD)]
        w_out_in = [sem(f"e_w_out_in{i}") for i in range(AHEAD)]
        rows_turned, rowsT_set, gated, upped = sem("e_rows_turned"), sem("e_rowsT_set"), sem("e_gated"), sem("e_upped")
        silu_set, hidden_set, hidden_turned, hiddenT_set = sem("e_silu_set"), sem("e_hidden_set"), sem("e_hidden_turned"), sem("e_hiddenT_set")
        summed, result_set = sem("e_summed"), sem("e_result_set")
        stored = [sem(f"e_stored{i}") for i in range(2)]
        in_dram = io["L0_ffn_gate_up_proj"].rearrange("e (c p) f -> p e c f", p=P)
        out_dram = io["L0_ffn_down_proj"].rearrange("e (c p) d -> p e c d", p=P)
        rows_dram = g.rows_in[:, :].rearrange("(j p) d -> p j d", p=P)
        results_dram = g.rows_out[:, :].rearrange("(j p) d -> p j d", p=P)

        ROUNDS = -(-BLOCKS // AHEAD)
        LAST = (BLOCKS - 1) % AHEAD

        def blocks(eng, step):
            def body(i, first, last):
                n = BLOCKS - AHEAD * (ROUNDS - 1) if last else AHEAD
                for q in range(n):
                    step(AHEAD * i + q, q, i, first and q == 0, last and q == n - 1)

            unrolled(eng, ROUNDS, body)

        with nc.Block() as block:
            @block.sync
            def _(sp):
                def load(j, q, i, first, last):
                    wait(sp, rows_turned, j - AHEAD + 1)
                    sp.dma_start(rows[q][:, :], rows_dram[:, bass.ds(j, 1), :]).then_inc(rows_in[q], 16)
                    expert = sp.value_load(g.block_expert[0:1, bass.ds(j, 1)], min_val=0, max_val=g.E - 1)
                    wait(sp, upped, j - AHEAD + 1)
                    sp.dma_start(w_in[q][:, :, :], in_dram[:, bass.ds(expert, 1), :, :]).then_inc(w_in_in[q], 16)
                    wait(sp, summed, j - AHEAD + 1)
                    sp.dma_start(w_out[q][:, :, :], out_dram[:, bass.ds(expert, 1), :, :]).then_inc(w_out_in[q], 16)

                blocks(sp, load)

            @block.gpsimd
            def _(pool):
                def store(j, q, i, first, last):
                    pool.wait_ge(result_set, j + 1)
                    pool.dma_start(results_dram[:, bass.ds(j, 1), :], result[q % 2][:, :]).then_inc(stored[q % 2], 16)

                blocks(pool, store)
                for par in range(2):
                    pool.wait_ge(stored[par], 16 * len(range(par, BLOCKS, 2)))

            @block.tensor
            def _(pe):
                def turn_rows(j, q, i):
                    pe.wait_ge(rows_in[q], 16 * i + 16)
                    wait(pe, rowsT_set, j)
                    for c in range(KC):
                        ins = pe.transpose(rowsT_ps[:, c, :], rows[q][:, c * P:(c + 1) * P], g.ident[:, :])
                    ins.then_inc(rows_turned, 1)

                def product(out, q, half, done):
                    for c in range(KC):
                        ins = pe.matmul(out[q % 2][:, :], rowsT[q % 2][:, c, :], w_in[q][:, c, half * F:(half + 1) * F],
                                        start=(c == 0), stop=(c == KC - 1))
                    ins.then_inc(done, 1)

                def turn_hidden(j, q):
                    pe.wait_ge(hidden_set, j + 1)
                    wait(pe, hiddenT_set, j)
                    for c in range(FC):
                        ins = pe.transpose(hiddenT_ps[:, c, :], hidden[q % 2][:, c * P:(c + 1) * P], g.ident[:, :])
                    ins.then_inc(hidden_turned, 1)

                def down(j, q, i):
                    pe.wait_ge(hiddenT_set, j + 1)
                    pe.wait_ge(w_out_in[q], 16 * i + 16)
                    wait(pe, result_set, j)
                    for c in range(FC):
                        ins = pe.matmul(result_ps[:, :], hiddenT[q % 2][:, c, :], w_out[q][:, c, :],
                                        start=(c == 0), stop=(c == FC - 1))
                    ins.then_inc(summed, 1)

                def step(j, q, i, first, last):
                    if not last:
                        turn_rows(j + 1, (q + 1) % AHEAD, i + (q + 1) // AHEAD)
                    pe.wait_ge(rowsT_set, j + 1)
                    pe.wait_ge(w_in_in[q], 16 * i + 16)
                    wait(pe, hidden_set, j - 1)
                    product(gate_ps, q, 0, gated)
                    if not first:
                        turn_hidden(j - 1, (q - 1) % AHEAD)
                    product(up_ps, q, 1, upped)
                    if not first:
                        down(j - 1, (q - 1) % AHEAD, i if q else i - 1)

                turn_rows(0, 0, 0)
                blocks(pe, step)
                turn_hidden(BLOCKS - 1, LAST)
                down(BLOCKS - 1, LAST, ROUNDS - 1)

            @block.scalar
            def _(act):
                def take_result(j, q, i):
                    act.wait_ge(summed, j + 1)
                    wait(act, stored[q % 2], 16 * ((AHEAD // 2) * i + q // 2))
                    act.activation(result[q % 2][:, :], result_ps[:, :], ACT.Copy).then_inc(result_set, 1)

                def step(j, q, i, first, last):
                    act.wait_ge(gated, j + 1)
                    wait(act, hidden_set, j - 1)
                    act.activation(silu[q % 2][:, :], gate_ps[q % 2][:, :], ACT.Silu).then_inc(silu_set, 1)
                    if not first:
                        take_result(j - 1, (q - 1) % AHEAD, i if q else i - 1)

                blocks(act, step)
                take_result(BLOCKS - 1, LAST, ROUNDS - 1)

            @block.vector
            def _(dve):
                def set_rowsT(j, q):
                    dve.wait_ge(rows_turned, j + 1)
                    wait(dve, upped, j - 1)
                    dve.tensor_copy(rowsT[q % 2][:, :, :], rowsT_ps[:, :, :]).then_inc(rowsT_set, 1)

                def set_hiddenT(j, q):
                    dve.wait_ge(hidden_turned, j + 1)
                    wait(dve, summed, j - 1)
                    dve.tensor_copy(hiddenT[q % 2][:, :, :], hiddenT_ps[:, :, :]).then_inc(hiddenT_set, 1)

                def step(j, q, i, first, last):
                    if not last:
                        set_rowsT(j + 1, (q + 1) % AHEAD)
                    if not first:
                        set_hiddenT(j - 1, (q - 1) % AHEAD)
                    dve.wait_ge(silu_set, j + 1)
                    dve.wait_ge(upped, j + 1)
                    wait(dve, hidden_turned, j - 1)
                    dve.tensor_tensor(hidden[q % 2][:, :], up_ps[q % 2][:, :], silu[q % 2][:, :], ALU.mult).then_inc(hidden_set, 1)

                set_rowsT(0, 0)
                blocks(dve, step)
                set_hiddenT(BLOCKS - 1, LAST)


def shared_expert(nc, g, io):
    D, KC, F, NT = g.D, g.KC, g.F, g.NT
    FC = F // P
    N = 512
    TILES = N // P
    GROUPS = NT // TILES
    with ExitStack() as ctx:
        def sb(name, shape, dt=F32):
            return ctx.enter_context(nc.sbuf_tensor(name, shape, dt))

        def psum(name, shape):
            return ctx.enter_context(nc.psum_tensor(name, shape, F32))

        def sem(name):
            return ctx.enter_context(nc.semaphore(name))

        names = ("L0_ffn_w_gate_T", "L0_ffn_w_up_T", "L0_ffn_w_down_T")
        raw = [sb("s_raw_g", [P, KC, F]), sb("s_raw_u", [P, KC, F]), sb("s_raw_d", [P, FC, D])]
        w_h = [sb("s_h_g", [P, KC, F], F32R), sb("s_h_u", [P, KC, F], F32R), sb("s_h_d", [P, FC, D], F32R)]
        w_l = [sb("s_l_g", [P, KC, F], F32R), sb("s_l_u", [P, KC, F], F32R), sb("s_l_d", [P, FC, D], F32R)]
        silu, hidden = [sb(f"s_silu{i}", [P, N]) for i in range(2)], [sb(f"s_hidden{i}", [P, N]) for i in range(2)]
        hid_h = [sb(f"s_hid_h{i}", [P, FC, N], F32R) for i in range(2)]
        hid_l = [sb(f"s_hid_l{i}", [P, FC, N], F32R) for i in range(2)]
        gate_ps = [psum(f"s_gate{i}", [P, N]) for i in range(2)]
        up_ps = [psum(f"s_up{i}", [P, N]) for i in range(2)]
        sum_ps = [psum(f"s_sum{i}", [P, 2, D]) for i in range(2)]
        w_in, wh_set, wl_set = sem("s_w_in"), sem("s_wh_set"), sem("s_wl_set")
        gated, upped, silu_set, hidden_set = sem("s_gated"), sem("s_upped"), sem("s_silu_set"), sem("s_hidden_set")
        high, low, summed, added = sem("s_high"), sem("s_low"), sem("s_summed"), sem("s_added")
        gathered = sem("s_gathered")

        with nc.Block() as block:
            @block.sync
            def _(sp):
                for dst, name in zip(raw, names):
                    sp.dma_start(dst[:, :, :], io[name].rearrange("(c p) n -> p c n", p=P)).then_inc(w_in, 16)

            @block.scalar
            def _(act):
                act.wait_ge(w_in, 48)
                for i in range(3):
                    act.activation(w_h[i][:, :, :], raw[i][:, :, :], ACT.Copy).then_inc(wh_set, 1)

                def silu_of(s, n):
                    act.wait_ge(gated, n + 1)
                    wait(act, hidden_set, n - 1)
                    act.activation(silu[s % 2][:, :], gate_ps[s % 2][:, :], ACT.Silu).then_inc(silu_set, 1)

                def high_of(s, n, grp):
                    act.wait_ge(hidden_set, n + 1)
                    wait(act, summed, grp - 1)
                    act.activation(hid_h[grp % 2][:, s, :], hidden[s % 2][:, :], ACT.Copy).then_inc(high, 1)

                for grp in range(GROUPS):
                    for s in range(FC):
                        silu_of(s, FC * grp + s)
                        high_of(s, FC * grp + s, grp)

            @block.gpsimd
            def _(pool):
                for t in range(g.NT):
                    pool.indirect_dma_start(g.xn[:, t, :], None, g.rows_out[:, :],
                                            bass.IndirectOffsetOnAxis(ap=g.row_of[:, t:t + 1], axis=0)
                                            ).then_inc(gathered, 16)
                pool.wait_ge(gathered, 16 * g.NT)

            @block.tensor
            def _(pe):
                def product(out, i, c, grp, done):
                    at = slice(grp * N, (grp + 1) * N)
                    passes = [(w, x, kc) for kc in range(KC)
                              for w, x in ((w_h, g.xT_h), (w_h, g.xT_l), (w_l, g.xT_h))]
                    for k, (w, x, kc) in enumerate(passes):
                        ins = pe.matmul(out[:, :], w[i][:, kc, c * P:(c + 1) * P], x[:, kc, at],
                                        start=(k == 0), stop=(k == len(passes) - 1))
                    ins.then_inc(done, 1)

                def down(grp):
                    pe.wait_ge(wl_set, 3)
                    pe.wait_ge(low, FC * (grp + 1))
                    wait(pe, added, grp)
                    high, low_part = hid_h[grp % 2], hid_l[grp % 2]
                    passes = [(h, w, c) for c in range(FC)
                              for h, w in ((high, w_h), (high, w_l), (low_part, w_h))]
                    for t in range(TILES):
                        for k, (h, w, c) in enumerate(passes):
                            ins = pe.matmul(sum_ps[t // 2][:, t % 2, :], h[:, c, t * P:(t + 1) * P], w[2][:, c, :],
                                            start=(k == 0), stop=(k == len(passes) - 1))
                    ins.then_inc(summed, 1)

                pe.wait_ge(wl_set, 2)
                for grp in range(GROUPS):
                    for c in range(FC):
                        n = FC * grp + c
                        wait(pe, hidden_set, n - 1)
                        product(gate_ps[n % 2], 0, c, grp, gated)
                        product(up_ps[n % 2], 1, c, grp, upped)
                        if c == 0 and grp:
                            down(grp - 1)
                down(GROUPS - 1)

            @block.vector
            def _(dve):
                def low_hidden(n):
                    dve.wait_ge(high, n + 1)
                    part = n // FC % 2
                    dve.tensor_tensor(hid_l[part][:, n % FC, :], hidden[n % 2][:, :], hid_h[part][:, n % FC, :],
                                      ALU.subtract).then_inc(low, 1)

                def add(grp):
                    dve.wait_ge(summed, grp + 1)
                    for i in range(2):
                        rows = g.x[:, grp * TILES + 2 * i:grp * TILES + 2 * i + 2, :]
                        ins = dve.tensor_tensor(rows, rows, sum_ps[i][:, :, :], ALU.add)
                    ins.then_inc(added, 1)

                for i in range(3):
                    dve.wait_ge(wh_set, i + 1)
                    dve.tensor_tensor(w_l[i][:, :, :], raw[i][:, :, :], w_h[i][:, :, :], ALU.subtract).then_inc(wl_set, 1)
                for grp in range(GROUPS):
                    for c in range(FC):
                        n = FC * grp + c
                        dve.wait_ge(silu_set, n + 1)
                        dve.wait_ge(upped, n + 1)
                        wait(dve, low, n - 1)
                        dve.tensor_tensor(hidden[c % 2][:, :], up_ps[c % 2][:, :], silu[c % 2][:, :],
                                          ALU.mult).then_inc(hidden_set, 1)
                        low_hidden(n)
                        if c == 1 and grp:
                            add(grp - 1)
                add(GROUPS - 1)


def add_rows(nc, g, io):
    NB = g.NB
    with ExitStack() as ctx:
        def sem(name):
            return ctx.enter_context(nc.semaphore(name))

        raw = [ctx.enter_context(nc.sbuf_tensor(f"g_raw{i}", [P, g.KC, g.D], F32)) for i in range(3)]
        out_raw = ctx.enter_context(nc.sbuf_tensor("g_out_raw", [P, g.CTX_GROUPS, g.D], F32))
        loaded, zeroed, raw_set = sem("g_loaded"), sem("g_zeroed"), sem("g_raw_set")
        wh_set = sem("g_wh_set")
        splits = [(g.ctx_w_l[i], raw[i], g.ctx_w_h[i]) for i in range(3)] + [(g.ctx_out_l, out_raw, g.ctx_out_h)]
        LOADS = 3 + 4 + 4
        norm = Norm(ctx, nc, g, "g")
        with nc.Block() as block:
            @block.sync
            def _(sp):
                for i, name in enumerate(("Wq", "Wk", "Wv")):
                    sp.dma_start(raw[i][:, :, :], io[f"L1_xattn_{name}_T"].rearrange("(c p) n -> p c n", p=P)).then_inc(loaded, 16)
                sp.dma_start(g.ctx_bias_q[:, :], io["L1_xattn_bq"]).then_inc(loaded, 16)
                sp.dma_start(g.ctx_bias_k[:, :], io["L1_xattn_bk"]).then_inc(loaded, 16)
                sp.dma_start(g.ctx_bias_v[:, :], io["L1_xattn_bv"].partition_broadcast(P)).then_inc(loaded, 16)
                sp.dma_start(g.ctx_bias_o[:, :], io["L1_xattn_bo"].partition_broadcast(P)).then_inc(loaded, 16)
                sp.wait_ge(zeroed, 1)
                rows = io["L1_xattn_Wo_T"].rearrange("(r j p) n -> j p r n", j=4, p=g.CTX_HEAD)
                for j in range(4):
                    sp.dma_start(out_raw[P // 4 * j:P // 4 * j + g.CTX_HEAD, :, :], rows[j]).then_inc(loaded, 16)

            @block.gpsimd
            def _(pool):
                pool.memset(out_raw[:, :, :], 0.0).then_inc(zeroed, 1)
                for n, (low, full, high) in enumerate(splits):
                    pool.wait_ge(wh_set, n + 1)
                    pool.tensor_tensor(low[:, :, :], full[:, :, :], high[:, :, :], ALU.subtract)
                batches(pool, NB, lambda b, par, first, last: norm.take_low(pool, b, par))

            @block.scalar
            def _(act):
                def step(b, par, first, last):
                    if not first:
                        norm.take_high(act, b - 1, 1 - par)

                act.wait_ge(loaded, 16 * LOADS)
                act.wait_ge(raw_set, 1)
                for _, full, high in splits:
                    act.activation(high[:, :, :], full[:, :, :], ACT.Copy).then_inc(wh_set, 1)
                norm.root(act)
                batches(act, NB, step)
                norm.take_high(act, NB - 1, 1)

            @block.tensor
            def _(pe):
                batches(pe, NB, lambda b, par, first, last: norm.turn(pe, b, par))

            @block.vector
            def _(dve):
                link = Chain(dve, norm.chain)

                def fill(b, par):
                    wait(dve, norm.low, b - 1)
                    norm.fill(dve, b, par)

                def step(b, par, first, last):
                    norm.apply(dve, b, par)
                    if not first:
                        fill(b - 1, 1 - par)

                dve.wait_ge(loaded, 16 * LOADS)
                dve.tensor_scalar(raw[0][:, :, :], raw[0][:, :, :], 1.0 / g.D ** 0.5, None, ALU.mult)
                dve.tensor_scalar(g.ctx_bias_q[:, :], g.ctx_bias_q[:, :], 1.0 / g.D ** 0.5, None, ALU.mult).then_inc(raw_set, 1)
                link(dve.tensor_tensor(g.x[:, :, :], g.x[:, :, :], g.xn[:, :, :], ALU.add))
                norm.moments(dve, link)
                batches(dve, NB, step)
                fill(NB - 1, 1)


def attend_context(nc, g, io):
    NB, S, D, KC = g.NB, g.S, g.D, g.KC
    HEADS, DH = 16, 16
    PER = P // DH
    UNITS, GROUPS, PAD = 16, 4, 32
    with ExitStack() as ctx:
        def sb(name, shape, dt=F32):
            return ctx.enter_context(nc.sbuf_tensor(name, shape, dt))

        def psum(name, shape):
            return ctx.enter_context(nc.psum_tensor(name, shape, F32))

        def sem(name):
            return ctx.enter_context(nc.semaphore(name))

        w_h, w_l, out_h, out_l = g.ctx_w_h, g.ctx_w_l, g.ctx_out_h, g.ctx_out_l
        WQ, WK, WV = range(3)
        bias_q, bias_k, bias_v, bias_o = g.ctx_bias_q, g.ctx_bias_k, g.ctx_bias_v, g.ctx_bias_o
        mask = sb("h_mask", [P, PER])
        ctx_raw = sb("h_ctx", [P, KC, S])
        ctx_h, ctx_l = sb("h_ctx_h", [P, KC, S], F32R), sb("h_ctx_l", [P, KC, S], F32R)
        q_h = [sb(f"h_q_h{i}", [P, KC, S], F32R) for i in range(2)]
        q_l = [sb(f"h_q_l{i}", [P, KC, S], F32R) for i in range(2)]
        k_full = sb("h_k", [P, KC, S])
        k_h, k_l = sb("h_k_h", [P, KC, S], F32R), sb("h_k_l", [P, KC, S], F32R)
        kz_h, kz_l = sb("h_kz_h", [P, KC, PER, S], F32R), sb("h_kz_l", [P, KC, PER, S], F32R)
        probsT = [sb(f"h_probsT{i}", [P, 4, 2, S]) for i in range(2)]
        probs = [sb(f"h_probs{i}", [P, 2, S]) for i in range(4)]
        v = [sb(f"h_v{i}", [P, 2, HEADS, PAD]) for i in range(2)]
        negmax, total = sb("h_negmax", [P, 4, 2]), sb("h_total", [P, 2, 2, 4])
        one_inverse = sb("h_one_inverse", [P, 2, 4])
        inverse = [sb(f"h_inverse{i}", [P, 2, 4, PAD]) for i in range(2)]
        scale_T, o_full = sb("h_scale_T", [P, 2, S]), [sb(f"h_o{i}", [P, S]) for i in range(2)]
        o_h, o_l = sb("h_o_h", [P, GROUPS, S], F32R), sb("h_o_l", [P, GROUPS, S], F32R)
        scores = [psum(f"h_scores{i}", [P, 2, S]) for i in range(2)]
        turned_p = [psum(f"h_turned{i}", [P, 2, 2, P]) for i in range(2)]
        proj, out_p, y_p = psum("h_proj", [P, 2, S]), psum("h_out", [P, 2, S]), psum("h_y", [P, 2, D])
        ctx_in, zeroed, chain = sem("h_ctx_in"), sem("h_zeroed"), sem("h_chain")
        mask_set, first_low = sem("h_mask_set"), sem("h_first_low")
        ctxh_set, ctxl_set = sem("h_ctxh_set"), sem("h_ctxl_set")
        q_done, qh_set, ql_set = sem("h_q_done"), sem("h_qh_set"), sem("h_ql_set")
        k_done, k_set, kh_set, kl_set, kz_set = sem("h_k_done"), sem("h_k_set"), sem("h_kh_set"), sem("h_kl_set"), sem("h_kz_set")
        v_done, v_set = sem("h_v_done"), sem("h_v_set")
        scored, max_set, exp_set, turned = sem("h_scored"), sem("h_max_set"), sem("h_exp_set"), sem("h_turned")
        even_set, odd_set = sem("h_even_set"), sem("h_odd_set")
        recip_set, inv_set = sem("h_recip_set"), sem("h_inv_set")
        o_done, scaleT_set, o_set, oh_set, ol_set = sem("h_o_done"), sem("h_scaleT_set"), sem("h_o_set"), sem("h_oh_set"), sem("h_ol_set")
        y_done, added, biased = sem("h_y_done"), sem("h_added"), sem("h_biased")
        ctx_dram = io["ctx_T"].rearrange("(c p) t -> p c t", p=P)

        with nc.Block() as block:
            @block.sync
            def _(sp):
                sp.dma_start(ctx_raw[:, :, :], ctx_dram[:, :, 0:S]).then_inc(ctx_in, 16)

                def load(b):
                    sp.wait_ge(ctxl_set, b)
                    sp.dma_start(ctx_raw[:, :, :], ctx_dram[:, :, bass.ds(b * S, S)]).then_inc(ctx_in, 16)

                with sp.Fori(1, NB) as b:
                    load(b)

            @block.gpsimd
            def _(pool):
                def pad(m, b, both=True):
                    def heads(part):
                        return part[:, m, :].unsqueeze(1).to_broadcast([P, PER, S])

                    own = mask[:, :].unsqueeze(2).to_broadcast([P, PER, S])
                    pool.wait_ge(kl_set, b + 1)
                    wait(pool, scored, UNITS * (b - 1) + (m + 1) * UNITS // 2)
                    ins = pool.tensor_tensor(kz_h[:, m, :, :], heads(k_h), own, ALU.mult)
                    if both:
                        ins = pool.tensor_tensor(kz_l[:, m, :, :], heads(k_l), own, ALU.mult)
                    ins.then_inc(kz_set, 1)

                def low_k(b):
                    pool.wait_ge(kh_set, b + 1)
                    pool.tensor_tensor(k_l[:, :, :], k_full[:, :, :], k_h[:, :, :], ALU.subtract).then_inc(kl_set, 1)

                def low_ctx(b):
                    pool.wait_ge(ctxh_set, b + 1)
                    pool.tensor_tensor(ctx_l[:, :, :], ctx_raw[:, :, :], ctx_h[:, :, :], ALU.subtract).then_inc(ctxl_set, 1)

                def low_o(b, grp):
                    pool.wait_ge(oh_set, GROUPS * b + grp + 1)
                    pool.tensor_tensor(o_l[:, grp, :], o_full[grp % 2][:, :], o_h[:, grp, :], ALU.subtract).then_inc(ol_set, 1)

                def add_bias(b):
                    rows = g.x[:, bass.ds(2 * b, 2), :]
                    pool.tensor_tensor(rows, rows, bias_o[:, :].unsqueeze(1).to_broadcast([P, 2, D]),
                                       ALU.add).then_inc(biased, 1)

                def step(b, par, first, last):
                    pad(1, b)
                    add_bias(b)
                    if not first:
                        low_o(b - 1, 2)
                        low_o(b - 1, 3)
                    if last < 2:
                        low_k(b + 1)
                        pad(0, b + 1)
                    low_o(b, 0)
                    low_o(b, 1)
                    if not last:
                        low_ctx(b + 2)

                link = Chain(pool, chain)
                link(pool.memset(mask[:, :], 1.0))
                link(pool.affine_select(out=mask[:, :], in_=mask[:, :], compare_op=ALU.is_ge, fill=0.0,
                                        base=0, pattern=[[-DH, PER]], channel_multiplier=1))
                link(pool.affine_select(out=mask[:, :], in_=mask[:, :], compare_op=ALU.is_ge, fill=0.0,
                                        base=DH - 1, pattern=[[DH, PER]], channel_multiplier=-1))
                pool.sem_inc(mask_set, 1)
                low_ctx(0)
                low_k(0)
                pad(0, 0, both=False)
                low_ctx(1)
                batches(pool, NB, step)
                low_o(NB - 1, 2)
                low_o(NB - 1, 3)

            @block.scalar
            def _(act):
                def high_ctx(b):
                    act.wait_ge(ctx_in, 16 * b + 16)
                    wait(act, v_done, b)
                    act.activation(ctx_h[:, :, :], ctx_raw[:, :, :], ACT.Copy).then_inc(ctxh_set, 1)

                def set_q(b, par):
                    act.wait_ge(q_done, b + 1)
                    for m in range(KC):
                        ins = act.activation(q_h[par][:, m, :], proj[:, m, :], ACT.Identity, bias=bias_q[:, m:m + 1])
                    ins.then_inc(qh_set, 1)

                def set_k(b):
                    act.wait_ge(k_done, b + 1)
                    wait(act, kz_set, 2 * b)
                    for m in range(KC):
                        ins = act.activation(k_full[:, m, :], proj[:, m, :], ACT.Identity, bias=bias_k[:, m:m + 1])
                    ins.then_inc(k_set, 1)
                    act.wait_ge(k_set, b + 1)
                    act.activation(k_h[:, :, :], k_full[:, :, :], ACT.Copy).then_inc(kh_set, 1)

                def exponent(b, u):
                    n = UNITS * b + u
                    pair, half = (u // 2) % 2, u % 2
                    act.wait_ge(max_set, n + 1)
                    wait(act, turned, n - 3)
                    if u % 4 == 0:
                        wait(act, inv_set, GROUPS * b + u // 4 - 1)
                    for h in range(2):
                        ins = act.activation(probs[u % 4][:, h, :], scores[u % 2][:, h, :], ACT.Exp,
                                             bias=negmax[:, u % 4, h:h + 1],
                                             accum_out=total[:, (u // 4) % 2, half, 2 * pair + h:2 * pair + h + 1])
                    ins.then_inc(exp_set, 1)

                def set_even(b, u):
                    n = UNITS * b + u
                    act.wait_ge(turned, n + 1)
                    wait(act, o_done, GROUPS * b + u // 4 - 1)
                    pair = (u // 2) % 2
                    act.activation(probsT[(u // 4) % 2][:, 2 * pair:2 * pair + 2, :, 0:P], turned_p[0][:, :, :, :],
                                   ACT.Copy).then_inc(even_set, 1)

                def high_o(b, grp):
                    act.wait_ge(o_set, GROUPS * b + grp + 1)
                    if grp == 0:
                        wait(act, y_done, b)
                    act.activation(o_h[:, grp, :], o_full[grp % 2][:, :], ACT.Copy).then_inc(oh_set, 1)

                def step(b, par, first, last):
                    for u in range(UNITS):
                        exponent(b, u)
                        if u == 1 and not first:
                            high_o(b - 1, 2)
                        if u == 5 and not first:
                            high_o(b - 1, 3)
                        if u == 6 and last < 2:
                            set_k(b + 1)
                        if u == 9:
                            high_o(b, 0)
                        if u == 10 and last < 2:
                            set_q(b + 1, 1 - par)
                        if u == 13:
                            high_o(b, 1)
                        if u == 14 and not last:
                            high_ctx(b + 2)
                        if u % 2 == 0 and u >= 2:
                            set_even(b, u - 2)
                        if u == 0 and not first:
                            set_even(b - 1, UNITS - 2)

                high_ctx(0)
                set_k(0)
                set_q(0, 0)
                high_ctx(1)
                batches(act, NB, step)
                set_even(NB - 1, UNITS - 2)
                high_o(NB - 1, 2)
                high_o(NB - 1, 3)

            @block.tensor
            def _(pe):
                def threefold(out, stationary, moving, kcs):
                    passes = [(s, m) for kc in kcs
                              for s, m in ((stationary(kc)[0], moving(kc)[0]), (stationary(kc)[0], moving(kc)[1]),
                                           (stationary(kc)[1], moving(kc)[0]))]
                    for i, (s, m) in enumerate(passes):
                        ins = pe.matmul(out, s, m, start=(i == 0), stop=(i == len(passes) - 1))
                    return ins

                def project_k(b):
                    wait(pe, v_set, b)
                    pe.wait_ge(ctxl_set, b + 1)
                    for m in range(KC):
                        ins = threefold(proj[:, m, :],
                                        lambda kc: (w_h[WK][:, kc, m * P:(m + 1) * P], w_l[WK][:, kc, m * P:(m + 1) * P]),
                                        lambda kc: (ctx_h[:, kc, :], ctx_l[:, kc, :]), range(KC))
                    ins.then_inc(k_done, 1)

                def project_q(b):
                    at = bass.ds(b * S, S)
                    pe.wait_ge(k_set, b + 1)
                    for m in range(KC):
                        ins = threefold(proj[:, m, :],
                                        lambda kc: (w_h[WQ][:, kc, m * P:(m + 1) * P], w_l[WQ][:, kc, m * P:(m + 1) * P]),
                                        lambda kc: (g.xT_h[:, kc, at], g.xT_l[:, kc, at]), range(KC))
                    ins.then_inc(q_done, 1)

                def project_v(b):
                    pe.wait_ge(ql_set, b + 1)
                    for c in range(2):
                        ins = threefold(proj[:, c, :],
                                        lambda kc: (ctx_h[:, kc, c * P:(c + 1) * P], ctx_l[:, kc, c * P:(c + 1) * P]),
                                        lambda kc: (w_h[WV][:, kc, :], w_l[WV][:, kc, :]), range(KC))
                    ins.then_inc(v_done, 1)

                def score(b, par, u):
                    n = UNITS * b + u
                    m, pair, half = u // 8, (u % 8) // 2, u % 2
                    if u == 0:
                        pe.wait_ge(ql_set, b + 1)
                    if u % 8 == 0:
                        pe.wait_ge(kz_set, 2 * b + m + 1)
                    wait(pe, exp_set, n - 1)
                    at, heads = slice(half * P, (half + 1) * P), slice(2 * pair, 2 * pair + 2)
                    threefold(scores[u % 2][:, :, :], lambda kc: (q_h[par][:, m, at], q_l[par][:, m, at]),
                              lambda kc: (kz_h[:, m, heads, :], kz_l[:, m, heads, :]), range(1)).then_inc(scored, 1)

                def turn(b, u):
                    n = UNITS * b + u
                    pe.wait_ge(exp_set, n + 1)
                    if u % 2:
                        wait(pe, odd_set, UNITS // 2 * b + u // 2)
                    else:
                        wait(pe, even_set, UNITS // 2 * b + u // 2)
                    for h in range(2):
                        for c in range(2):
                            ins = pe.transpose(turned_p[u % 2][:, h, c, :], probs[u % 4][:, h, c * P:(c + 1) * P],
                                               g.ident[:, :])
                    ins.then_inc(turned, 1)

                def weigh(b, par, grp):
                    n = GROUPS * b + grp
                    if grp == 0:
                        pe.wait_ge(v_set, b + 1)
                    pe.wait_ge(even_set, 2 * n + 2)
                    pe.wait_ge(odd_set, 2 * n + 2)
                    pe.wait_ge(inv_set, n + 1)
                    wait(pe, o_set, n)
                    for half in range(2):
                        pe.transpose(out_p[:, 1, half * P:(half + 1) * P],
                                     inverse[grp % 2][:, half, :, :], g.ident[:, :])
                    for c in range(2):
                        for j in range(4):
                            ins = pe.matmul(out_p[PAD * j:PAD * (j + 1), 0, :], v[par][:, c, 4 * grp + j, :],
                                            probsT[grp % 2][:, j, c, :], start=(c == 0), stop=(c == 1))
                    ins.then_inc(o_done, 1)

                def project_out(b):
                    pe.wait_ge(ol_set, GROUPS * b + GROUPS)
                    wait(pe, added, b)
                    for t in range(2):
                        at = slice(t * P, (t + 1) * P)
                        ins = threefold(y_p[:, t, :], lambda r: (o_h[:, r, at], o_l[:, r, at]),
                                        lambda r: (out_h[:, r, :], out_l[:, r, :]), range(GROUPS))
                    ins.then_inc(y_done, 1)

                def step(b, par, first, last):
                    for u in range(UNITS):
                        score(b, par, u)
                        if u >= 2:
                            turn(b, u - 2)
                        elif not first:
                            turn(b - 1, UNITS + u - 2)
                        if u == 3 and not first:
                            weigh(b - 1, 1 - par, 3)
                        if u in (7, 11, 15):
                            weigh(b, par, (u - 7) // 4)
                        if u == 5 and last < 2:
                            project_k(b + 1)
                        if u == 8 and not first:
                            project_out(b - 1)
                        if u == 9 and last < 2:
                            project_q(b + 1)
                        if u == 12 and last < 2:
                            project_v(b + 1)

                project_k(0)
                project_q(0)
                project_v(0)
                pe.wait_ge(first_low, 1)
                batches(pe, NB, step)
                turn(NB - 1, UNITS - 2)
                turn(NB - 1, UNITS - 1)
                weigh(NB - 1, 1, 3)
                project_out(NB - 1)

            @block.vector
            def _(dve):
                def part_q(b, par):
                    dve.wait_ge(qh_set, b + 1)
                    for m in range(KC):
                        ins = dve.scalar_tensor_tensor(q_l[par][:, m, :], proj[:, m, :], bias_q[:, m:m + 1],
                                                       q_h[par][:, m, :], ALU.add, ALU.subtract)
                    ins.then_inc(ql_set, 1)

                def set_v(b, par):
                    dve.wait_ge(v_done, b + 1)
                    dve.tensor_tensor(v[par][:, :, :, 0:DH], proj[:, :, :].rearrange("p c (h d) -> p c h d", h=HEADS),
                                      bias_v[:, :].rearrange("p (h d) -> p h d", h=HEADS).unsqueeze(1)
                                      .to_broadcast([P, 2, HEADS, DH]), ALU.add).then_inc(v_set, 1)

                def maximum(b, u):
                    dve.wait_ge(scored, UNITS * b + u + 1)
                    dve.tensor_reduce(negmax[:, u % 4, :], scores[u % 2][:, :, :], AX.X, ALU.max,
                                      negate=True).then_inc(max_set, 1)

                def set_odd(b, u):
                    dve.wait_ge(turned, UNITS * b + u + 1)
                    wait(dve, o_done, GROUPS * b + u // 4 - 1)
                    pair = (u // 2) % 2
                    dve.tensor_copy(probsT[(u // 4) % 2][:, 2 * pair:2 * pair + 2, :, P:2 * P],
                                    turned_p[1][:, :, :, :]).then_inc(odd_set, 1)

                def invert(b, grp):
                    n = GROUPS * b + grp
                    dve.wait_ge(exp_set, 4 * n + 4)
                    wait(dve, o_done, n - 1)
                    dve.reciprocal(one_inverse[:, :, :], total[:, grp % 2, :, :]).then_inc(recip_set, 1)
                    dve.wait_ge(recip_set, n + 1)
                    dve.tensor_copy(inverse[grp % 2][:, :, :, :],
                                    one_inverse[:, :, :].unsqueeze(3).to_broadcast([P, 2, 4, PAD])).then_inc(inv_set, 1)

                def set_out(b, grp):
                    n = GROUPS * b + grp
                    dve.wait_ge(o_done, n + 1)
                    dve.tensor_copy(scale_T[:, grp % 2, :], out_p[:, 1, :]).then_inc(scaleT_set, 1)
                    dve.wait_ge(scaleT_set, n + 1)
                    wait(dve, ol_set, n - 1)
                    dve.tensor_tensor(o_full[grp % 2][:, :], out_p[:, 0, :], scale_T[:, grp % 2, :],
                                      ALU.mult).then_inc(o_set, 1)

                def add(b):
                    dve.wait_ge(y_done, b + 1)
                    dve.wait_ge(biased, b + 1)
                    rows = g.x[:, bass.ds(2 * b, 2), :]
                    dve.tensor_tensor(rows, rows, y_p[:, :, :], ALU.add).then_inc(added, 1)

                def step(b, par, first, last):
                    for u in range(UNITS):
                        maximum(b, u)
                        if u % 4 == 1:
                            if u > 1:
                                invert(b, u // 4 - 1)
                            elif not first:
                                invert(b - 1, 3)
                        if u % 2 == 1 and u >= 3:
                            set_odd(b, u - 2)
                        if u == 1 and not first:
                            set_odd(b - 1, UNITS - 1)
                        if u == 0 and not first:
                            set_out(b - 1, 2)
                        if u == 4 and not first:
                            set_out(b - 1, 3)
                        if u in (8, 12):
                            set_out(b, (u - 8) // 4)
                        if u == 9 and not first:
                            add(b - 1)
                        if u == 10 and last < 2:
                            part_q(b + 1, 1 - par)
                        if u == 13 and last < 2:
                            set_v(b + 1, 1 - par)

                for i in range(2):
                    dve.memset(v[i][:, :, :, :], 0.0).then_inc(zeroed, 1)
                dve.wait_ge(mask_set, 1)
                dve.wait_ge(kl_set, 1)
                dve.tensor_tensor(kz_l[:, 0, :, :], k_l[:, 0, :].unsqueeze(1).to_broadcast([P, PER, S]),
                                  mask[:, :].unsqueeze(2).to_broadcast([P, PER, S]), ALU.mult).then_inc(first_low, 1)
                dve.wait_ge(zeroed, 2)
                part_q(0, 0)
                set_v(0, 0)
                batches(dve, NB, step)
                invert(NB - 1, 3)
                set_odd(NB - 1, UNITS - 1)
                set_out(NB - 1, 2)
                set_out(NB - 1, 3)
                add(NB - 1)


def norm_and_gate(nc, g, io):
    NB, S, KC, E = g.NB, g.S, g.KC, g.CHOOSERS
    with ExitStack() as ctx:
        def sem(name):
            return ctx.enter_context(nc.semaphore(name))

        gate = ctx.enter_context(nc.sbuf_tensor("k_gate", [P, KC, E], F32))
        logit_ps = [ctx.enter_context(nc.psum_tensor(f"k_logit{i}", [P, 2, E], F32)) for i in range(2)]
        gate_in, logit_done, logit_set, kept = sem("k_gate_in"), sem("k_logit_done"), sem("k_logit_set"), sem("k_kept")
        norm = Norm(ctx, nc, g, "k")

        with nc.Block() as block:
            @block.sync
            def _(sp):
                sp.dma_start(gate[:, :, :], io["L1_ffn_gate_w_T"].rearrange("(c p) e -> p c e", p=P)).then_inc(gate_in, 16)

            @block.scalar
            def _(act):
                def take_logits(b, par):
                    act.wait_ge(logit_done, b + 1)
                    act.activation(g.gate_logits[:, :, bass.ds(b, 1), :].rearrange("p t b e -> p t (b e)"),
                                   logit_ps[par][:, :, :], ACT.Copy).then_inc(logit_set, 1)

                def step(b, par, first, last):
                    act.wait_ge(norm.normed, b + 1)
                    act.activation(g.xn[:, bass.ds(2 * b, 2), :], norm.xn[par][:, :, :], ACT.Copy).then_inc(kept, 1)
                    if not first:
                        take_logits(b - 1, 1 - par)

                norm.root(act)
                batches(act, NB, step)
                take_logits(NB - 1, 1)

            @block.tensor
            def _(pe):
                def route(b, par):
                    pe.wait_ge(norm.filled, b + 1)
                    wait(pe, logit_set, b - 1)
                    for t in range(2):
                        for kc in range(KC):
                            ins = pe.matmul(logit_ps[par][:, t, :], norm.full[par][:, kc, t * P:(t + 1) * P],
                                            gate[:, kc, :], start=(kc == 0), stop=(kc == KC - 1))
                    ins.then_inc(logit_done, 1)

                def step(b, par, first, last):
                    norm.turn(pe, b, par)
                    if not first:
                        route(b - 1, 1 - par)

                pe.wait_ge(gate_in, 16)
                batches(pe, NB, step)
                route(NB - 1, 1)

            @block.vector
            def _(dve):
                link = Chain(dve, norm.chain)

                def fill(b, par):
                    wait(dve, logit_done, b - 1)
                    norm.fill(dve, b, par)

                def step(b, par, first, last):
                    wait(dve, kept, b - 1)
                    norm.apply(dve, b, par)
                    if not first:
                        fill(b - 1, 1 - par)

                norm.moments(dve, link)
                batches(dve, NB, step)
                fill(NB - 1, 1)


def exact_exp(dve, link, x, power, power_i, rest, series):
    LN2_HIGH = 0.693359375
    LN2_LOW = math.log(2) - LN2_HIGH
    ROUND = 1.5 * 2.0 ** 23
    TERMS = 8
    link(dve.tensor_scalar(x, x, -87.0, None, ALU.max))
    link(dve.tensor_scalar(power, x, 1 / math.log(2), ROUND, ALU.mult, ALU.add))
    link(dve.tensor_scalar(power, power, ROUND, None, ALU.subtract))
    link(dve.scalar_tensor_tensor(rest, power, -LN2_HIGH, x, ALU.mult, ALU.add))
    link(dve.scalar_tensor_tensor(rest, power, -LN2_LOW, rest, ALU.mult, ALU.add))
    link(dve.tensor_scalar(series, rest, 1 / math.factorial(TERMS), None, ALU.mult))
    for n in range(TERMS - 1, 0, -1):
        link(dve.scalar_tensor_tensor(series, series, 1 / math.factorial(n), rest, ALU.add, ALU.mult))
    link(dve.tensor_scalar(power, power, 127.0, None, ALU.add))
    link(dve.tensor_copy(power_i, power))
    link(dve.tensor_scalar(power_i, power_i, 23, None, ALU.logical_shift_left))
    link(dve.scalar_tensor_tensor(x, series, 1.0, power_i.bitcast(F32), ALU.add, ALU.mult))


def choose_tokens(nc, g, io):
    NB, S, E, SLOTS = g.NB, g.S, g.CHOOSERS, g.SLOTS
    ROWS = NB * E
    with ExitStack() as ctx:
        def sb(name, shape, dt=F32):
            return ctx.enter_context(nc.sbuf_tensor(name, shape, dt))

        def sem(name):
            return ctx.enter_context(nc.semaphore(name))

        peak, total = sb("t_peak", [P, 2 * NB]), sb("t_total", [P, 2 * NB])
        inverse = sb("t_inverse", [P, 2 * NB])
        work = [sb(f"t_work{i}", [ROWS, S]) for i in range(2)]
        top = sb("t_top", [ROWS, 8])
        chosen, rank, none = sb("t_chosen", [ROWS, S]), sb("t_rank", [ROWS, S]), sb("t_none", [ROWS, S])
        rows_ps = ctx.enter_context(nc.psum_tensor("t_rows_ps", [ROWS, 2, P], F32))
        place_ps = ctx.enter_context(nc.psum_tensor("t_place_ps", [P, 2, ROWS], F32))
        power, rest, series = (sb(f"t_{name}", [P, 2 * NB, E]) for name in ("power", "rest", "series"))
        power_i = sb("t_power_i", [P, 2 * NB, E], I32)
        ready, turned = sem("t_ready"), sem("t_turned")
        ranked, returned, chain, none_set = sem("t_ranked"), sem("t_returned"), sem("t_chain"), sem("t_none_set")
        by_token = g.gate_logits[:, :, :, :].rearrange("p t b e -> p (t b) e")
        affinity = g.affinity[:, :, :].rearrange("p t (b e) -> p (t b) e", e=E)

        def along(ap):
            return ap.unsqueeze(2).to_broadcast([P, 2 * NB, E])

        with nc.Block() as block:
            @block.gpsimd
            def _(pool):
                pool.memset(none[:, :], 0.0).then_inc(none_set, 1)
                pool.iota(g.slot[:, :], [[1, SLOTS]], base=1, channel_multiplier=0,
                          allow_small_or_imprecise_dtypes=True).then_inc(none_set, 1)

            @block.tensor
            def _(pe):
                pe.wait_ge(ready, 1)
                for t in range(2):
                    ins = pe.transpose(rows_ps[:, t, :], g.affinity[:, t, :], g.ident[:, :])
                ins.then_inc(turned, 1)
                pe.wait_ge(ranked, 1)
                for t in range(2):
                    ins = pe.transpose(place_ps[:, t, :], rank[:, t * P:(t + 1) * P], g.ident[0:ROWS, 0:ROWS])
                ins.then_inc(returned, 1)

            @block.vector
            def _(dve):
                link = Chain(dve, chain)
                link(dve.tensor_reduce(peak[:, :], by_token, AX.X, ALU.max))
                link(dve.tensor_tensor(by_token, by_token, along(peak[:, :]), ALU.subtract))
                exact_exp(dve, link, by_token, power[:, :, :], power_i[:, :, :], rest[:, :, :], series[:, :, :])
                link(dve.tensor_reduce(total[:, :], by_token, AX.X, ALU.add))
                link(dve.reciprocal(inverse[:, :], total[:, :]))
                dve.tensor_tensor(affinity, by_token, along(inverse[:, :]), ALU.mult).then_inc(ready, 1)
                dve.wait_ge(turned, 1)
                link(dve.tensor_copy(work[0][:, :], rows_ps[:, :, :].rearrange("r t p -> r (t p)")))
                for i in range(SLOTS // 8):
                    link(dve.max(top[:, :], work[i % 2][:, :]))
                    link(dve.match_replace(work[1 - i % 2][:, :], top[:, :], work[i % 2][:, :], -1.0))
                link(dve.tensor_scalar(chosen[:, :], work[SLOTS // 8 % 2][:, :], 0.0, None, ALU.is_lt))
                dve.wait_ge(none_set, 2)
                link(dve.tensor_tensor_scan(rank[:, :], chosen[:, :], none[:, :], 0.0, ALU.add, ALU.add))
                dve.tensor_tensor(rank[:, :], rank[:, :], chosen[:, :], ALU.mult).then_inc(ranked, 1)
                dve.wait_ge(returned, 1)
                dve.tensor_copy(g.place[:, :, :], place_ps[:, :, :])


def collect_tokens(nc, g, io):
    NB, D, KC, E, SLOTS = g.NB, g.D, g.KC, g.CHOOSERS, g.SLOTS
    with ExitStack() as ctx:
        def sem(name):
            return ctx.enter_context(nc.semaphore(name))

        x_h = [ctx.enter_context(nc.sbuf_tensor(f"l_x_h{i}", [P, 2, D], F32R)) for i in range(2)]
        x_l = [ctx.enter_context(nc.sbuf_tensor(f"l_x_l{i}", [P, 2, D], F32R)) for i in range(2)]
        slots = [ctx.enter_context(nc.sbuf_tensor(f"l_slots{i}", [P, 2, E, SLOTS], F32R)) for i in range(2)]
        ps = [[ctx.enter_context(nc.psum_tensor(f"l_ps{i}{kc}", [P, E, SLOTS], F32)) for kc in range(KC)] for i in range(2)]
        xh_set, xl_set, collected = sem("l_xh_set"), sem("l_xl_set"), sem("l_collected")
        slots_set = sem("l_slots_set")
        high, low = sem("l_high"), sem("l_low")

        def place_of(part, kc, b):
            return part[:, kc, :, bass.ds(b, 1), :].rearrange("p e b s -> p e (b s)")

        with nc.Block() as block:
            @block.gpsimd
            def _(pool):
                def step(b, par, first, last):
                    pool.wait_ge(xh_set, b + 1)
                    pool.tensor_tensor(x_l[par][:, :, :], g.xn[:, bass.ds(2 * b, 2), :], x_h[par][:, :, :],
                                       ALU.subtract).then_inc(xl_set, 1)

                batches(pool, NB, step)

            @block.scalar
            def _(act):
                def high_x(b, par):
                    wait(act, collected, b - 1)
                    act.activation(x_h[par][:, :, :], g.xn[:, bass.ds(2 * b, 2), :], ACT.Copy).then_inc(xh_set, 1)

                def step(b, par, first, last):
                    if last < 2:
                        high_x(b + 1, 1 - par)
                    act.wait_ge(collected, b + 1)
                    for kc in range(KC):
                        ins = act.activation(place_of(g.xin_h, kc, b), ps[par][kc][:, :, :], ACT.Copy)
                    ins.then_inc(high, 1)

                high_x(0, 0)
                batches(act, NB, step)

            @block.tensor
            def _(pe):
                def step(b, par, first, last):
                    pe.wait_ge(slots_set, b + 1)
                    pe.wait_ge(xl_set, b + 1)
                    wait(pe, low, b - 1)
                    for kc in range(KC):
                        passes = [(x, t) for t in range(2) for x in (x_h[par], x_l[par])]
                        for i, (x, t) in enumerate(passes):
                            ins = pe.matmul(ps[par][kc][:, :, :], x[:, t, kc * P:(kc + 1) * P], slots[par][:, t, :, :],
                                            start=(i == 0), stop=(i == len(passes) - 1))
                    ins.then_inc(collected, 1)

                batches(pe, NB, step)

            @block.vector
            def _(dve):
                def choose(b, par):
                    wait(dve, collected, b - 1)
                    for t in range(2):
                        ins = dve.tensor_tensor(slots[par][:, t, :, :],
                                                g.place[:, t, bass.ds(b * E, E)].unsqueeze(2).to_broadcast([P, E, SLOTS]),
                                                g.slot[:, :].unsqueeze(1).to_broadcast([P, E, SLOTS]), ALU.is_equal)
                    ins.then_inc(slots_set, 1)

                def step(b, par, first, last):
                    if last < 2:
                        choose(b + 1, 1 - par)
                    dve.wait_ge(high, b + 1)
                    for kc in range(KC):
                        ins = dve.tensor_tensor(place_of(g.xin_l, kc, b), ps[par][kc][:, :, :],
                                                place_of(g.xin_h, kc, b), ALU.subtract)
                    ins.then_inc(low, 1)

                choose(0, 0)
                batches(dve, NB, step)


def run_choosing_experts(nc, g, io):
    NB, D, KC, E, SLOTS = g.NB, g.D, g.KC, g.CHOOSERS, g.SLOTS
    CHUNKS = g.I // P
    N = NB * SLOTS
    TILES = N // P
    W = 2 * KC * P + D
    RAWS = 4
    with ExitStack() as ctx:
        def sb(name, shape, dt=F32):
            return ctx.enter_context(nc.sbuf_tensor(name, shape, dt))

        def sem(name):
            return ctx.enter_context(nc.semaphore(name))

        raw = [sb(f"n_raw{i}", [P, W]) for i in range(RAWS)]
        w_h, w_l = [sb(f"n_w_h{i}", [P, W], F32R) for i in range(RAWS)], [sb(f"n_w_l{i}", [P, W], F32R) for i in range(RAWS)]
        silu, hidden = [sb(f"n_silu{i}", [P, N]) for i in range(2)], [sb(f"n_hidden{i}", [P, N]) for i in range(2)]
        hid_h = [sb(f"n_hid_h{i}", [P, N], F32R) for i in range(2)]
        hid_l = [sb(f"n_hid_l{i}", [P, N], F32R) for i in range(2)]
        result = sb("n_result", [P, TILES, D])
        gate_ps = [ctx.enter_context(nc.psum_tensor(f"n_gate{i}", [P, N], F32)) for i in range(2)]
        up_ps = [ctx.enter_context(nc.psum_tensor(f"n_up{i}", [P, N], F32)) for i in range(2)]
        sum_ps = [ctx.enter_context(nc.psum_tensor(f"n_sum{i}", [P, D], F32)) for i in range(TILES)]
        raw_in = [sem(f"n_raw_in{i}") for i in range(RAWS)]
        wh_set, wl_set, gated, upped = sem("n_wh_set"), sem("n_wl_set"), sem("n_gated"), sem("n_upped")
        silu_set, hidden_set, high, low = sem("n_silu_set"), sem("n_hidden_set"), sem("n_high"), sem("n_low")
        downed, taken, stored = sem("n_downed"), sem("n_taken"), sem("n_stored")
        store = g.chosen_out.rearrange("(q r) (e s) d -> r s e q d", r=2, e=E)

        def chunk_before(e, m):
            return (e - 1, CHUNKS - 1) if m == 0 else (e, m - 1)

        with nc.Block() as block:
            @block.sync
            def _(sp):
                def step(e, first, last):
                    for m in range(CHUNKS):
                        if not first or m >= RAWS:
                            sp.wait_ge(wl_set, CHUNKS * e + m - RAWS + 1)
                        sp.dma_start(raw[m % RAWS][:, :], io["L1_ffn_w"][bass.ds(e, 1), m, :, :]
                                     .rearrange("e p w -> p (e w)")).then_inc(raw_in[m % RAWS], 16)

                unrolled(sp, E, step)

            @block.scalar
            def _(act):
                def high_w(e, m):
                    act.wait_ge(raw_in[m % RAWS], 16 * ((CHUNKS // RAWS) * e + m // RAWS + 1))
                    wait(act, downed, CHUNKS * e + m - RAWS + 1)
                    act.activation(w_h[m % RAWS][:, :], raw[m % RAWS][:, :], ACT.Copy).then_inc(wh_set, 1)

                def step(e, first, last):
                    for m in range(CHUNKS):
                        c = CHUNKS * e + m
                        act.wait_ge(gated, c + 1)
                        if not first or m >= 2:
                            act.wait_ge(hidden_set, c - 1)
                        act.activation(silu[m % 2][:, :], gate_ps[m % 2][:, :], ACT.Silu).then_inc(silu_set, 1)
                        if m + 2 < CHUNKS:
                            high_w(e, m + 2)
                        elif not last:
                            high_w(e + 1, m + 2 - CHUNKS)
                        act.wait_ge(hidden_set, c + 1)
                        if not first or m >= 2:
                            act.wait_ge(downed, c - 1)
                        act.activation(hid_h[m % 2][:, :], hidden[m % 2][:, :], ACT.Copy).then_inc(high, 1)

                high_w(0, 0)
                high_w(0, 1)
                unrolled(act, E, step)

            @block.gpsimd
            def _(pool):
                def step(e, first, last):
                    for m in range(CHUNKS):
                        c = CHUNKS * e + m
                        pool.wait_ge(wh_set, c + 1)
                        pool.tensor_tensor(w_l[m % RAWS][:, :], raw[m % RAWS][:, :], w_h[m % RAWS][:, :],
                                           ALU.subtract).then_inc(wl_set, 1)
                        if m == 4 and not first:
                            keep(e - 1)

                def keep(e):
                    pool.wait_ge(taken, e + 1)
                    for r in range(2):
                        pool.dma_start(store[r, :, bass.ds(e, 1), :, :].rearrange("s e q d -> s (e q) d"),
                                       result[r * SLOTS:(r + 1) * SLOTS, :, :]).then_inc(stored, 16)

                unrolled(pool, E, step)
                keep(E - 1)
                pool.wait_ge(stored, 32 * E)

            @block.tensor
            def _(pe):
                def product(out, e, m, at, done):
                    passes = [(w, x, kc) for kc in range(KC)
                              for w, x in ((w_h, g.xin_h), (w_h, g.xin_l), (w_l, g.xin_h))]
                    for i, (w, x, kc) in enumerate(passes):
                        ins = pe.matmul(out[:, :], w[m % RAWS][:, at + kc * P:at + (kc + 1) * P],
                                        x[:, kc, bass.ds(e, 1), :, :].rearrange("p e b s -> p (e b s)"),
                                        start=(i == 0), stop=(i == len(passes) - 1))
                    ins.then_inc(done, 1)

                def down(e, m):
                    pe.wait_ge(low, CHUNKS * e + m + 1)
                    if m == 0:
                        wait(pe, taken, e)
                    at = slice(2 * KC * P, W)
                    for t in range(TILES):
                        of = slice(t * P, (t + 1) * P)
                        passes = ((hid_h, w_h), (hid_h, w_l), (hid_l, w_h))
                        for i, (h, w) in enumerate(passes):
                            ins = pe.matmul(sum_ps[t][:, :], h[m % 2][:, of], w[m % RAWS][:, at],
                                            start=(m == 0 and i == 0), stop=(m == CHUNKS - 1 and i == len(passes) - 1))
                    ins.then_inc(downed, 1)

                def step(e, first, last):
                    for m in range(CHUNKS):
                        c = CHUNKS * e + m
                        pe.wait_ge(wl_set, c + 1)
                        if not first or m >= 2:
                            pe.wait_ge(hidden_set, c - 1)
                        product(gate_ps[m % 2], e, m, 0, gated)
                        product(up_ps[m % 2], e, m, KC * P, upped)
                        if not first or m:
                            down(*chunk_before(e, m))

                unrolled(pe, E, step)
                down(E - 1, CHUNKS - 1)

            @block.vector
            def _(dve):
                def take(e):
                    dve.wait_ge(downed, CHUNKS * (e + 1))
                    wait(dve, stored, 32 * e)
                    for t in range(TILES):
                        ins = dve.tensor_copy(result[:, t, :], sum_ps[t][:, :])
                    ins.then_inc(taken, 1)

                def step(e, first, last):
                    for m in range(CHUNKS):
                        c = CHUNKS * e + m
                        dve.wait_ge(silu_set, c + 1)
                        dve.wait_ge(upped, c + 1)
                        if not first or m >= 2:
                            dve.wait_ge(low, c - 1)
                        dve.tensor_tensor(hidden[m % 2][:, :], up_ps[m % 2][:, :], silu[m % 2][:, :],
                                          ALU.mult).then_inc(hidden_set, 1)
                        dve.wait_ge(high, c + 1)
                        dve.tensor_tensor(hid_l[m % 2][:, :], hidden[m % 2][:, :], hid_h[m % 2][:, :],
                                          ALU.subtract).then_inc(low, 1)
                        if m == 0 and not first:
                            take(e - 1)

                unrolled(dve, E, step)
                take(E - 1)


def return_tokens(nc, g, io):
    NB, D, E, SLOTS = g.NB, g.D, g.CHOOSERS, g.SLOTS
    PAIRS = E * SLOTS // P
    with ExitStack() as ctx:
        def sb(name, shape, dt=F32):
            return [ctx.enter_context(nc.sbuf_tensor(f"{name}{i}", shape, dt)) for i in range(2)]

        def sem(name):
            return ctx.enter_context(nc.semaphore(name))

        y, y_h, y_l = sb("u_y", [P, PAIRS, D]), sb("u_y_h", [P, PAIRS, D], F32R), sb("u_y_l", [P, PAIRS, D], F32R)
        slots, gates = sb("u_slots", [P, 2, E, SLOTS]), sb("u_gates", [P, 2, E, SLOTS])
        gate_h, gate_l = sb("u_gate_h", [P, 2, PAIRS, P], F32R), sb("u_gate_l", [P, 2, PAIRS, P], F32R)
        turn_ps = [[ctx.enter_context(nc.psum_tensor(f"u_turn{i}{t}", [P, PAIRS, P], F32)) for t in range(2)] for i in range(2)]
        sum_ps = [ctx.enter_context(nc.psum_tensor(f"u_sum{i}", [P, 2, D], F32)) for i in range(2)]
        y_in = [sem(f"u_y_in{i}") for i in range(2)]
        yh_set, yl_set, chosen, weighed, turned = sem("u_yh_set"), sem("u_yl_set"), sem("u_chosen"), sem("u_weighed"), sem("u_turned")
        high, low, summed, added, stored = sem("u_high"), sem("u_low"), sem("u_summed"), sem("u_added"), sem("u_stored")
        results = g.chosen_out.rearrange("b (c p) d -> p b c d", p=P)
        out = io["out"].rearrange("b (t p) d -> p b t d", p=P)

        def halves(eng, step):
            def body(i, first, last):
                step(2 * i, 0, first, 1 if last else 0, i)
                step(2 * i + 1, 1, False, 2 if last else 0, i)

            unrolled(eng, NB // 2, body)

        with nc.Block() as block:
            @block.sync
            def _(sp):
                def step(b, par, first, last):
                    wait(sp, yl_set, b - 1)
                    sp.dma_start(y[par][:, :, :], results[:, bass.ds(b, 1), :, :]).then_inc(y_in[par], 16)

                batches(sp, NB, step)

            @block.gpsimd
            def _(pool):
                def step(b, par, first, last):
                    pool.wait_ge(yh_set, b + 1)
                    pool.tensor_tensor(y_l[par][:, :, :], y[par][:, :, :], y_h[par][:, :, :], ALU.subtract).then_inc(yl_set, 1)
                    if not first:
                        store(b - 1)

                def store(b):
                    pool.wait_ge(added, b + 1)
                    pool.dma_start(out[:, bass.ds(b, 1), :, :], g.x[:, bass.ds(2 * b, 2), :]).then_inc(stored, 16)

                batches(pool, NB, step)
                store(NB - 1)
                pool.wait_ge(stored, 16 * NB)

            @block.scalar
            def _(act):
                def high_y(b, par, i):
                    act.wait_ge(y_in[par], 16 * i + 16)
                    wait(act, summed, b - 1)
                    act.activation(y_h[par][:, :, :], y[par][:, :, :], ACT.Copy).then_inc(yh_set, 1)

                def high_gates(b, par):
                    act.wait_ge(turned, b + 1)
                    wait(act, summed, b - 1)
                    for t in range(2):
                        ins = act.activation(gate_h[par][:, t, :, :], turn_ps[par][t][:, :, :], ACT.Copy)
                    ins.then_inc(high, 1)

                def step(b, par, first, last, i):
                    if last < 2:
                        high_gates(b + 1, 1 - par)
                        high_y(b + 1, 1 - par, i + par)

                high_gates(0, 0)
                high_y(0, 0, 0)
                halves(act, step)

            @block.tensor
            def _(pe):
                def turn(b, par):
                    pe.wait_ge(weighed, b + 1)
                    wait(pe, low, b - 1)
                    for t in range(2):
                        for c in range(PAIRS):
                            ins = pe.transpose(turn_ps[par][t][:, c, :], gates[par][:, t, 2 * c:2 * c + 2, :], g.ident[:, :])
                    ins.then_inc(turned, 1)

                def step(b, par, first, last):
                    pe.wait_ge(low, b + 1)
                    pe.wait_ge(yl_set, b + 1)
                    wait(pe, added, b - 1)
                    for t in range(2):
                        passes = [(s, m, c) for c in range(PAIRS)
                                  for s, m in ((gate_h, y_h), (gate_h, y_l), (gate_l, y_h))]
                        for i, (s, m, c) in enumerate(passes):
                            ins = pe.matmul(sum_ps[par][:, t, :], s[par][:, t, c, :], m[par][:, c, :],
                                            start=(i == 0), stop=(i == len(passes) - 1))
                    ins.then_inc(summed, 1)
                    if not last:
                        turn(b + 2, par)

                turn(0, 0)
                turn(1, 1)
                batches(pe, NB, step)

            @block.vector
            def _(dve):
                def weigh(b, par):
                    for t in range(2):
                        ins = dve.tensor_tensor(slots[par][:, t, :, :],
                                                g.place[:, t, bass.ds(b * E, E)].unsqueeze(2).to_broadcast([P, E, SLOTS]),
                                                g.slot[:, :].unsqueeze(1).to_broadcast([P, E, SLOTS]), ALU.is_equal)
                    ins.then_inc(chosen, 1)
                    dve.wait_ge(chosen, b + 1)
                    wait(dve, turned, b - 1)
                    for t in range(2):
                        ins = dve.tensor_tensor(gates[par][:, t, :, :], slots[par][:, t, :, :],
                                                g.affinity[:, t, bass.ds(b * E, E)].unsqueeze(2).to_broadcast([P, E, SLOTS]),
                                                ALU.mult)
                    ins.then_inc(weighed, 1)

                def take_low(b, par):
                    dve.wait_ge(high, b + 1)
                    for t in range(2):
                        ins = dve.tensor_tensor(gate_l[par][:, t, :, :], turn_ps[par][t][:, :, :],
                                                gate_h[par][:, t, :, :], ALU.subtract)
                    ins.then_inc(low, 1)

                def step(b, par, first, last):
                    if not last:
                        weigh(b + 2, par)
                    if last < 2:
                        take_low(b + 1, 1 - par)
                    dve.wait_ge(summed, b + 1)
                    rows = g.x[:, bass.ds(2 * b, 2), :]
                    dve.tensor_tensor(rows, rows, sum_ps[par][:, :, :], ALU.add).then_inc(added, 1)

                weigh(0, 0)
                weigh(1, 1)
                take_low(0, 0)
                batches(dve, NB, step)


def clear_semaphores(nc):
    numbers = sorted(nc.free_semaphores)
    runs = [[numbers[0], numbers[0]]]
    for number in numbers[1:]:
        if number == runs[-1][1] + 1:
            runs[-1][1] = number
        else:
            runs.append([number, number])
    with nc.Block() as block:
        @block.sync
        def _(sp):
            for first, last in runs:
                sp.sem_clear(range(first, last + 1))


def program(nc, io):
    g = Shared()
    g.NB, g.S, g.D = io["x"].shape
    g.KC, g.NT = g.D // P, g.NB * g.S // P
    g.E, _, two_f = io["L0_ffn_gate_up_proj"].shape
    g.F = two_f // 2
    g.BLOCKS = g.NT + g.E - 1
    g.CHOOSERS, chunks = io["L1_ffn_w"].shape[:2]
    g.I, g.SLOTS = chunks * P, g.S // g.CHOOSERS * 2
    g.rows_in = nc.dram_tensor("rows_in", [g.BLOCKS * P, g.D], F32, kind="Internal").ap()
    g.rows_out = nc.dram_tensor("rows_out", [g.BLOCKS * P, g.D], F32, kind="Internal").ap()
    g.chosen_out = nc.dram_tensor("chosen_out", [g.NB, g.CHOOSERS * g.SLOTS, g.D], F32, kind="Internal").ap()
    with ExitStack() as whole:
        def keep(ctx, name, shape, dt=F32):
            return ctx.enter_context(nc.sbuf_tensor(name, shape, dt))

        g.x = keep(whole, "x", [P, g.NT, g.D])
        g.ident, g.eps = keep(whole, "ident", [P, P]), keep(whole, "eps", [P, 1])
        g.row_of = keep(whole, "row_of", [P, g.NT], U32)
        g.block_expert = keep(whole, "block_expert", [P, g.BLOCKS], I32)
        attend_latents(nc, g, io)
        clear_semaphores(nc)
        with ExitStack() as ctx:
            g.xT_h = keep(ctx, "xT_h", [P, g.KC, g.NB * g.S], F32R)
            g.xT_l = keep(ctx, "xT_l", [P, g.KC, g.NB * g.S], F32R)
            g.CTX_HEAD, g.CTX_GROUPS = g.D // 16, 16 // (P // 32)
            g.ctx_w_h = [keep(ctx, f"ctx_w_h{i}", [P, g.KC, g.D], F32R) for i in range(3)]
            g.ctx_w_l = [keep(ctx, f"ctx_w_l{i}", [P, g.KC, g.D], F32R) for i in range(3)]
            g.ctx_out_h = keep(ctx, "ctx_out_h", [P, g.CTX_GROUPS, g.D], F32R)
            g.ctx_out_l = keep(ctx, "ctx_out_l", [P, g.CTX_GROUPS, g.D], F32R)
            g.ctx_bias_q, g.ctx_bias_k = keep(ctx, "bias_q", [P, g.KC]), keep(ctx, "bias_k", [P, g.KC])
            g.ctx_bias_v, g.ctx_bias_o = keep(ctx, "bias_v", [P, g.D]), keep(ctx, "bias_o", [P, g.D])
            with ExitStack() as inner:
                g.xn = keep(inner, "xn", [P, g.NT, g.D])
                g.logits = keep(inner, "logits", [P, g.NT, g.E])
                norm_and_route(nc, g, io)
                clear_semaphores(nc)
                route_tokens(nc, g, io)
                clear_semaphores(nc)
                run_experts(nc, g, io)
                clear_semaphores(nc)
                shared_expert(nc, g, io)
                clear_semaphores(nc)
                add_rows(nc, g, io)
                clear_semaphores(nc)
            attend_context(nc, g, io)
            clear_semaphores(nc)
        g.gate_logits = keep(whole, "gate_logits", [P, 2, g.NB, g.CHOOSERS])
        g.affinity, g.place = keep(whole, "affinity", [P, 2, g.NB * g.CHOOSERS]), keep(whole, "place", [P, 2, g.NB * g.CHOOSERS])
        g.slot = keep(whole, "slot", [P, g.SLOTS])
        g.xin_h = keep(whole, "xin_h", [P, g.KC, g.CHOOSERS, g.NB, g.SLOTS], F32R)
        g.xin_l = keep(whole, "xin_l", [P, g.KC, g.CHOOSERS, g.NB, g.SLOTS], F32R)
        with ExitStack() as ctx:
            g.xn = keep(ctx, "xn_last", [P, g.NT, g.D])
            norm_and_gate(nc, g, io)
            clear_semaphores(nc)
            choose_tokens(nc, g, io)
            clear_semaphores(nc)
            collect_tokens(nc, g, io)
            clear_semaphores(nc)
        run_choosing_experts(nc, g, io)
        clear_semaphores(nc)
        return_tokens(nc, g, io)


def lay_out(inputs):
    import numpy as np

    same = ("x", "ctx_1024", "L0_xattn_Wq", "L0_xattn_Wkv", "L0_xattn_Wo", "L0_ffn_gate_up_proj",
            "L0_ffn_down_proj", "L1_xattn_bv", "L1_xattn_bo")
    transposed = ("L0_ffn_w_gate", "L0_ffn_w_up", "L0_ffn_w_down", "L1_xattn_Wq", "L1_xattn_Wk",
                  "L1_xattn_Wv", "L1_xattn_Wo", "L1_ffn_gate_w")
    by_partition = ("L0_xattn_ln1_w", "L0_xattn_ln1_b", "L0_xattn_ln2_w", "L0_xattn_ln2_b",
                    "L1_xattn_bq", "L1_xattn_bk")
    a = {name: np.asarray(value) for name, value in inputs.items()}
    out = {name: a[name] for name in same}
    out["L0_ffn_w_router_T"] = a["L0_ffn_w_router"].T
    out["ctx_T"] = a["ctx_1024"].reshape(-1, a["ctx_1024"].shape[-1]).T
    for name in transposed:
        out[f"{name}_T"] = a[name].T
    for name in by_partition:
        out[name] = a[name].reshape(-1, P).T
    e, i, d = a["L1_ffn_w_gate"].shape

    def of_inputs(w):
        return w.reshape(e, i // P, P, d // P, P).transpose(0, 1, 4, 3, 2).reshape(e, i // P, P, d)

    down = a["L1_ffn_w_down"].reshape(e, d, i // P, P).transpose(0, 2, 3, 1)
    out["L1_ffn_w"] = np.concatenate([of_inputs(a["L1_ffn_w_gate"]), of_inputs(a["L1_ffn_w_up"]), down], axis=-1)
    return {name: np.ascontiguousarray(value) for name, value in out.items()}


def kernel(**inputs):
    import numpy as np
    import concourse.bacc as bacc
    from concourse import mybir
    from concourse.bass_utils import run_bass_kernel_spmd as run

    nc = bacc.Bacc("TRN2", target_bir_lowering=False, num_devices=1)
    arrays, io = {}, {}
    for name, a in lay_out(inputs).items():
        arrays[f"in_{name}"] = a
        io[name] = nc.dram_tensor(f"in_{name}", a.shape, mybir.dt.from_np(a.dtype), kind="ExternalInput").ap()
    io["out"] = nc.dram_tensor("out_x", io["x"].shape, mybir.dt.from_np(np.dtype("float32")), kind="ExternalOutput").ap()
    program(nc, io)
    return run(nc, [arrays], core_ids=[0]).results[0]["out_x"]
```
